# Optimizing a Trainium2 kernel written in Bass

```python
import numpy as np
import jax
import jax.numpy as jnp

def _softmax(x, axis=-1):
    return jax.nn.softmax(x, axis=axis)

def _gelu(x):
    return jax.nn.gelu(x, approximate=True)

def _silu(x):
    return jax.nn.silu(x)

def _sigmoid(x):
    return jax.nn.sigmoid(x)

def _layernorm(x, axis=-1, eps=1e-05):
    m = jnp.mean(x, axis=axis, keepdims=True)
    v = jnp.var(x, axis=axis, keepdims=True)
    return (x - m) / jnp.sqrt(v + eps)

def _scatter_add(tgt, idx, src, axis=0):
    return tgt.at[idx].add(src)

def _segment_sum(src, seg, n):
    return jax.ops.segment_sum(src, seg, n)
kernel_name = 'mk_seq_postln_d2_jaxref_r4_6b682e'

def setup_inputs(seed: int=0):
    np.random.seed(seed)
    _w = jnp.asarray

    def _L0_attn_setup():
        import jax, jax.numpy as jnp
        import numpy as np
        NUM_HEADS = 32
        EPS = 1e-15
        key = jax.random.key(seed)
        k1, k2, k3, k4 = jax.random.split(key, 4)
        B, N, C = (8, 1024, 256)
        x = jax.random.normal(k1, (B, N, C), dtype=jnp.float32)
        qkv_weight = jax.random.normal(k2, (3 * C, C), dtype=jnp.float32) * C ** (-0.5)
        proj_weight = jax.random.normal(k3, (C, C), dtype=jnp.float32) * C ** (-0.5)
        proj_bias = jax.random.normal(k4, (C,), dtype=jnp.float32) * 0.01
        return {'x': x, 'qkv_weight': qkv_weight, 'proj_weight': proj_weight, 'proj_bias': proj_bias}
    _L0_attn_in = _L0_attn_setup()

    def _L0_ffn_setup():
        import math
        import jax, jax.numpy as jnp
        import numpy as np
        NUM_EXPERTS = 8
        TOP_K = 2
        CAPACITY_FACTOR = 1.0
        B, S, H, I = (4, 512, 256, 1024)
        key = jax.random.key(seed)
        k_x, k_rw, k_wi, k_wo = jax.random.split(key, 4)
        x = jax.random.normal(k_x, (B, S, H), dtype=jnp.float32)
        lim = math.sqrt(6.0 / (H + NUM_EXPERTS))
        router_w = jax.random.uniform(k_rw, (NUM_EXPERTS, H), minval=-lim, maxval=lim, dtype=jnp.float32)
        router_b = jnp.zeros((NUM_EXPERTS,), dtype=jnp.float32)
        experts_inter = jax.random.normal(k_wi, (NUM_EXPERTS - 1, H, I), dtype=jnp.float32) / math.sqrt(H)
        experts_out = jax.random.normal(k_wo, (NUM_EXPERTS - 1, I, H), dtype=jnp.float32) / math.sqrt(I)
        return {'x': x, 'router_w': router_w, 'router_b': router_b, 'experts_inter': experts_inter, 'experts_out': experts_out}
    _L0_ffn_in = _L0_ffn_setup()

    def _L1_attn_setup():
        import math
        import jax, jax.numpy as jnp
        import numpy as np
        D, DK, DV = (256, 256, 256)
        B, S = (4, 512)
        key = jax.random.key(seed)
        ks = jax.random.split(key, 4)
        std_qk = math.sqrt(2.0 / (D + DK))
        std_v = math.sqrt(2.0 / (D + DV))
        return {'X': jax.random.normal(ks[0], (B, S, D), dtype=jnp.float32), 'W_q': jax.random.normal(ks[1], (D, DK), dtype=jnp.float32) * std_qk, 'W_k': jax.random.normal(ks[2], (D, DK), dtype=jnp.float32) * std_qk, 'W_v': jax.random.normal(ks[3], (D, DV), dtype=jnp.float32) * std_v, 'b_q': jnp.zeros((DK,), dtype=jnp.float32), 'b_k': jnp.zeros((DK,), dtype=jnp.float32), 'b_v': jnp.zeros((DV,), dtype=jnp.float32)}
    _L1_attn_in = _L1_attn_setup()

    def _L1_ffn_setup():
        import jax, jax.numpy as jnp
        import numpy as np
        DIM = 256
        LATENT = 128
        INTER = 128
        SHARED = 1024
        E = 8
        TOPK = 2
        NGROUP = 2
        TOPKG = 1
        NORM_TOPK = True
        SCALE = 1.0
        B, S = (2, 256)

        def relu2(x):
            r = jnp.maximum(x, 0.0)
            return r * r
        key = jax.random.key(seed)
        ks = jax.random.split(key, 8)

        def w(k, shape, std=0.02):
            return jax.random.normal(k, shape, dtype=jnp.float32) * std
        return {'x': jax.random.normal(ks[0], (B, S, DIM), dtype=jnp.float32), 'gate': w(ks[1], (E, DIM)), 'corr_bias': jnp.zeros((E,), jnp.float32), 'w1': w(ks[2], (E, INTER, LATENT)), 'w2': w(ks[3], (E, LATENT, INTER)), 'fc1_w': w(ks[4], (LATENT, DIM)), 'fc2_w': w(ks[5], (DIM, LATENT)), 'up_w': w(ks[6], (SHARED, DIM)), 'down_w': w(ks[7], (DIM, SHARED))}
    _L1_ffn_in = _L1_ffn_setup()
    _d = {'L0_attn_x': _L0_attn_in['x'], 'L0_attn_qkv_weight': _L0_attn_in['qkv_weight'], 'L0_attn_proj_weight': _L0_attn_in['proj_weight'], 'L0_attn_proj_bias': _L0_attn_in['proj_bias'], 'L0_ffn_router_w': _L0_ffn_in['router_w'], 'L0_ffn_router_b': _L0_ffn_in['router_b'], 'L0_ffn_experts_inter': _L0_ffn_in['experts_inter'], 'L0_ffn_experts_out': _L0_ffn_in['experts_out'], 'L1_attn_W_q': _L1_attn_in['W_q'], 'L1_attn_W_k': _L1_attn_in['W_k'], 'L1_attn_W_v': _L1_attn_in['W_v'], 'L1_attn_b_q': _L1_attn_in['b_q'], 'L1_attn_b_k': _L1_attn_in['b_k'], 'L1_attn_b_v': _L1_attn_in['b_v'], 'L1_ffn_gate': _L1_ffn_in['gate'], 'L1_ffn_corr_bias': _L1_ffn_in['corr_bias'], 'L1_ffn_w1': _L1_ffn_in['w1'], 'L1_ffn_w2': _L1_ffn_in['w2'], 'L1_ffn_fc1_w': _L1_ffn_in['fc1_w'], 'L1_ffn_fc2_w': _L1_ffn_in['fc2_w'], 'L1_ffn_up_w': _L1_ffn_in['up_w'], 'L1_ffn_down_w': _L1_ffn_in['down_w']}
    _x0 = _d['L0_attn_x']
    _d['L0_attn_x'] = jax.random.normal(jax.random.fold_in(jax.random.key(seed), 1), (8, 1024, 256), dtype=_x0.dtype)
    del _x0
    return _d

def reference(L0_attn_x, L0_attn_qkv_weight, L0_attn_proj_weight, L0_attn_proj_bias, L0_ffn_router_w, L0_ffn_router_b, L0_ffn_experts_inter, L0_ffn_experts_out, L1_attn_W_q, L1_attn_W_k, L1_attn_W_v, L1_attn_b_q, L1_attn_b_k, L1_attn_b_v, L1_ffn_gate, L1_ffn_corr_bias, L1_ffn_w1, L1_ffn_w2, L1_ffn_fc1_w, L1_ffn_fc2_w, L1_ffn_up_w, L1_ffn_down_w):

    def _L0_attn_ref(x, qkv_weight, proj_weight, proj_bias):
        import jax, jax.numpy as jnp
        import numpy as np
        NUM_HEADS = 32
        EPS = 1e-15
        B, N, C = x.shape
        H = NUM_HEADS
        D = C // H
        qkv = jax.nn.relu(jnp.einsum('bnc,oc->bno', x, qkv_weight))
        qkv = qkv.reshape(B, N, 3, H, D)
        q, k, v = (qkv[:, :, 0], qkv[:, :, 1], qkv[:, :, 2])
        v_pad = jnp.concatenate([v, jnp.ones((B, N, H, 1), dtype=v.dtype)], axis=-1)
        vk = jnp.einsum('bnhe,bnhd->bhed', v_pad.astype(jnp.float32), k.astype(jnp.float32))
        vk_q = jnp.einsum('bhed,bnhd->bnhe', vk, q.astype(jnp.float32))
        proj_input = (vk_q[..., :D] / (vk_q[..., D:] + EPS)).astype(qkv.dtype)
        proj_input = proj_input.reshape(B, N, C)
        y = jnp.einsum('bnc,oc->bno', proj_input, proj_weight) + proj_bias
        return y

    def _L0_ffn_ref(x, router_w, router_b, experts_inter, experts_out):
        import math
        import jax, jax.numpy as jnp
        import numpy as np
        NUM_EXPERTS = 8
        TOP_K = 2
        CAPACITY_FACTOR = 1.0
        B, S, H, I = (4, 512, 256, 1024)
        batch, seq, hidden = x.shape
        n_exp = router_w.shape[0]
        n_tok = batch * seq
        cap = math.ceil(n_tok / n_exp * CAPACITY_FACTOR)
        logits = jnp.einsum('bsh,eh->bse', x, router_w) + router_b
        weights_flat = jax.nn.softmax(logits, axis=-1).reshape(n_tok, n_exp)
        x_flat = x.reshape(n_tok, hidden)
        topk_vals, topk_idx = jax.lax.top_k(weights_flat, TOP_K)
        rows = jnp.arange(n_tok)[:, None]
        topk_flat = jnp.zeros_like(weights_flat).at[rows, topk_idx].set(topk_vals)
        routing_mask = (topk_flat > 0).astype(jnp.int32)
        noop_w = topk_flat[:, -1]
        noop_mask = routing_mask[:, -1].astype(x.dtype)
        expert_w = topk_flat[:, :-1]
        expert_mask = routing_mask[:, :-1]
        sorted_indices = jnp.argsort(-expert_mask, axis=0)[:cap]
        sorted_mask = jnp.take_along_axis(expert_mask, sorted_indices, axis=0)
        used_idx = (sorted_indices * sorted_mask).reshape(-1)
        inputs = x_flat[used_idx] * sorted_mask.reshape(-1).astype(x.dtype)[:, None]
        inputs = inputs.reshape(cap, n_exp - 1, hidden)
        in_w = jnp.take_along_axis(expert_w, sorted_indices, axis=0)
        h = jax.nn.relu(jnp.einsum('ceh,ehi->cei', inputs, experts_inter))
        out = jnp.einsum('cei,eih->ceh', h, experts_out) * in_w[..., None]
        combined = jnp.zeros_like(x_flat).at[used_idx].add(out.reshape(-1, hidden))
        combined = combined + x_flat * (noop_w * noop_mask)[:, None]
        return combined.reshape(batch, seq, hidden)

    def _L1_attn_ref(X, W_q, W_k, W_v, b_q, b_k, b_v):
        import math
        import jax, jax.numpy as jnp
        import numpy as np
        D, DK, DV = (256, 256, 256)
        B, S = (4, 512)
        scale = 1.0 / math.sqrt(DK)
        Q = X @ W_q + b_q
        K = X @ W_k + b_k
        V = X @ W_v + b_v
        A = jnp.einsum('bsd,btd->bst', Q, K) * scale
        A = jax.nn.softmax(A, axis=2)
        return jnp.einsum('bst,btv->bsv', A, V)

    def _L1_ffn_ref(x, gate, corr_bias, w1, w2, fc1_w, fc2_w, up_w, down_w):
        import jax, jax.numpy as jnp
        import numpy as np
        DIM = 256
        LATENT = 128
        INTER = 128
        SHARED = 1024
        E = 8
        TOPK = 2
        NGROUP = 2
        TOPKG = 1
        NORM_TOPK = True
        SCALE = 1.0
        B, S = (2, 256)

        def relu2(x):
            r = jnp.maximum(x, 0.0)
            return r * r
        Bv, Sv, D = x.shape
        xf = x.reshape(-1, D)
        N = xf.shape[0]
        scores = jax.nn.sigmoid(xf.astype(jnp.float32) @ gate.T)
        sfc = scores + corr_bias
        gs = E // NGROUP
        if NGROUP > 1:
            group_scores = jax.lax.top_k(sfc.reshape(N, NGROUP, gs), 2)[0].sum(-1)
            gidx = jax.lax.top_k(group_scores, TOPKG)[1]
            gmask = jnp.zeros((N, NGROUP), sfc.dtype).at[jnp.arange(N)[:, None], gidx].set(1.0)
            smask = jnp.repeat(gmask, gs, axis=1)
            sfc = jnp.where(smask > 0, sfc, 0.0)
        sel = jax.lax.top_k(sfc, TOPK)[1]
        top_scores = jnp.take_along_axis(scores, sel, axis=1)
        if NORM_TOPK:
            top_scores = top_scores / (top_scores.sum(-1, keepdims=True) + 1e-20)
        flat = sel.reshape(-1)
        perm = jnp.argsort(flat, stable=True)
        sorted_eid = flat[perm]
        scores_sorted = top_scores.reshape(-1)[perm]
        tok = perm // TOPK
        lat = xf @ fc1_w.T
        xs = lat[tok]
        out = jnp.zeros_like(xs)
        for e in range(E):
            he = relu2(xs @ w1[e].T) @ w2[e].T
            out = jnp.where((sorted_eid == e)[:, None], he, out)
        out = out * scores_sorted[:, None]
        comb = jnp.zeros((N, LATENT), out.dtype).at[tok].add(out)
        routed = comb @ fc2_w.T * SCALE
        shared = relu2(xf @ up_w.T) @ down_w.T
        return (routed + shared).reshape(Bv, Sv, D)
    x = L0_attn_x
    x = _layernorm(x + _L0_attn_ref(x, L0_attn_qkv_weight, L0_attn_proj_weight, L0_attn_proj_bias), axis=-1)
    x = _layernorm(x + _L0_ffn_ref(x, L0_ffn_router_w, L0_ffn_router_b, L0_ffn_experts_inter, L0_ffn_experts_out), axis=-1)
    x = _layernorm(x + _L1_attn_ref(x, L1_attn_W_q, L1_attn_W_k, L1_attn_W_v, L1_attn_b_q, L1_attn_b_k, L1_attn_b_v), axis=-1)
    x = _layernorm(x + _L1_ffn_ref(x, L1_ffn_gate, L1_ffn_corr_bias, L1_ffn_w1, L1_ffn_w2, L1_ffn_fc1_w, L1_ffn_fc2_w, L1_ffn_up_w, L1_ffn_down_w), axis=-1)
    return x

_drawn_inputs = setup_inputs


def setup_inputs(seed=0):
    import zlib

    import numpy as np

    out = dict(_drawn_inputs(seed))
    spreads = {'L0_ffn_router_b': (0.0, 0.1),
     'L1_attn_b_q': (0.0, 0.8),
     'L1_attn_b_k': (0.0, 2.0),
     'L1_attn_b_v': (0.0, 0.1),
     'L1_ffn_corr_bias': (0.0, 0.8)}
    factors = {'L0_attn_proj_bias': 2.969,
     'L1_ffn_gate': 8.0,
     'L1_ffn_w1': 8.0,
     'L1_ffn_w2': 8.0,
     'L1_ffn_fc1_w': 8.0,
     'L1_ffn_fc2_w': 8.0,
     'L1_ffn_up_w': 8.0,
     'L1_ffn_down_w': 8.0}
    for name, (base, spread) in spreads.items():
        noise = np.random.default_rng([zlib.crc32(name.encode()), seed]).standard_normal(out[name].shape)
        drawn = base * np.exp(spread * noise) if base else spread * noise
        out[name] = jnp.asarray(drawn.astype(out[name].dtype))
    for name, factor in factors.items():
        out[name] = (out[name] * factor).astype(out[name].dtype)
    return out
```

```python
import concourse.bass as bass
from concourse import mybir
from contextlib import ExitStack

F32 = mybir.dt.float32
F32R = mybir.dt.float32r
BF16 = mybir.dt.bfloat16
I32 = mybir.dt.int32
U32 = mybir.dt.uint32
ALU = mybir.AluOpType
ACT = mybir.ActivationFunctionType
AX = mybir.AxisListType

P = 128
BATCHES, SEQ, C = 8, 1024, 256
TOKENS = BATCHES * SEQ
TILES = SEQ // P
CH = C // P
HALF = SEQ // 2
HTILES = HALF // P
HEADS = 32
HEAD = C // HEADS
ATTN_EPS = 1e-15
LN_EPS = 1e-5
EXPERTS = 8
REAL = EXPERTS - 1
INTER = 1024
ICH = INTER // P
CAP = TOKENS // EXPERTS
TRASH = REAL * CAP
LATENT = 128
SHARED = 1024
GROUPS = 2
GSIZE = EXPERTS // GROUPS
NORM_EPS = 1e-20
SCALE = C ** -0.5
LOWEST = -3.0e38
RSQRT_MAGIC = 0x5F3759DF
BANKS = 8


def count(i, first, each):
    if isinstance(i, int):
        return 0 if i == 0 else first + (i - 1) * each
    return i * each + (first - each)


def wait_past(eng, sem, value):
    if not isinstance(value, int) or value > 0:
        eng.wait_ge(sem, value)


class Turns:

    def __init__(self, start, offset, banks):
        self.start, self.offset, self.banks, self.n = start, offset, banks, 0

    def take(self):
        bank = self.banks[(self.offset + self.n) % len(self.banks)]
        self.n += 1
        return bank, self.start + (self.n - 1)


class Chain:

    def __init__(self, eng, sem, start):
        self.eng, self.sem, self.start, self.n = eng, sem, start, 0

    def step(self, instruction):
        self.n += 1
        instruction.then_inc(self.sem, 1)

    def wait(self):
        wait_past(self.eng, self.sem, self.start + self.n)

    def then(self, instruction_of, *args, **kw):
        self.wait()
        self.step(instruction_of(*args, **kw))


def f32(ap):
    return ap.bitcast(F32)


def across(ap, n):
    return ap.unsqueeze(2).to_broadcast([P, ap.shape[1], n])


def along(ap, n):
    return ap.unsqueeze(1).to_broadcast([P, n, ap.shape[1]])


def product(pe, out, terms):
    last = None
    for j, (lh, ll, rh, rl) in enumerate(terms):
        pe.matmul(out, lh, rh, start=(j == 0), stop=False)
        pe.matmul(out, lh, rl, start=False, stop=False)
        last = pe.matmul(out, ll, rh, start=False, stop=(j == len(terms) - 1))
    return last


def reciprocal_root(v, chain, out, x, t):
    chain.then(v.tensor_scalar, t.bitcast(I32), x.bitcast(I32), 1, None, ALU.arith_shift_right)
    chain.then(v.tensor_scalar, out.bitcast(I32), t.bitcast(I32), -1.0, float(RSQRT_MAGIC), ALU.mult, ALU.add)
    for _ in range(3):
        chain.then(v.tensor_tensor, t, out, out, ALU.mult)
        chain.then(v.tensor_tensor, t, t, x, ALU.mult)
        chain.then(v.tensor_scalar, t, t, -0.5, 1.5, ALU.mult, ALU.add)
        chain.then(v.tensor_tensor, out, out, t, ALU.mult)


RR_STEPS = 14
MEAN_STEPS = 7


def layer_norm_stats(v, chain, rows, stats, mean, rstd, tmp, n):
    for t in range(n):
        chain.step(v.bn_stats(stats[:, t, :], rows[:, t, :]))
    even, odd, var, t = stats[:, :, 1], stats[:, :, 4], tmp[:, 0, :], tmp[:, 1, :]
    chain.then(v.tensor_tensor, mean, even, odd, ALU.add)
    chain.then(v.tensor_scalar, mean, mean, 0.5, None, ALU.mult)
    chain.then(v.tensor_tensor, t, even, odd, ALU.subtract)
    chain.then(v.scalar_tensor_tensor, t, t, 0.25, t, ALU.mult, ALU.mult)
    chain.then(v.tensor_tensor, var, stats[:, :, 2], stats[:, :, 5], ALU.add)
    chain.then(v.scalar_tensor_tensor, var, var, 1.0 / C, t, ALU.mult, ALU.add)
    chain.then(v.tensor_scalar, var, var, LN_EPS, None, ALU.add)
    reciprocal_root(v, chain, rstd, var, t)
    chain.wait()


def top_two(v, chain, first, second, values, falling, m, key, n):
    for out, of in ((first, values), (second, key[1])):
        if out is second:
            chain.then(v.scalar_tensor_tensor, key[1], first, LOWEST, values, ALU.mult, ALU.add)
        chain.then(v.tensor_reduce, m, of, AX.X, ALU.max)
        chain.then(v.tensor_tensor, key[0], of, across(m, EXPERTS), ALU.is_equal)
        chain.then(v.tensor_tensor, key[0], key[0], along(falling, n), ALU.mult)
        chain.then(v.tensor_reduce, m, key[0], AX.X, ALU.max)
        chain.then(v.tensor_tensor, out, key[0], across(m, EXPERTS), ALU.is_equal)


TOP_STEPS = 11


def stage_a(nc, d):
    HEAD_GROUPS = TILES + CH + 2 * CH
    LATE_GROUPS = 2 * CH + 1
    MAIN_GROUPS = 4 * CH + TILES // 2
    FIRST = HEAD_GROUPS + MAIN_GROUPS
    EACH = FIRST + LATE_GROUPS + 1
    CONSTS = 24
    LN_STEPS = TILES + MEAN_STEPS + RR_STEPS
    ROUTE_STEPS = 4 + TOP_STEPS + 10

    with ExitStack() as ctx:
        def sb(name, shape, dt=F32):
            return ctx.enter_context(nc.sbuf_tensor("a_" + name, shape, dt))

        def sem(name):
            return ctx.enter_context(nc.semaphore("a_" + name))

        ps = ctx.enter_context(nc.psum_tensor("a_ps", [P, BANKS, 512], F32))

        wkv_raw, wkv_hi, wkv_lo = sb("wkv_raw", [P, CH, 2 * C]), sb("wkv_hi", [P, CH, 2 * C], F32R), sb("wkv_lo", [P, CH, 2 * C], F32R)
        wq_raw, wq_hi, wq_lo = sb("wq_raw", [P, CH, C]), sb("wq_hi", [P, CH, C], F32R), sb("wq_lo", [P, CH, C], F32R)
        wp_raw, wp_hi, wp_lo = sb("wp_raw", [P, CH, C]), sb("wp_hi", [P, CH, C], F32R), sb("wp_lo", [P, CH, C], F32R)
        wr_raw, wr_hi, wr_lo = sb("wr_raw", [P, CH, EXPERTS]), sb("wr_hi", [P, CH, EXPERTS], F32R), sb("wr_lo", [P, CH, EXPERTS], F32R)
        bias_p, bias_r = sb("bias_p", [P, C]), sb("bias_r", [P, EXPERTS])
        zeros = sb("zeros", [P, 2 * SEQ])
        ident = sb("ident", [P, P])
        same_head = sb("same_head", [P, 2 * P])
        ones_f = sb("ones_f", [P, P])
        before, ones = sb("before", [P, P], BF16), sb("ones", [P, P], BF16)
        falling, real, slot0 = sb("falling", [P, EXPERTS]), sb("real", [P, EXPERTS]), sb("slot0", [P, EXPERTS])
        xT_raw, xT_hi, xT_lo = sb("xT_raw", [P, CH, SEQ]), sb("xT_hi", [P, CH, SEQ], F32R), sb("xT_lo", [P, CH, SEQ], F32R)
        x_rows = sb("x_rows", [P, TILES, C])
        kv_hi, kv_lo = sb("kv_hi", [P, TILES, 5 * P], F32R), sb("kv_lo", [P, TILES, 4 * P], F32R)
        vk_m, vk_hi, vk_lo = sb("vk_m", [P, CH, 2 * P]), sb("vk_hi", [P, CH, 2 * P], F32R), sb("vk_lo", [P, CH, 2 * P], F32R)
        q_hi, q_lo = sb("q_hi", [P, CH, SEQ], F32R), sb("q_lo", [P, CH, SEQ], F32R)
        den, rden, mix = sb("den", [P, HALF]), sb("rden", [P, HALF]), sb("mix", [P, 2, HALF])
        mix_hi, mix_lo = sb("mix_hi", [P, CH, SEQ], F32R), sb("mix_lo", [P, CH, SEQ], F32R)
        rows, x1, x1_copy = sb("rows", [P, TILES, C]), sb("x1", [P, TILES, C]), sb("x1_copy", [P, TILES, C])
        x1T_hi, x1T_lo = sb("x1T_hi", [P, CH, SEQ], F32R), sb("x1T_lo", [P, CH, SEQ], F32R)
        stats, mean = sb("stats", [P, TILES, 6]), sb("mean", [P, TILES])
        rstd, rr_tmp = sb("rstd", [P, TILES]), sb("rr_tmp", [P, 2, TILES])
        logit, expd, weight = (sb(n, [P, TILES, EXPERTS]) for n in ("logit", "expd", "weight"))
        first, second = sb("first", [P, TILES, EXPERTS]), sb("second", [P, TILES, EXPERTS])
        key0, key1 = sb("key0", [P, TILES, EXPERTS]), sb("key1", [P, TILES, EXPERTS])
        row_m, row_s = sb("row_m", [P, TILES]), sb("row_s", [P, TILES])
        mask = sb("mask", [P, TILES, EXPERTS], BF16)
        tile_sum, carry = sb("tile_sum", [P, EXPERTS]), sb("carry", [P, EXPERTS])
        carry_b = sb("carry_b", [P, EXPERTS], BF16)
        slot, room = sb("slot", [P, TILES, EXPERTS]), sb("room", [P, TILES, EXPERTS])
        picked = sb("picked", [P, 2, TILES])
        slots = sb("slots", [P, 2, TILES], U32)
        gates = sb("gates", [P, 3, TILES])

        weights_in, consts = sem("weights_in"), sem("consts")
        xT_in, x_in = sem("xT_in"), sem("x_in")
        zero_filled = sem("zero_filled")
        weights_hi, weights_split = sem("weights_hi"), sem("weights_split")
        xT_hi_done, xT_split = sem("xT_hi_done"), sem("xT_split")
        bank_full, bank_free = sem("bank_full"), sem("bank_free")
        kv_hi_done, q_hi_done, vk_hi_done, vk_split = sem("kv_hi_done"), sem("q_hi_done"), sem("vk_hi_done"), sem("vk_split")
        recip_done, mix_hi_done, mix_split = sem("recip_done"), sem("mix_hi_done"), sem("mix_split")
        x_biased, x1_done, x1_stored, x1_copied = sem("x_biased"), sem("x1_done"), sem("x1_stored"), sem("x1_copied")
        x1T_hi_done, logit_done, exp_done = sem("x1T_hi_done"), sem("logit_done"), sem("exp_done")
        ln_chain, route_chain, slot_chain = sem("ln_chain"), sem("route_chain"), sem("slot_chain")
        mask_done, slots_done, slots_stored, scattered = sem("mask_done"), sem("slots_done"), sem("slots_stored"), sem("scattered")
        SLOT_STEPS = 9

        def turns(i):
            return Turns(count(i, FIRST, EACH), 0 if isinstance(i, int) and i == 0 else FIRST, range(BANKS))

        block = ctx.enter_context(nc.Block())

        @block.sync
        def _(sp):
            for raw, w in ((wkv_raw, "wkvT"), (wq_raw, "wqT"), (wp_raw, "projT"), (wr_raw, "routerT")):
                sp.dma_start(raw[:], d[w].rearrange("(a p) n -> p a n", p=P)).then_inc(weights_in, 16)
            sp.dma_start(bias_p[:], d["proj_bias"].partition_broadcast(P)).then_inc(weights_in, 16)
            sp.dma_start(bias_r[:], d["router_b"].partition_broadcast(P)).then_inc(weights_in, 16)

            def load(i):
                if not (isinstance(i, int) and i == 0):
                    sp.wait_ge(xT_split, i)
                sp.dma_start(xT_raw[:], d["xT"][:, bass.ds(i * SEQ, SEQ)].rearrange("(a p) n -> p a n", p=P)).then_inc(xT_in, 16)
                if not (isinstance(i, int) and i == 0):
                    sp.wait_ge(bank_free, count(i - 1, FIRST, EACH) + (FIRST if isinstance(i, int) and i == 1 else EACH - 1))
                sp.dma_start(x_rows[:], d["x"][bass.ds(i * SEQ, SEQ), :].rearrange("(t p) c -> p t c", p=P)).then_inc(x_in, 16)

            def store(i):
                sp.wait_ge(x1_done, i + 1)
                sp.dma_start(d["x1"][bass.ds(i * SEQ, SEQ), :].rearrange("(t p) c -> p t c", p=P), x1[:]).then_inc(x1_stored, 16)

            def store_slots(i):
                sp.wait_ge(slots_done, i + 1)
                sp.dma_start(d["slots"][bass.ds(i * P, P), :], slots[:].rearrange("p a t -> p (a t)")).then_inc(slots_stored, 16)
                sp.dma_start(d["gates"][bass.ds(i * P, P), :], gates[:].rearrange("p a t -> p (a t)")).then_inc(slots_stored, 16)

            load(0)
            load(1)
            store(0)
            with sp.Fori(1, BATCHES - 1) as i:
                load(i + 1)
                store_slots(i - 1)
                store(i)
            store_slots(BATCHES - 2)
            store(BATCHES - 1)
            store_slots(BATCHES - 1)
            sp.wait_ge(x1_stored, 16 * BATCHES)
            sp.wait_ge(slots_stored, 32 * BATCHES)

        @block.gpsimd
        def _(pool):
            def const(instruction):
                instruction.then_inc(consts, 1)

            const(pool.memset(zeros[:], 0.0))
            const(pool.memset(ident[:], 0.0))
            const(pool.memset(ones_f[:], 1.0))
            const(pool.memset(same_head[:], 1.0))
            const(pool.memset(before[:], 1.0))
            const(pool.memset(ones[:], 1.0))
            const(pool.memset(real[:], 1.0))
            const(pool.memset(carry[:], 0.0))
            const(pool.memset(carry_b[:], 0.0))
            for e in range(EXPERTS):
                const(pool.memset(falling[:, e:e + 1], float(EXPERTS - e)))
            pool.wait_ge(consts, 9 + EXPERTS)
            for part in range(REAL * CAP * C // (P * 2 * SEQ)):
                pool.dma_start(d["xs"].rearrange("(a p r) c -> a p (r c)", p=P, r=2 * SEQ // C)[part, :, :], zeros[:]).then_inc(zero_filled, 16)
            pool.dma_start(d["ys"][TRASH:TRASH + P, :], zeros[:, 0:C]).then_inc(zero_filled, 16)
            ZERO_FILLS = REAL * CAP * C // (P * 2 * SEQ) + 1
            const(pool.affine_select(out=ident[:], in_=ident[:], compare_op=ALU.not_equal, fill=1.0,
                                     base=0, pattern=[[-1, P]], channel_multiplier=1))
            const(pool.affine_select(out=before[:], in_=before[:], compare_op=ALU.is_ge, fill=0.0,
                                     base=-1, pattern=[[1, P]], channel_multiplier=-1))
            heads = same_head[:].rearrange("p (a h e) -> p a h e", a=2, e=HEAD)
            const(pool.affine_select(out=heads, in_=heads, compare_op=ALU.is_ge, fill=0.0, base=0,
                                     pattern=[[0, 2], [-HEAD, P // HEAD], [0, HEAD]], channel_multiplier=1))
            pool.wait_ge(consts, 9 + EXPERTS + 3)
            const(pool.affine_select(out=heads, in_=heads, compare_op=ALU.is_ge, fill=0.0, base=HEAD - 1,
                                     pattern=[[0, 2], [HEAD, P // HEAD], [0, HEAD]], channel_multiplier=-1))
            const(pool.memset(real[:, REAL:EXPERTS], 0.0))
            const(pool.iota(slots[:].rearrange("p a t -> p (a t)").bitcast(I32)[:, 0:EXPERTS], pattern=[[CAP, EXPERTS]], base=-TRASH, channel_multiplier=0))
            pool.wait_ge(consts, 9 + EXPERTS + 6)
            const(pool.tensor_copy(slot0[:], slots[:].rearrange("p a t -> p (a t)").bitcast(I32)[:, 0:EXPERTS]))

            def bias(i):
                pool.wait_ge(x_in, 16 * i + 16)
                if isinstance(i, int) and i == 0:
                    pool.wait_ge(weights_in, 16 * 6)
                pool.tensor_tensor(x_rows[:], x_rows[:], bias_p[:].unsqueeze(1).to_broadcast([P, TILES, C]), ALU.add).then_inc(x_biased, 1)

            def late(i):
                pool.wait_ge(zero_filled, 16 * ZERO_FILLS)
                pool.wait_ge(x1_copied, i + 1)
                pool.wait_ge(slots_done, i + 1)
                for t in range(TILES):
                    for a in range(2):
                        pool.indirect_dma_start(d["xs"], bass.IndirectOffsetOnAxis(ap=slots[:, a, t:t + 1], axis=0),
                                                x1_copy[:, t, :], None, bounds_check=TRASH - 1, oob_is_err=False).then_inc(scattered, 16)

            bias(0)
            bias(1)
            late(0)
            with pool.Fori(2, BATCHES) as i:
                bias(i)
                late(i - 1)
            late(BATCHES - 1)
            pool.wait_ge(scattered, 32 * TILES * BATCHES)

        @block.scalar
        def _(act):
            act.wait_ge(weights_in, 16 * 6)
            for hi, raw in ((wkv_hi, wkv_raw), (wq_hi, wq_raw), (wp_hi, wp_raw), (wr_hi, wr_raw)):
                act.activation(hi[:], raw[:], ACT.Copy).then_inc(weights_hi, 1)
            act.wait_ge(consts, CONSTS)
            act.activation(kv_hi[:, :, 4 * P:], ones_f[:].unsqueeze(1).to_broadcast([P, TILES, P]), ACT.Copy).then_inc(weights_hi, 1)

            def split_xT(i):
                act.wait_ge(xT_in, 16 * i + 16)
                act.activation(xT_hi[:], xT_raw[:], ACT.Copy).then_inc(xT_hi_done, 1)

            def late(i, turn):
                for c in range(CH):
                    for h in range(2):
                        bank, n = turn.take()
                        act.wait_ge(bank_full, n + 1)
                        act.activation(x1T_hi[:, c, bass.ts(h, HALF)], ps[:, bank, :], ACT.Copy).then_inc(x1T_hi_done, 1)
                turn.take()
                act.wait_ge(logit_done, i + 1)
                act.activation(expd[:], logit[:], ACT.Exp).then_inc(exp_done, 1)
                if not (isinstance(i, int) and i == 0):
                    act.wait_ge(scattered, 32 * TILES * i)
                act.activation(x1_copy[:], x1[:], ACT.Copy).then_inc(x1_copied, 1)

            def body(i, start, end):
                turn = turns(i)
                for t in range(TILES):
                    bank, n = turn.take()
                    act.wait_ge(bank_full, n + 1)
                    act.activation(kv_hi[:, t, 0:4 * P], ps[:, bank, :], ACT.Relu).then_inc(kv_hi_done, 1)
                for p in range(CH):
                    bank, n = turn.take()
                    act.wait_ge(bank_free, n + 1)
                    act.activation(vk_hi[:, p, :], vk_m[:, p, :], ACT.Copy).then_inc(vk_hi_done, 1)
                for h in range(2):
                    for p in range(CH):
                        bank, n = turn.take()
                        act.wait_ge(bank_full, n + 1)
                        act.activation(q_hi[:, p, bass.ts(h, HALF)], ps[:, bank, :], ACT.Relu).then_inc(q_hi_done, 1)
                if not end:
                    split_xT(i + 1)
                if not start:
                    late(i - 1, turn)
                for h in range(2):
                    for p in range(CH):
                        turn.take()
                        bank, n = turn.take()
                        act.wait_ge(bank_free, n + 1)
                        act.activation(mix_hi[:, p, bass.ts(h, HALF)], mix[:, p, :], ACT.Copy).then_inc(mix_hi_done, 1)

            split_xT(0)
            body(0, True, False)
            with act.Fori(1, BATCHES - 1) as i:
                body(i, False, False)
            body(BATCHES - 1, False, True)
            late(BATCHES - 1, turns(BATCHES))

        @block.vector
        def _(v):
            for j, (lo, raw, hi) in enumerate(((wkv_lo, wkv_raw, wkv_hi), (wq_lo, wq_raw, wq_hi), (wp_lo, wp_raw, wp_hi), (wr_lo, wr_raw, wr_hi))):
                v.wait_ge(weights_hi, j + 1)
                v.tensor_tensor(lo[:], raw[:], f32(hi[:]), ALU.subtract).then_inc(weights_split, 1)
            v.wait_ge(consts, CONSTS)

            def split_xT(i):
                v.wait_ge(xT_hi_done, i + 1)
                v.tensor_tensor(xT_lo[:], xT_raw[:], f32(xT_hi[:]), ALU.subtract).then_inc(xT_split, 1)

            def late(i, turn):
                for c in range(CH):
                    for h in range(2):
                        bank, n = turn.take()
                        v.wait_ge(x1T_hi_done, 4 * i + 2 * c + h + 1)
                        v.tensor_tensor(x1T_lo[:, c, bass.ts(h, HALF)], ps[:, bank, :], f32(x1T_hi[:, c, bass.ts(h, HALF)]), ALU.subtract).then_inc(bank_free, 1)
                bank, n = turn.take()
                v.wait_ge(bank_full, n + 1)
                v.tensor_tensor(logit[:], ps[:, bank, 0:TILES * EXPERTS].rearrange("p (t e) -> p t e", e=EXPERTS), along(bias_r[:], TILES), ALU.add).then_inc(bank_free, 1)
                chain = Chain(v, route_chain, i * ROUTE_STEPS)
                v.wait_ge(bank_free, n + 1)
                chain.step(v.tensor_reduce(row_m[:], logit[:], AX.X, ALU.max))
                chain.wait()
                v.tensor_tensor(logit[:], logit[:], across(row_m[:], EXPERTS), ALU.subtract).then_inc(logit_done, 1)
                v.wait_ge(exp_done, i + 1)
                chain.step(v.tensor_reduce(row_s[:], expd[:], AX.X, ALU.add))
                chain.then(v.reciprocal, row_s[:], row_s[:])
                chain.then(v.tensor_tensor, weight[:], expd[:], across(row_s[:], EXPERTS), ALU.mult)
                top_two(v, chain, first[:], second[:], weight[:], falling[:], row_m[:], (key0[:], key1[:]), TILES)
                chain.then(v.tensor_scalar, key0[:], weight[:], 0.0, None, ALU.is_gt)
                chain.then(v.tensor_tensor, second[:], second[:], key0[:], ALU.mult)
                chain.then(v.tensor_tensor, first[:], first[:], key0[:], ALU.mult)
                chain.then(v.tensor_tensor, key1[:], first[:], second[:], ALU.add)
                if not (isinstance(i, int) and i == 0):
                    v.wait_ge(slots_stored, 32 * i)
                chain.then(v.tensor_tensor, key0[:], first[:], weight[:], ALU.mult)
                chain.then(v.tensor_reduce, gates[:, 0, :], key0[:], AX.X, ALU.add)
                chain.then(v.tensor_tensor, key0[:], second[:], weight[:], ALU.mult)
                chain.then(v.tensor_reduce, gates[:, 1, :], key0[:], AX.X, ALU.add)
                chain.then(v.tensor_tensor, gates[:, 2, :], key1[:, :, REAL], weight[:, :, REAL], ALU.mult)
                chain.then(v.tensor_copy, slot[:], key1[:])
                assert chain.n == ROUTE_STEPS, chain.n
                v.tensor_copy(mask[:], key1[:]).then_inc(mask_done, 1)

            def late_slots(i, turn):
                bank, n = turn.take()
                chain = Chain(v, slot_chain, i * SLOT_STEPS)
                v.wait_ge(bank_full, n + 1)
                if not (isinstance(i, int) and i == 0):
                    v.wait_ge(scattered, 32 * TILES * i)
                position = ps[:, bank, 0:TILES * EXPERTS].rearrange("p (t e) -> p t e", e=EXPERTS)
                chain.step(v.scalar_tensor_tensor(room[:], position, float(CAP), along(real[:], TILES), ALU.is_lt, ALU.mult))
                v.tensor_tensor(slot[:], position, along(slot0[:], TILES), ALU.add).then_inc(bank_free, 1)
                v.wait_ge(bank_free, n + 1)
                chain.then(v.tensor_tensor, slot[:], slot[:], room[:], ALU.mult)
                for a, chosen in ((0, first), (1, second)):
                    chain.then(v.tensor_tensor, room[:], slot[:], chosen[:], ALU.mult)
                    chain.then(v.tensor_reduce, picked[:, a, :], room[:], AX.X, ALU.add)
                chain.then(v.tensor_reduce, tile_sum[:], mask[:].rearrange("p t e -> p e t"), AX.X, ALU.add)
                chain.then(v.tensor_tensor, carry[:], carry[:], tile_sum[:], ALU.add)
                chain.then(v.tensor_copy, carry_b[:], carry[:])
                assert chain.n == SLOT_STEPS, chain.n
                chain.wait()
                v.tensor_scalar(slots[:], picked[:], float(TRASH), None, ALU.add).then_inc(slots_done, 1)

            def body(i, start, end):
                turn = turns(i)
                for t in range(TILES):
                    bank, n = turn.take()
                    v.wait_ge(kv_hi_done, TILES * i + t + 1)
                    v.scalar_tensor_tensor(kv_lo[:, t, :], ps[:, bank, :], 0.0, f32(kv_hi[:, t, 0:4 * P]), ALU.max, ALU.subtract).then_inc(bank_free, 1)
                for p in range(CH):
                    bank, n = turn.take()
                    v.wait_ge(bank_full, n + 1)
                    v.tensor_tensor(vk_m[:, p, :], ps[:, bank, 0:2 * P], same_head[:], ALU.mult).then_inc(bank_free, 1)
                for h in range(2):
                    for p in range(CH):
                        bank, n = turn.take()
                        v.wait_ge(q_hi_done, 2 * CH * i + CH * h + p + 1)
                        v.scalar_tensor_tensor(q_lo[:, p, bass.ts(h, HALF)], ps[:, bank, :], 0.0, f32(q_hi[:, p, bass.ts(h, HALF)]), ALU.max, ALU.subtract).then_inc(bank_free, 1)
                for p in range(CH):
                    v.wait_ge(vk_hi_done, CH * i + p + 1)
                    v.tensor_tensor(vk_lo[:, p, :], vk_m[:, p, :], f32(vk_hi[:, p, :]), ALU.subtract).then_inc(vk_split, 1)
                if not end:
                    split_xT(i + 1)
                if not start:
                    late(i - 1, turn)

                def split_mix(j):
                    h, p = j // CH, j % CH
                    v.wait_ge(mix_hi_done, 2 * CH * i + j + 1)
                    v.tensor_tensor(mix_lo[:, p, bass.ts(h, HALF)], mix[:, p, :], f32(mix_hi[:, p, bass.ts(h, HALF)]), ALU.subtract).then_inc(mix_split, 1)

                for j in range(2 * CH):
                    bank, n = turn.take()
                    v.wait_ge(bank_full, n + 1)
                    v.tensor_scalar(den[:], ps[:, bank, :], ATTN_EPS, None, ALU.add).then_inc(bank_free, 1)
                    v.wait_ge(bank_free, n + 1)
                    v.reciprocal(rden[:], den[:]).then_inc(recip_done, 1)
                    bank, n = turn.take()
                    v.wait_ge(bank_full, n + 1)
                    v.wait_ge(recip_done, 2 * CH * i + j + 1)
                    v.tensor_tensor(mix[:, j % CH, :], ps[:, bank, :], rden[:], ALU.mult).then_inc(bank_free, 1)
                    if j:
                        split_mix(j - 1)
                split_mix(2 * CH - 1)
                v.wait_ge(x_biased, i + 1)
                for j in range(TILES // 2):
                    bank, n = turn.take()
                    v.wait_ge(bank_full, n + 1)
                    v.tensor_tensor(rows[:, 2 * j:2 * j + 2, :], ps[:, bank, :].rearrange("p (t c) -> p t c", c=C), x_rows[:, 2 * j:2 * j + 2, :], ALU.add).then_inc(bank_free, 1)
                chain = Chain(v, ln_chain, i * LN_STEPS)
                v.wait_ge(bank_free, n + 1)
                layer_norm_stats(v, chain, rows[:], stats[:], mean[:], rstd[:], rr_tmp[:], TILES)
                assert chain.n == LN_STEPS, chain.n
                if not start:
                    v.wait_ge(x1_copied, i)
                    v.wait_ge(x1_stored, 16 * i)
                for t in range(TILES):
                    norm = v.tensor_scalar(x1[:, t, :], rows[:, t, :], mean[:, t:t + 1], rstd[:, t:t + 1], ALU.subtract, ALU.mult)
                norm.then_inc(x1_done, 1)
                if not start:
                    late_slots(i - 1, turn)

            split_xT(0)
            body(0, True, False)
            with v.Fori(1, BATCHES - 1) as i:
                body(i, False, False)
            body(BATCHES - 1, False, True)
            turn = turns(BATCHES)
            late(BATCHES - 1, turn)
            late_slots(BATCHES - 1, turn)

        @block.tensor
        def _(pe):
            def late(i, open_bank):
                pe.wait_ge(x1_done, i + 1)
                for c in range(CH):
                    for h in range(2):
                        out, n = open_bank()
                        for t in range(HTILES):
                            last = pe.transpose(out[:, bass.ts(t, P)], x1[:, HTILES * h + t, bass.ts(c, P)], ident[:])
                        last.then_inc(bank_full, 1)
                pe.wait_ge(bank_free, n + 1)
                out, n = open_bank()
                for t in range(TILES):
                    last = product(pe, out[:, bass.ts(t, EXPERTS)],
                                   [(x1T_hi[:, c, bass.ts(t, P)], x1T_lo[:, c, bass.ts(t, P)], wr_hi[:, c, :], wr_lo[:, c, :]) for c in range(CH)])
                last.then_inc(bank_full, 1)

            def late_slots(i, open_bank):
                out, n = open_bank()
                out = out[:, 0:TILES * EXPERTS].rearrange("p (t e) -> p t e", e=EXPERTS)
                pe.wait_ge(mask_done, i + 1)
                pe.matmul(out, before[:], mask[:], start=True, stop=False)
                for t in range(TILES - 1):
                    rest = TILES - 1 - t
                    pe.matmul(out[:, t + 1:, :], ones[:], along(mask[:, t, :], rest), start=False, stop=False)
                if not (isinstance(i, int) and i == 0):
                    pe.wait_ge(slots_done, i)
                pe.matmul(out, ones[:], along(carry_b[:], TILES), start=False, stop=True).then_inc(bank_full, 1)

            def body(i, start, end):
                turn = turns(i)

                def open_bank():
                    bank, n = turn.take()
                    wait_past(pe, bank_free, n + 1 - BANKS)
                    return ps[:, bank, :], n

                pe.wait_ge(xT_split, i + 1)
                for t in range(TILES):
                    out, n = open_bank()
                    product(pe, out, [(xT_hi[:, c, bass.ts(t, P)], xT_lo[:, c, bass.ts(t, P)], wkv_hi[:, c, :], wkv_lo[:, c, :])
                                      for c in range(CH)]).then_inc(bank_full, 1)
                pe.wait_ge(bank_free, n + 1)
                blocks = kv_hi[:].rearrange("p t (b n) -> p t b n", n=P)
                for p in range(CH):
                    out, n = open_bank()
                    for t in range(TILES):
                        v_ones = blocks[:, t, 2 + p::2 - p, :]
                        pe.matmul(out[:, 0:2 * P], kv_hi[:, t, bass.ts(p, P)], v_ones, start=(t == 0), stop=False)
                        pe.matmul(out[:, 0:P], kv_hi[:, t, bass.ts(p, P)], kv_lo[:, t, bass.ts(2 + p, P)], start=False, stop=False)
                        last = pe.matmul(out[:, 0:2 * P], kv_lo[:, t, bass.ts(p, P)], v_ones, start=False, stop=(t == TILES - 1))
                    last.then_inc(bank_full, 1)
                for h in range(2):
                    for p in range(CH):
                        out, q_n = open_bank()
                        product(pe, out, [(wq_hi[:, c, bass.ts(p, P)], wq_lo[:, c, bass.ts(p, P)], xT_hi[:, c, bass.ts(h, HALF)], xT_lo[:, c, bass.ts(h, HALF)])
                                          for c in range(CH)]).then_inc(bank_full, 1)
                if not start:
                    late(i - 1, open_bank)
                pe.wait_ge(bank_free, q_n + 1)
                pe.wait_ge(vk_split, CH * i + CH)
                for h in range(2):
                    for p in range(CH):
                        for part in (1, 0):
                            out, n = open_bank()
                            product(pe, out, [(vk_hi[:, p, bass.ts(part, P)], vk_lo[:, p, bass.ts(part, P)],
                                               q_hi[:, p, bass.ts(h, HALF)], q_lo[:, p, bass.ts(h, HALF)])]).then_inc(bank_full, 1)
                for j in range(TILES // 2):
                    if j % HTILES // 2 == 0 or j == HTILES // 2:
                        pe.wait_ge(mix_split, 2 * CH * i + CH * (1 + j // (HTILES // 2)))
                    out, n = open_bank()
                    for t in (2 * j, 2 * j + 1):
                        last = product(pe, out[:, bass.ts(t % 2, C)],
                                       [(mix_hi[:, p, bass.ts(t, P)], mix_lo[:, p, bass.ts(t, P)], wp_hi[:, p, :], wp_lo[:, p, :]) for p in range(CH)])
                    last.then_inc(bank_full, 1)
                if not start:
                    late_slots(i - 1, open_bank)

            pe.wait_ge(weights_split, 4)
            pe.wait_ge(weights_hi, 5)
            pe.wait_ge(consts, CONSTS)
            body(0, True, False)
            with pe.Fori(1, BATCHES - 1) as i:
                body(i, False, False)
            body(BATCHES - 1, False, True)
            turn = turns(BATCHES)

            def open_bank():
                bank, n = turn.take()
                pe.wait_ge(bank_free, n + 1 - BANKS)
                return ps[:, bank, :], n

            late(BATCHES - 1, open_bank)
            late_slots(BATCHES - 1, open_bank)


def stage_b(nc, d):
    EACH = 2 * ICH + HTILES // 2 + 2 * CH + HTILES // 2
    PROLOGUE = 2 * CH
    with ExitStack() as ctx:
        def sb(name, shape, dt=F32):
            return ctx.enter_context(nc.sbuf_tensor("b_" + name, shape, dt))

        def sem(name):
            return ctx.enter_context(nc.semaphore("b_" + name))

        ps = ctx.enter_context(nc.psum_tensor("b_ps", [P, BANKS, 512], F32))
        ident = sb("ident", [P, P])
        xs = sb("xs", [P, TILES, C])
        xsT_hi, xsT_lo = sb("xsT_hi", [P, CH, CAP], F32R), sb("xsT_lo", [P, CH, CAP], F32R)
        win_raw, win_hi, win_lo = sb("win_raw", [P, CH, INTER]), sb("win_hi", [P, CH, INTER], F32R), sb("win_lo", [P, CH, INTER], F32R)
        wout_raw, wout_hi, wout_lo = sb("wout_raw", [P, ICH, C]), sb("wout_hi", [P, ICH, C], F32R), sb("wout_lo", [P, ICH, C], F32R)
        hT_hi, hT_lo = sb("hT_hi", [P, 2, ICH, HALF], F32R), sb("hT_lo", [P, 2, ICH, HALF], F32R)
        results = sb("results", [P, TILES, C])

        ident_done, xs_in, win_in, wout_in = sem("ident_done"), sem("xs_in"), sem("win_in"), sem("wout_in")
        win_hi_done, win_split = sem("win_hi_done"), sem("win_split")
        wout_hi_done, wout_split = sem("wout_hi_done"), sem("wout_split")
        bank_full, bank_free = sem("bank_full"), sem("bank_free")
        xsT_hi_done, hT_hi_done, results_stored = sem("xsT_hi_done"), sem("hT_hi_done"), sem("results_stored")

        def group(i, n):
            return PROLOGUE + i * EACH + n

        def turns(i):
            return Turns(group(i, 0), PROLOGUE, range(BANKS))

        OUT_A, ROWS, OUT_B = 2 * ICH, 2 * ICH + HTILES // 2, 2 * ICH + HTILES // 2 + 2 * CH
        block = ctx.enter_context(nc.Block())

        @block.sync
        def _(sp):
            def load_rows(e):
                sp.dma_start(xs[:], d["xs"][bass.ds(e * CAP, CAP), :].rearrange("(t p) c -> p t c", p=P)).then_inc(xs_in, 16)

            def load_in(e):
                sp.dma_start(win_raw[:], d["w_in"][bass.ds(e * C, C), :].rearrange("(a p) n -> p a n", p=P)).then_inc(win_in, 16)

            def load_out(e):
                sp.dma_start(wout_raw[:], d["w_out"][bass.ds(e * INTER, INTER), :].rearrange("(a p) n -> p a n", p=P)).then_inc(wout_in, 16)

            def body(e, end):
                if not end:
                    sp.wait_ge(bank_full, PROLOGUE if isinstance(e, int) and e == 0 else group(e - 1, OUT_B))
                    load_rows(e + 1)
                    sp.wait_ge(win_split, e + 1)
                    load_in(e + 1)
                    sp.wait_ge(wout_split, e + 1)
                    load_out(e + 1)
                for h, at in ((0, ROWS), (1, EACH)):
                    sp.wait_ge(bank_free, group(e, at) if h == 0 or not end else group(e, EACH - 2 * CH))
                    sp.dma_start(d["ys"][bass.ds(e * CAP + h * HALF, HALF), :].rearrange("(t p) c -> p t c", p=P),
                                 results[:, bass.ts(h, HTILES), :]).then_inc(results_stored, 16)

            load_rows(0)
            load_in(0)
            load_out(0)
            body(0, False)
            with sp.Fori(1, REAL - 1) as e:
                body(e, False)
            body(REAL - 1, True)
            sp.wait_ge(results_stored, 32 * REAL)

        @block.gpsimd
        def _(pool):
            pool.memset(ident[:], 0.0).then_inc(ident_done, 1)
            pool.wait_ge(ident_done, 1)
            pool.affine_select(out=ident[:], in_=ident[:], compare_op=ALU.not_equal, fill=1.0,
                               base=0, pattern=[[-1, P]], channel_multiplier=1).then_inc(ident_done, 1)

        @block.scalar
        def _(act):
            def split_in(e):
                act.wait_ge(win_in, 16 * e + 16)
                act.activation(win_hi[:], win_raw[:], ACT.Copy).then_inc(win_hi_done, 1)

            def split_out(e):
                act.wait_ge(wout_in, 16 * e + 16)
                act.activation(wout_hi[:], wout_raw[:], ACT.Copy).then_inc(wout_hi_done, 1)

            def split_rows(turn):
                for c in range(CH):
                    for h in range(2):
                        bank, n = turn.take()
                        act.wait_ge(bank_full, n + 1)
                        act.activation(xsT_hi[:, c, bass.ts(h, HALF)], ps[:, bank, :], ACT.Copy).then_inc(xsT_hi_done, 1)

            def body(e, end):
                turn = turns(e)
                if not (isinstance(e, int) and e == 0):
                    act.wait_ge(bank_full, group(e - 1, EACH))
                split_out(e)
                for h in range(2):
                    for k in range(ICH):
                        bank, n = turn.take()
                        act.wait_ge(bank_full, n + 1)
                        act.activation(hT_hi[:, h, k, :], ps[:, bank, :], ACT.Relu).then_inc(hT_hi_done, 1)
                if not end:
                    split_in(e + 1)
                    for _ in range(HTILES // 2):
                        turn.take()
                    split_rows(turn)

            split_in(0)
            split_rows(Turns(0, 0, range(BANKS)))
            body(0, False)
            with act.Fori(1, REAL - 1) as e:
                body(e, False)
            body(REAL - 1, True)

        @block.vector
        def _(v):
            def split_in(e):
                v.wait_ge(win_hi_done, e + 1)
                v.tensor_tensor(win_lo[:], win_raw[:], f32(win_hi[:]), ALU.subtract).then_inc(win_split, 1)

            def split_out(e):
                v.wait_ge(wout_hi_done, e + 1)
                v.tensor_tensor(wout_lo[:], wout_raw[:], f32(wout_hi[:]), ALU.subtract).then_inc(wout_split, 1)

            def split_rows(e, turn):
                for c in range(CH):
                    for h in range(2):
                        bank, n = turn.take()
                        v.wait_ge(xsT_hi_done, 2 * CH * e + 2 * c + h + 1)
                        v.tensor_tensor(xsT_lo[:, c, bass.ts(h, HALF)], ps[:, bank, :], f32(xsT_hi[:, c, bass.ts(h, HALF)]), ALU.subtract).then_inc(bank_free, 1)

            def store_pairs(e, h, turn):
                if not (isinstance(e, int) and e == 0):
                    v.wait_ge(results_stored, 32 * e)
                for j in range(HTILES // 2):
                    bank, n = turn.take()
                    v.wait_ge(bank_full, n + 1)
                    t = HTILES * h + 2 * j
                    v.tensor_copy(results[:, t:t + 2, :], ps[:, bank, :].rearrange("p (t c) -> p t c", c=C)).then_inc(bank_free, 1)

            def body(e, end):
                turn = turns(e)
                split_out(e)
                for h in range(2):
                    for k in range(ICH):
                        bank, n = turn.take()
                        v.wait_ge(hT_hi_done, 2 * ICH * e + ICH * h + k + 1)
                        v.scalar_tensor_tensor(hT_lo[:, h, k, :], ps[:, bank, :], 0.0, f32(hT_hi[:, h, k, :]), ALU.max, ALU.subtract).then_inc(bank_free, 1)
                if not end:
                    split_in(e + 1)
                store_pairs(e, 0, turn)
                if not end:
                    split_rows(e + 1, turn)
                store_pairs(e, 1, turn)

            split_in(0)
            split_rows(0, Turns(0, 0, range(BANKS)))
            body(0, False)
            with v.Fori(1, REAL - 1) as e:
                body(e, False)
            body(REAL - 1, True)

        @block.tensor
        def _(pe):
            def opener(turn):
                def open_bank():
                    bank, n = turn.take()
                    wait_past(pe, bank_free, n + 1 - BANKS)
                    return ps[:, bank, :], n
                return open_bank

            def turn_rows(e, open_bank):
                pe.wait_ge(xs_in, 16 * e + 16)
                for c in range(CH):
                    for h in range(2):
                        out, n = open_bank()
                        for t in range(HTILES):
                            last = pe.transpose(out[:, bass.ts(t, P)], xs[:, HTILES * h + t, bass.ts(c, P)], ident[:])
                        last.then_inc(bank_full, 1)

            def hidden(e, h, open_bank):
                for k in range(ICH):
                    out, n = open_bank()
                    product(pe, out, [(win_hi[:, c, bass.ts(k, P)], win_lo[:, c, bass.ts(k, P)],
                                       xsT_hi[:, c, bass.ts(h, HALF)], xsT_lo[:, c, bass.ts(h, HALF)]) for c in range(CH)]).then_inc(bank_full, 1)
                return n

            def result(h, open_bank):
                for j in range(HTILES // 2):
                    out, n = open_bank()
                    for t in (2 * j, 2 * j + 1):
                        last = product(pe, out[:, bass.ts(t % 2, C)],
                                       [(hT_hi[:, h, k, bass.ts(t, P)], hT_lo[:, h, k, bass.ts(t, P)], wout_hi[:, k, :], wout_lo[:, k, :])
                                        for k in range(ICH)])
                    last.then_inc(bank_full, 1)

            def body(e, end):
                open_bank = opener(turns(e))
                pe.wait_ge(win_split, e + 1)
                pe.wait_ge(bank_free, PROLOGUE if isinstance(e, int) and e == 0 else group(e - 1, OUT_B))
                last_a = hidden(e, 0, open_bank)
                last_b = hidden(e, 1, open_bank)
                pe.wait_ge(wout_split, e + 1)
                pe.wait_ge(bank_free, last_a + 1)
                result(0, open_bank)
                if not end:
                    turn_rows(e + 1, open_bank)
                pe.wait_ge(bank_free, last_b + 1)
                result(1, open_bank)

            pe.wait_ge(ident_done, 2)
            turn_rows(0, opener(Turns(0, 0, range(BANKS))))
            body(0, False)
            with pe.Fori(1, REAL - 1) as e:
                body(e, False)
            body(REAL - 1, True)


def stage_c(nc, d):
    HALVES = 2
    ORDER = [("q", j) for j in range(4)] + [("k", j) for j in range(4)] + [("v", j) for j in range(4)] + [("score", 0)]
    for s in range(TILES):
        ORDER += [("score", s + 1)] if s + 1 < TILES else []
        ORDER += [("mix", s - 1)] if s else []
        ORDER += [("turn", s)]
        ORDER += [("x3T", 0), ("gate", 0)] if s == TILES - 2 else []
    ORDER += [("mix", TILES - 1), ("scoreT", 0)]
    for h in range(HALVES):
        ORDER += [("latent", h), ("up", h)]
        ORDER += [("x3T", 1), ("gate", 1)] if h == 0 else []
        ORDER += [("expert", h)]
        ORDER += [("scoreT", 1)] if h == 0 else [("x2T", 0)]
        ORDER += [("comb", h), ("out", h)]
    V_BANKS = {"q": 1, "k": 1, "v": 1, "mix": 1, "turn": 2, "x3T": 2, "gate": 1, "scoreT": 1, "latent": 1, "x2T": 4, "comb": 1, "out": 2}
    S_BANKS = {"score": 2, "up": EXPERTS, "expert": EXPERTS}
    V_AT, S_AT, V_EACH, S_EACH = {}, {}, 0, 0
    for unit in ORDER:
        V_EACH += V_BANKS.get(unit[0], 0)
        S_EACH += S_BANKS.get(unit[0], 0)
        V_AT[unit], S_AT[unit] = V_EACH, S_EACH
    PROLOGUE = V_BANKS["x2T"]
    HIDDEN = 2 * EXPERTS
    RING_R, RING_H = 2, 2
    GATHER = 4
    LN_STEPS = TILES + MEAN_STEPS + RR_STEPS
    HALF_LN_STEPS = HTILES + MEAN_STEPS + RR_STEPS
    PRE_STEPS = 2 * TILES + LN_STEPS
    ROUTE_STEPS = 2 + 8 + 3 + TOP_STEPS + 5
    CONSTS = 2 + EXPERTS

    with ExitStack() as ctx:
        def sb(name, shape, dt=F32):
            return ctx.enter_context(nc.sbuf_tensor("c_" + name, shape, dt))

        def pair(name, shape):
            return sb(name + "_hi", shape, F32R), sb(name + "_lo", shape, F32R)

        def sem(name):
            return ctx.enter_context(nc.semaphore("c_" + name))

        ps = ctx.enter_context(nc.psum_tensor("c_ps", [P, BANKS, 512], F32))
        wq_hi, wq_lo = pair("wq", [P, CH, C])
        wk_hi, wk_lo = pair("wk", [P, CH, C])
        wv_hi, wv_lo = pair("wv", [P, CH, C])
        gate_hi, gate_lo = pair("gate", [P, CH, EXPERTS])
        fc1_hi, fc1_lo = pair("fc1", [P, CH, LATENT])
        fc2_hi, fc2_lo = pair("fc2", [P, 1, C])
        w1_hi, w1_lo = pair("w1", [P, EXPERTS, P])
        w2_hi, w2_lo = pair("w2", [P, EXPERTS, LATENT])
        up_hi, up_lo = pair("up", [P, CH, SHARED])
        down_hi, down_lo = pair("down", [P, SHARED // P, C])
        bias_q, bias_k, bias_qs = sb("bias_q", [P, CH]), sb("bias_k", [P, CH]), sb("bias_qs", [P, CH])
        bias_v, bias_corr = sb("bias_v", [P, C]), sb("bias_corr", [P, EXPERTS])
        ident, falling = sb("ident", [P, P]), sb("falling", [P, EXPERTS])
        x2, x3 = sb("x2", [P, TILES, C]), sb("x3", [P, TILES, C])
        x2T = sb("x2T", [P, 2, CH, SEQ], F32R)
        x2T_hi, x2T_lo = x2T[:, 0], x2T[:, 1]
        score_rows = x2T[:].rearrange("p a c s -> p (a c s)").bitcast(F32)
        place = sb("place", [P, 16 * SEQ], F32R)
        q_hi, q_lo, k_hi, k_lo = (place[:, j * CH * SEQ:(j + 1) * CH * SEQ].rearrange("p (c s) -> p c s", c=CH) for j in range(4))
        v_hi, v_lo = (place[:, (8 + 2 * j) * SEQ:(10 + 2 * j) * SEQ].rearrange("p (t c) -> p t c", c=C) for j in range(2))
        probT_hi, probT_lo = (place[:, (12 + j) * SEQ:(13 + j) * SEQ].rearrange("p (t s) -> p t s", s=P) for j in range(2))
        hid_hi, hid_lo = (place[:, 8 * j * SEQ:8 * (j + 1) * SEQ].rearrange("p (k s) -> p k s", s=HALF) for j in range(2))
        prob = sb("prob", [P, 2, SEQ])
        neg_max, row_sum, row_inv = sb("neg_max", [P, TILES]), sb("row_sum", [P, TILES]), sb("row_inv", [P, TILES])
        x3T_hi, x3T_lo = pair("x3T", [P, CH, HALF])
        lat_hi, lat_lo = pair("lat", [P, HALF])
        comb_hi, comb_lo = pair("comb", [P, HALF])
        relu, square = sb("relu", [P, RING_R, HALF]), sb("square", [P, RING_H, HALF])
        gathered = sb("gathered", [P, GATHER, 2, C])
        slots, gates = sb("slots", [P, 2, TILES], U32), sb("gates", [P, 3, TILES])
        stats, mean = sb("stats", [P, TILES, 6]), sb("mean", [P, TILES])
        rstd, rr_tmp = sb("rstd", [P, TILES]), sb("rr_tmp", [P, 3, TILES])
        expd, score, choice = (sb(n, [P, HTILES, EXPERTS]) for n in ("expd", "score", "choice"))
        first, second, key0, key1 = (sb(n, [P, HTILES, EXPERTS]) for n in ("first", "second", "key0", "key1"))
        row_m, row_s = sb("row_m", [P, HTILES]), sb("row_s", [P, HTILES])
        group_m, group_n = sb("group_m", [P, HTILES, GROUPS]), sb("group_n", [P, HTILES, GROUPS])
        score_et, scoreT = sb("score_et", [P, EXPERTS, HTILES]), sb("scoreT", [EXPERTS * HTILES, P])

        consts, biases_in = sem("consts"), sem("biases_in")
        weight_in = [sem("weight_in0"), sem("weight_in1")]
        weight_hi, weight_split = sem("weight_hi"), sem("weight_split")
        v_full, v_free = sem("v_full"), sem("v_free")
        s_full, s_free = sem("s_full"), sem("s_free")
        slots_in, gates_in, x2_in = sem("slots_in"), sem("gates_in"), sem("x2_in")
        rows_in = [sem(f"rows_in{j}") for j in range(GATHER)]
        combined, x2_done, bias_added = sem("combined"), sem("x2_done"), sem("bias_added")
        pre_chain, ln_chain, route_chain = sem("pre_chain"), sem("ln_chain"), sem("route_chain")
        hi_done = sem("hi_done")
        max_done, inv_done, x3_done = sem("max_done"), sem("inv_done"), sem("x3_done")
        exp_done, score_done, scores_stored, scores_in = sem("exp_done"), sem("score_done"), sem("scores_stored"), sem("scores_in")
        scaled, squared, hid_hi_done, hid_split = sem("scaled"), sem("squared"), sem("hid_hi_done"), sem("hid_split")
        out_done, out_stored = sem("out_done"), sem("out_stored")

        WEIGHTS = [("wq", wq_hi, wq_lo, 0, CH, SCALE), ("wk", wk_hi, wk_lo, 0, CH, 1.0), ("wv", wv_hi, wv_lo, 0, CH, 1.0),
                   ("gateT", gate_hi, gate_lo, 0, CH, 1.0), ("fc1T", fc1_hi, fc1_lo, 0, CH, 1.0),
                   ("upT", up_hi, up_lo, 0, 1, 1.0), ("upT", up_hi, up_lo, 1, 2, 1.0),
                   ("w1T", w1_hi, w1_lo, 0, EXPERTS, 1.0), ("w2T", w2_hi, w2_lo, 0, EXPERTS, 1.0),
                   ("fc2T", fc2_hi, fc2_lo, 0, 1, 1.0),
                   ("downT", down_hi, down_lo, 0, 4, 1.0), ("downT", down_hi, down_lo, 4, 8, 1.0)]
        EARLY = 3

        def staged(j):
            _, hi, _, a, b, _ = WEIGHTS[j]
            return prob[:, j % 2, 0:(b - a) * hi.shape[2]].rearrange("p (k n) -> p k n", k=b - a)

        def v_turns(i):
            return Turns(PROLOGUE + i * V_EACH, PROLOGUE, range(4, 8))

        def s_turns(i):
            return Turns(i * S_EACH, 0, range(0, 4))

        def v_upto(i, unit):
            skipped = V_BANKS["x2T"] if isinstance(i, int) and i == BATCHES - 1 and V_AT[unit] >= V_AT["x2T", 0] else 0
            return PROLOGUE + i * V_EACH + V_AT[unit] - skipped

        def s_upto(i, unit):
            return i * S_EACH + S_AT[unit]

        def x2T_upto(i):
            return PROLOGUE if isinstance(i, int) and i == 0 else v_upto(i - 1, ("x2T", 0))

        HI_BANKS = {k: n for k, n in V_BANKS.items() if k in ("q", "k", "v", "turn", "x3T", "latent", "comb", "x2T")}
        HI_EACH = sum(HI_BANKS.get(unit[0], 0) for unit in ORDER)

        def order(end):
            return [unit for unit in ORDER if not (end and unit[0] == "x2T")]

        block = ctx.enter_context(nc.Block())

        @block.sync
        def _(sp):
            def load_plan(b):
                sp.dma_start(slots[:].rearrange("p a t -> p (a t)"), d["slots"][bass.ds(b * P, P), :]).then_inc(slots_in, 16)
                sp.dma_start(gates[:].rearrange("p a t -> p (a t)"), d["gates"][bass.ds(b * P, P), :]).then_inc(gates_in, 16)

            def load_rows(b):
                sp.dma_start(x2[:], d["x1"][bass.ds(b * SEQ, SEQ), :].rearrange("(t p) c -> p t c", p=P)).then_inc(x2_in, 16)

            def spread_scores(b, h):
                sp.wait_ge(v_free, v_upto(b, ("scoreT", h)))
                sp.dma_start(d["score_rows"][bass.ds(2 * b + h, 1), :].rearrange("a (r s) -> (a r) s", s=P), scoreT[:]).then_inc(scores_stored, 16)
                sp.wait_ge(scores_stored, 32 * b + 16 * h + 16)
                if h == 1:
                    sp.wait_ge(scaled, 2 * EXPERTS * b + EXPERTS)
                sp.dma_start(score_rows, d["score_rows"][bass.ds(2 * b + h, 1), :].to_broadcast([P, EXPERTS * HALF])).then_inc(scores_in, 16)

            def store(b, h):
                sp.wait_ge(out_done, 2 * b + h + 1)
                sp.dma_start(d["out"][bass.ds(b * SEQ + h * HALF, HALF), :].rearrange("(t p) c -> p t c", p=P),
                             x3[:, bass.ts(h, HTILES), :]).then_inc(out_stored, 16)

            def body(b, end):
                if not end:
                    sp.wait_ge(x2_done, b + 1)
                    load_plan(b + 1)
                spread_scores(b, 0)
                if not end:
                    sp.wait_ge(x3_done, 2 * b + 2)
                    load_rows(b + 1)
                spread_scores(b, 1)
                store(b, 0)
                store(b, 1)

            load_plan(0)
            load_rows(0)
            sp.dma_start(bias_q[:], d["bq"]).then_inc(biases_in, 16)
            sp.dma_start(bias_k[:], d["bk"]).then_inc(biases_in, 16)
            sp.dma_start(bias_v[:], d["bv"].partition_broadcast(P)).then_inc(biases_in, 16)
            sp.dma_start(bias_corr[:], d["corr"].partition_broadcast(P)).then_inc(biases_in, 16)
            for j, (w, _, _, a, b, _) in enumerate(WEIGHTS):
                wait_past(sp, weight_split, j - 1)
                sp.dma_start(staged(j), d[w].rearrange("(k p) n -> p k n", p=P)[:, a:b, :] if w not in ("w1T", "w2T")
                             else d[w].rearrange("p (k n) -> p k n", k=EXPERTS)).then_inc(weight_in[j % 2], 16)
            body(0, False)
            with sp.Fori(1, BATCHES - 1) as b:
                body(b, False)
            body(BATCHES - 1, True)
            sp.wait_ge(out_stored, 32 * BATCHES)

        @block.gpsimd
        def _(pool):
            pool.memset(ident[:], 0.0).then_inc(consts, 1)
            for e in range(EXPERTS):
                pool.memset(falling[:, e:e + 1], float(EXPERTS - e)).then_inc(consts, 1)
            pool.wait_ge(consts, 1)
            pool.affine_select(out=ident[:], in_=ident[:], compare_op=ALU.not_equal, fill=1.0,
                               base=0, pattern=[[-1, P]], channel_multiplier=1).then_inc(consts, 1)

            def gather(b, t0):
                for t in range(t0, t0 + GATHER):
                    producer, upto = (combined, TILES * b + t - GATHER + 1) if t0 else (slots_in, 16 * b + 16)
                    pool.to_reg(upto)
                    pool.wait_ge(biases_in, 64)
                    pool.wait_ge(producer, upto)
                    for a in range(2):
                        pool.indirect_dma_start(gathered[:, t % GATHER, a, :], None, d["ys"],
                                                bass.IndirectOffsetOnAxis(ap=slots[:, a, t:t + 1], axis=0),
                                                bounds_check=TRASH + P - 1, oob_is_err=False).then_inc(rows_in[t % GATHER], 16)

            def scale(b, h):
                pool.wait_ge(scores_in, 32 * b + 16 * h + 16)
                for e in range(EXPERTS):
                    u = 2 * HIDDEN * b + HIDDEN * h + EXPERTS + e
                    pool.wait_ge(s_free, s_upto(b, ("expert", h)) - EXPERTS + e + 1)
                    pool.wait_ge(hid_split, u - RING_H + 1)
                    pool.tensor_tensor(square[:, (EXPERTS + e) % RING_H, :], relu[:, (EXPERTS + e) % RING_R, :],
                                       score_rows[:, bass.ts(e, HALF)], ALU.mult).then_inc(scaled, 1)

            def add_bias(b):
                pool.wait_ge(v_full, x2T_upto(b))
                pool.tensor_tensor(x2[:], x2[:], bias_v[:].unsqueeze(1).to_broadcast([P, TILES, C]), ALU.add).then_inc(bias_added, 1)

            def body(b, end):
                if not end:
                    gather(b + 1, 0)
                scale(b, 0)
                if not end:
                    gather(b + 1, GATHER)
                scale(b, 1)
                if not end:
                    add_bias(b + 1)

            gather(0, 0)
            gather(0, GATHER)
            add_bias(0)
            body(0, False)
            with pool.Fori(1, BATCHES - 1) as b:
                body(b, False)
            body(BATCHES - 1, True)

        @block.scalar
        def _(act):
            def split_weights(js):
                for j in js:
                    _, hi, _, a, b, scale = WEIGHTS[j]
                    act.wait_ge(weight_in[j % 2], 16 * (j // 2) + 16)
                    act.activation(hi[:, a:b, :], staged(j), ACT.Copy, scale=scale).then_inc(weight_hi, 1)

            def turn_rows(turn):
                for c in range(CH):
                    for h in range(2):
                        bank, n = turn.take()
                        act.wait_ge(v_full, n + 1)
                        act.activation(x2T_hi[:, c, bass.ts(h, HALF)], ps[:, bank, :], ACT.Copy).then_inc(hi_done, 1)

            def body(b, end):
                turn, s_turn = v_turns(b), s_turns(b)

                def copy_hi(out, func=ACT.Copy, **kw):
                    bank, n = turn.take()
                    act.wait_ge(v_full, n + 1)
                    act.activation(out, ps[:, bank, :], func, **kw).then_inc(hi_done, 1)

                for kind, j in order(end):
                    if kind == "q":
                        copy_hi(q_hi[:, j % CH, bass.ts(j // CH, HALF)], ACT.Identity, bias=bias_qs[:, j % CH:j % CH + 1])
                    elif kind == "k":
                        copy_hi(k_hi[:, j % CH, bass.ts(j // CH, HALF)], ACT.Identity, bias=bias_k[:, j % CH:j % CH + 1])
                    elif kind == "v":
                        copy_hi(v_hi[:, 2 * j:2 * j + 2, :].rearrange("p t c -> p (t c)"))
                    elif kind == "score":
                        bank, n = s_turn.take()
                        s_turn.take()
                        act.wait_ge(max_done, TILES * b + j + 1)
                        act.activation(prob[:, j % 2, :], ps[:, bank:bank + 2, :].rearrange("p a n -> p (a n)"), ACT.Exp,
                                       bias=neg_max[:, j:j + 1], accum_out=row_sum[:, j:j + 1]).then_inc(s_free, 2)
                    elif kind == "turn":
                        for g in range(2):
                            copy_hi(probT_hi[:, 4 * g:4 * g + 4, :].rearrange("p t s -> p (t s)"))
                    elif kind == "x3T":
                        for c in range(CH):
                            copy_hi(x3T_hi[:, c, :])
                    elif kind == "gate":
                        bank, n = turn.take()
                        act.wait_ge(v_full, n + 1)
                        act.activation(expd[:].rearrange("p t e -> p (t e)"), ps[:, bank, 0:HTILES * EXPERTS], ACT.Exp, scale=-1.0).then_inc(exp_done, 1)
                    elif kind == "latent":
                        copy_hi(lat_hi[:])
                    elif kind == "comb":
                        copy_hi(comb_hi[:])
                    elif kind == "x2T":
                        act.wait_ge(scaled, 2 * EXPERTS * (b + 1))
                        turn_rows(turn)
                    elif kind in ("up", "expert"):
                        base, lag = (0, 1) if kind == "up" else (EXPERTS, 2)
                        u0 = 2 * HIDDEN * b + HIDDEN * j + base
                        for k in range(EXPERTS + lag):
                            if k < EXPERTS:
                                bank, n = s_turn.take()
                                act.wait_ge(s_full, n + 1)
                                wait_past(act, squared, u0 + k - RING_R + 1)
                                if kind == "up" or k < RING_R:
                                    wait_past(act, hid_hi_done, u0 + k - RING_R + 1)
                                act.activation(relu[:, k % RING_R, :], ps[:, bank, :], ACT.Relu).then_inc(s_free, 1)
                            if k >= lag:
                                g = k - lag
                                if kind == "up":
                                    act.wait_ge(s_free, s_upto(b, (kind, j)) - EXPERTS + g + 1)
                                    act.activation(hid_hi[:, base + g, :], relu[:, g % RING_R, :], ACT.Square).then_inc(hid_hi_done, 1)
                                else:
                                    act.wait_ge(squared, u0 + g + 1)
                                    act.activation(hid_hi[:, base + g, :], square[:, g % RING_H, :], ACT.Copy).then_inc(hid_hi_done, 1)
                    else:
                        for _ in range(V_BANKS[kind]):
                            turn.take()

            split_weights(range(EARLY))
            turn_rows(Turns(0, 0, range(4, 8)))
            split_weights(range(EARLY, len(WEIGHTS)))
            act.wait_ge(biases_in, 64)
            act.wait_ge(weight_split, len(WEIGHTS) + 1)
            body(0, False)
            with act.Fori(1, BATCHES - 1) as b:
                body(b, False)
            body(BATCHES - 1, True)

        @block.vector
        def _(v):
            def split_weights(js):
                for j in js:
                    _, hi, lo, a, b, scale = WEIGHTS[j]
                    v.wait_ge(weight_hi, j + 1)
                    v.scalar_tensor_tensor(lo[:, a:b, :], staged(j), scale, f32(hi[:, a:b, :]), ALU.mult, ALU.subtract).then_inc(weight_split, 1)

            def split_rows(b, hi_n, turn):
                for c in range(CH):
                    for h in range(2):
                        bank, n = turn.take()
                        v.wait_ge(hi_done, hi_n + 2 * c + h + 1)
                        v.tensor_tensor(x2T_lo[:, c, bass.ts(h, HALF)], ps[:, bank, :], f32(x2T_hi[:, c, bass.ts(h, HALF)]), ALU.subtract).then_inc(v_free, 1)

            def normed(chain, out, rows, t0, n):
                layer_norm_stats(v, chain, rows[:, t0:t0 + n, :], stats[:, 0:n, :], mean[:, 0:n], rstd[:, 0:n], rr_tmp[:, :, 0:n], n)
                for t in range(n):
                    last = v.tensor_scalar(out[:, t0 + t, :], rows[:, t0 + t, :], mean[:, t:t + 1], rstd[:, t:t + 1], ALU.subtract, ALU.mult)
                return last

            def combine(b):
                chain = Chain(v, pre_chain, b * PRE_STEPS)
                v.wait_ge(x2_in, 16 * b + 16)
                v.wait_ge(gates_in, 16 * b + 16)
                for t in range(TILES):
                    v.wait_ge(rows_in[t % GATHER], 32 * (TILES // GATHER * b + t // GATHER + 1))
                    rows, place = x2[:, t, :], gathered[:, t % GATHER]
                    chain.step(v.scalar_tensor_tensor(rows, rows, gates[:, 2, t:t + 1], rows, ALU.mult, ALU.add))
                    chain.then(v.scalar_tensor_tensor, rows, place[:, 0, :], gates[:, 0, t:t + 1], rows, ALU.mult, ALU.add)
                    chain.wait()
                    v.scalar_tensor_tensor(rows, place[:, 1, :], gates[:, 1, t:t + 1], rows, ALU.mult, ALU.add).then_inc(combined, 1)
                v.wait_ge(combined, TILES * (b + 1))
                normed(chain, x2, x2, 0, TILES).then_inc(x2_done, 1)
                assert chain.n == PRE_STEPS, chain.n

            def route(b, h, n):
                chain = Chain(v, route_chain, (2 * b + h) * ROUTE_STEPS)
                v.wait_ge(exp_done, 2 * b + h + 1)
                v.tensor_scalar(expd[:], expd[:], 1.0, None, ALU.add).then_inc(v_free, 1)
                v.wait_ge(v_free, n + 1)
                chain.step(v.reciprocal(score[:], expd[:]))
                chain.then(v.tensor_tensor, choice[:], score[:], along(bias_corr[:], HTILES), ALU.add)
                groups = choice[:].rearrange("p t (g e) -> p (t g) e", g=GROUPS)
                keys = key0[:].rearrange("p t (g e) -> p (t g) e", g=GROUPS)
                keys1 = key1[:].rearrange("p t (g e) -> p (t g) e", g=GROUPS)
                marks, seconds = group_m[:].rearrange("p t g -> p (t g)"), group_n[:].rearrange("p t g -> p (t g)")
                chain.then(v.tensor_reduce, marks, groups, AX.X, ALU.max)
                chain.then(v.tensor_tensor, keys, groups, across(marks, GSIZE), ALU.is_equal)
                chain.then(v.tensor_tensor, keys, keys, along(falling[:, 0:GSIZE], HTILES * GROUPS), ALU.mult)
                chain.then(v.tensor_reduce, seconds, keys, AX.X, ALU.max)
                chain.then(v.tensor_tensor, keys, keys, across(seconds, GSIZE), ALU.is_equal)
                chain.then(v.scalar_tensor_tensor, keys1, keys, LOWEST, groups, ALU.mult, ALU.add)
                chain.then(v.tensor_reduce, seconds, keys1, AX.X, ALU.max)
                chain.then(v.tensor_tensor, group_m[:], group_m[:], group_n[:], ALU.add)
                chain.then(v.tensor_tensor, group_n[:, :, 0], group_m[:, :, 0], group_m[:, :, 1], ALU.is_ge)
                chain.then(v.tensor_scalar, group_n[:, :, 1], group_n[:, :, 0], -1.0, 1.0, ALU.mult, ALU.add)
                chain.then(v.tensor_tensor, groups, groups, across(seconds, GSIZE), ALU.mult)
                top_two(v, chain, first[:], second[:], choice[:], falling[:], row_m[:], (key0[:], key1[:]), HTILES)
                chain.then(v.tensor_tensor, first[:], first[:], second[:], ALU.add)
                chain.then(v.tensor_tensor, score[:], score[:], first[:], ALU.mult)
                chain.then(v.tensor_reduce, row_s[:], score[:], AX.X, ALU.add)
                chain.then(v.tensor_scalar, row_s[:], row_s[:], NORM_EPS, None, ALU.add)
                chain.then(v.reciprocal, row_s[:], row_s[:])
                chain.wait()
                v.tensor_tensor(score_et[:].rearrange("p e t -> p t e"), score[:], across(row_s[:], EXPERTS), ALU.mult).then_inc(score_done, 1)
                assert chain.n == ROUTE_STEPS, chain.n

            def body(b, end):
                turn, s_turn = v_turns(b), s_turns(b)
                hi_n = [b * HI_EACH + HI_BANKS["x2T"]]

                def split_lo(hi, lo, bias=None):
                    bank, n = turn.take()
                    hi_n[0] = hi_n[0] + 1
                    v.wait_ge(hi_done, hi_n[0])
                    if bias is None:
                        v.tensor_tensor(lo, ps[:, bank, :], f32(hi), ALU.subtract).then_inc(v_free, 1)
                    else:
                        v.scalar_tensor_tensor(lo, ps[:, bank, :], bias, f32(hi), ALU.add, ALU.subtract).then_inc(v_free, 1)
                    return n

                for kind, j in order(end):
                    if kind == "q":
                        at = (slice(None), j % CH, bass.ts(j // CH, HALF))
                        split_lo(q_hi[at], q_lo[at], bias_qs[:, j % CH:j % CH + 1])
                    elif kind == "k":
                        at = (slice(None), j % CH, bass.ts(j // CH, HALF))
                        split_lo(k_hi[at], k_lo[at], bias_k[:, j % CH:j % CH + 1])
                    elif kind == "v":
                        split_lo(v_hi[:, 2 * j:2 * j + 2, :].rearrange("p t c -> p (t c)"), v_lo[:, 2 * j:2 * j + 2, :].rearrange("p t c -> p (t c)"))
                    elif kind == "score":
                        bank, n = s_turn.take()
                        s_turn.take()
                        v.wait_ge(s_full, n + 2)
                        v.tensor_reduce(neg_max[:, j:j + 1], ps[:, bank:bank + 2, :].rearrange("p a n -> p (a n)"), AX.X, ALU.max, negate=True).then_inc(max_done, 1)
                    elif kind == "turn":
                        for g in range(2):
                            at = (slice(None), slice(4 * g, 4 * g + 4))
                            split_lo(probT_hi[at].rearrange("p t s -> p (t s)"), probT_lo[at].rearrange("p t s -> p (t s)"))
                    elif kind == "mix":
                        bank, n = turn.take()
                        v.wait_ge(s_free, s_upto(b, ("score", j)))
                        v.reciprocal(row_inv[:, j:j + 1], row_sum[:, j:j + 1]).then_inc(inv_done, 1)
                        v.wait_ge(v_full, n + 1)
                        v.wait_ge(bias_added, b + 1)
                        v.wait_ge(inv_done, TILES * b + j + 1)
                        v.scalar_tensor_tensor(x2[:, j, :], ps[:, bank, 0:C], row_inv[:, j:j + 1], x2[:, j, :], ALU.mult, ALU.add).then_inc(v_free, 1)
                        if (j + 1) % HTILES == 0:
                            h = j // HTILES
                            chain = Chain(v, ln_chain, (4 * b + h) * HALF_LN_STEPS)
                            v.wait_ge(v_free, n + 1)
                            if not (isinstance(b, int) and b == 0):
                                v.wait_ge(out_stored, 32 * b)
                            normed(chain, x3, x2, HTILES * h, HTILES).then_inc(x3_done, 1)
                            assert chain.n == HALF_LN_STEPS, chain.n
                    elif kind == "x3T":
                        for c in range(CH):
                            split_lo(x3T_hi[:, c, :], x3T_lo[:, c, :])
                    elif kind == "gate":
                        bank, n = turn.take()
                        route(b, j, n)
                    elif kind == "scoreT":
                        bank, n = turn.take()
                        v.wait_ge(v_full, n + 1)
                        if not (isinstance(b, int) and b == 0 and j == 0):
                            v.wait_ge(scores_stored, 32 * b + 16 * j)
                        v.tensor_copy(scoreT[:], ps[0:EXPERTS * HTILES, bank, 0:P]).then_inc(v_free, 1)
                    elif kind == "latent":
                        split_lo(lat_hi[:], lat_lo[:])
                    elif kind == "comb":
                        split_lo(comb_hi[:], comb_lo[:])
                        if j == 0 and not end:
                            combine(b + 1)
                    elif kind == "x2T":
                        split_rows(b + 1, hi_n[0], turn)
                        hi_n[0] = hi_n[0] + HI_BANKS["x2T"]
                    elif kind in ("up", "expert"):
                        base = 0 if kind == "up" else EXPERTS
                        u0 = 2 * HIDDEN * b + HIDDEN * j + base
                        for k in range(EXPERTS + 1):
                            if k < EXPERTS:
                                bank, n = s_turn.take()
                                if kind == "up":
                                    v.wait_ge(s_free, n + 1)
                                    wait_past(v, hid_split, u0 + k - RING_H + 1)
                                    v.tensor_tensor(square[:, k % RING_H, :], relu[:, k % RING_R, :], relu[:, k % RING_R, :], ALU.mult).then_inc(squared, 1)
                                else:
                                    v.wait_ge(scaled, 2 * EXPERTS * b + EXPERTS * j + k + 1)
                                    v.tensor_tensor(square[:, k % RING_H, :], square[:, k % RING_H, :], relu[:, k % RING_R, :], ALU.mult).then_inc(squared, 1)
                            if k:
                                g = k - 1
                                v.wait_ge(squared, u0 + g + 1)
                                v.wait_ge(hid_hi_done, u0 + g + 1)
                                v.tensor_tensor(hid_lo[:, base + g, :], square[:, g % RING_H, :], f32(hid_hi[:, base + g, :]), ALU.subtract).then_inc(hid_split, 1)
                    elif kind == "out":
                        for g in range(2):
                            bank, n = turn.take()
                            at = (slice(None), slice(HTILES * j + 2 * g, HTILES * j + 2 * g + 2))
                            v.wait_ge(v_full, n + 1)
                            v.tensor_tensor(x3[at], ps[:, bank, :].rearrange("p (t c) -> p t c", c=C), x3[at], ALU.add).then_inc(v_free, 1)
                        chain = Chain(v, ln_chain, (4 * b + 2 + j) * HALF_LN_STEPS)
                        v.wait_ge(v_free, n + 1)
                        normed(chain, x3, x3, HTILES * j, HTILES).then_inc(out_done, 1)
                        assert chain.n == HALF_LN_STEPS, chain.n

            v.wait_ge(consts, CONSTS)
            split_weights(range(EARLY))
            combine(0)
            split_rows(0, 0, Turns(0, 0, range(4, 8)))
            split_weights(range(EARLY, len(WEIGHTS)))
            v.wait_ge(biases_in, 64)
            v.tensor_scalar(bias_qs[:], bias_q[:], SCALE, None, ALU.mult).then_inc(weight_split, 1)
            v.wait_ge(weight_split, len(WEIGHTS) + 1)
            body(0, False)
            with v.Fori(1, BATCHES - 1) as b:
                body(b, False)
            body(BATCHES - 1, True)

        @block.tensor
        def _(pe):
            def v_opener(turn):
                def open_bank():
                    bank, n = turn.take()
                    wait_past(pe, v_free, n + 1 - 4)
                    return ps[:, bank, :], n
                return open_bank

            def turn_rows(b, open_bank):
                pe.wait_ge(x2_done, b + 1)
                for c in range(CH):
                    for h in range(2):
                        out, n = open_bank()
                        for t in range(HTILES):
                            last = pe.transpose(out[:, bass.ts(t, P)], x2[:, HTILES * h + t, bass.ts(c, P)], ident[:])
                        last.then_inc(v_full, 1)

            def body(b, end):
                open_v, s_turn = v_opener(v_turns(b)), s_turns(b)

                def open_s():
                    bank, n = s_turn.take()
                    wait_past(pe, s_free, n + 1 - 4)
                    return ps[:, bank, :]

                pe.wait_ge(v_free, x2T_upto(b))
                for kind, j in order(end):
                    if kind in ("q", "k"):
                        w_hi, w_lo = (wq_hi, wq_lo) if kind == "q" else (wk_hi, wk_lo)
                        h, p = j // CH, j % CH
                        out, n = open_v()
                        product(pe, out, [(w_hi[:, c, bass.ts(p, P)], w_lo[:, c, bass.ts(p, P)], x2T_hi[:, c, bass.ts(h, HALF)], x2T_lo[:, c, bass.ts(h, HALF)])
                                          for c in range(CH)]).then_inc(v_full, 1)
                    elif kind == "v":
                        out, n = open_v()
                        for t in (2 * j, 2 * j + 1):
                            last = product(pe, out[:, bass.ts(t % 2, C)],
                                           [(x2T_hi[:, c, bass.ts(t, P)], x2T_lo[:, c, bass.ts(t, P)], wv_hi[:, c, :], wv_lo[:, c, :]) for c in range(CH)])
                        last.then_inc(v_full, 1)
                    elif kind == "score":
                        pe.wait_ge(v_free, v_upto(b, ("k", 3)))
                        for h in range(2):
                            out = open_s()
                            product(pe, out, [(q_hi[:, c, bass.ts(j, P)], q_lo[:, c, bass.ts(j, P)], k_hi[:, c, bass.ts(h, HALF)], k_lo[:, c, bass.ts(h, HALF)])
                                              for c in range(CH)]).then_inc(s_full, 1)
                    elif kind == "turn":
                        pe.wait_ge(s_free, s_upto(b, ("score", j)))
                        for g in range(2):
                            out, n = open_v()
                            for t in range(4):
                                last = pe.transpose(out[:, bass.ts(t, P)], prob[:, j % 2, bass.ts(4 * g + t, P)], ident[:])
                            last.then_inc(v_full, 1)
                    elif kind == "mix":
                        pe.wait_ge(v_free, v_upto(b, ("turn", j)))
                        out, n = open_v()
                        product(pe, out[:, 0:C], [(probT_hi[:, t, :], probT_lo[:, t, :], v_hi[:, t, :], v_lo[:, t, :]) for t in range(TILES)]).then_inc(v_full, 1)
                    elif kind == "x3T":
                        pe.wait_ge(x3_done, 2 * b + j + 1)
                        for c in range(CH):
                            out, n = open_v()
                            for t in range(HTILES):
                                last = pe.transpose(out[:, bass.ts(t, P)], x3[:, HTILES * j + t, bass.ts(c, P)], ident[:])
                            last.then_inc(v_full, 1)
                    elif kind == "gate":
                        pe.wait_ge(v_free, v_upto(b, ("x3T", j)))
                        out, n = open_v()
                        for t in range(HTILES):
                            last = product(pe, out[:, bass.ts(t, EXPERTS)],
                                           [(x3T_hi[:, c, bass.ts(t, P)], x3T_lo[:, c, bass.ts(t, P)], gate_hi[:, c, :], gate_lo[:, c, :]) for c in range(CH)])
                        last.then_inc(v_full, 1)
                    elif kind == "scoreT":
                        pe.wait_ge(score_done, 2 * b + j + 1)
                        out, n = open_v()
                        pe.transpose(out[0:EXPERTS * HTILES, 0:P], score_et[:].rearrange("p e t -> p (e t)"), ident[:]).then_inc(v_full, 1)
                    elif kind == "latent":
                        out, n = open_v()
                        product(pe, out, [(fc1_hi[:, c, :], fc1_lo[:, c, :], x3T_hi[:, c, :], x3T_lo[:, c, :]) for c in range(CH)]).then_inc(v_full, 1)
                    elif kind == "up":
                        for k in range(EXPERTS):
                            product(pe, open_s(), [(up_hi[:, c, bass.ts(k, P)], up_lo[:, c, bass.ts(k, P)], x3T_hi[:, c, :], x3T_lo[:, c, :])
                                                   for c in range(CH)]).then_inc(s_full, 1)
                    elif kind == "expert":
                        pe.wait_ge(v_free, v_upto(b, ("latent", j)))
                        for e in range(EXPERTS):
                            product(pe, open_s(), [(w1_hi[:, e, :], w1_lo[:, e, :], lat_hi[:], lat_lo[:])]).then_inc(s_full, 1)
                    elif kind == "x2T":
                        turn_rows(b + 1, open_v)
                    elif kind == "comb":
                        pe.wait_ge(hid_split, 2 * HIDDEN * b + HIDDEN * (j + 1))
                        out, n = open_v()
                        product(pe, out, [(w2_hi[:, e, :], w2_lo[:, e, :], hid_hi[:, EXPERTS + e, :], hid_lo[:, EXPERTS + e, :])
                                          for e in range(EXPERTS)]).then_inc(v_full, 1)
                    elif kind == "out":
                        pe.wait_ge(v_free, v_upto(b, ("comb", j)))
                        for g in range(2):
                            out, n = open_v()
                            for t in (2 * g, 2 * g + 1):
                                last = product(pe, out[:, bass.ts(t % 2, C)],
                                               [(hid_hi[:, k, bass.ts(t, P)], hid_lo[:, k, bass.ts(t, P)], down_hi[:, k, :], down_lo[:, k, :])
                                                for k in range(SHARED // P)]
                                               + [(comb_hi[:, bass.ts(t, P)], comb_lo[:, bass.ts(t, P)], fc2_hi[:, 0, :], fc2_lo[:, 0, :])])
                            last.then_inc(v_full, 1)

            pe.wait_ge(consts, CONSTS)
            turn_rows(0, v_opener(Turns(0, 0, range(4, 8))))
            pe.wait_ge(weight_split, len(WEIGHTS) + 1)
            body(0, False)
            with pe.Fori(1, BATCHES - 1) as b:
                body(b, False)
            body(BATCHES - 1, True)


def program(nc, d):
    d["x1"] = nc.dram_tensor("x1_rows", (TOKENS, C), F32).ap()
    d["xs"] = nc.dram_tensor("expert_rows", (REAL * CAP, C), F32).ap()
    d["ys"] = nc.dram_tensor("expert_results", (REAL * CAP + P, C), F32).ap()
    d["slots"] = nc.dram_tensor("slot_rows", (BATCHES * P, 2 * TILES), U32).ap()
    d["gates"] = nc.dram_tensor("gate_rows", (BATCHES * P, 3 * TILES), F32).ap()
    d["score_rows"] = nc.dram_tensor("score_rows", (2 * BATCHES, EXPERTS * HALF), F32).ap()
    stage_a(nc, d)
    stage_b(nc, d)
    stage_c(nc, d)


def kernel(**inputs):
    import numpy as np
    import concourse.bacc as bacc
    from concourse.bass_utils import run_bass_kernel_spmd

    def rows(name):
        a = np.asarray(inputs[name])
        return a.reshape(-1, a.shape[-1])

    qkv = rows("L0_attn_qkv_weight")
    arrays = {
        "x": rows("L0_attn_x"), "xT": rows("L0_attn_x").T,
        "wqT": qkv[:C].T, "wkvT": qkv[C:].T, "projT": rows("L0_attn_proj_weight").T, "proj_bias": inputs["L0_attn_proj_bias"],
        "routerT": rows("L0_ffn_router_w").T, "router_b": inputs["L0_ffn_router_b"],
        "w_in": rows("L0_ffn_experts_inter"), "w_out": rows("L0_ffn_experts_out"),
        "wq": rows("L1_attn_W_q"), "wk": rows("L1_attn_W_k"), "wv": rows("L1_attn_W_v"),
        "bq": np.asarray(inputs["L1_attn_b_q"]).reshape(CH, P).T, "bk": np.asarray(inputs["L1_attn_b_k"]).reshape(CH, P).T, "bv": inputs["L1_attn_b_v"],
        "gateT": rows("L1_ffn_gate").T, "corr": inputs["L1_ffn_corr_bias"],
        "fc1T": rows("L1_ffn_fc1_w").T, "fc2T": rows("L1_ffn_fc2_w").T,
        "w1T": rows("L1_ffn_w1").T, "w2T": rows("L1_ffn_w2").reshape(EXPERTS, LATENT, -1).transpose(2, 0, 1).reshape(-1, EXPERTS * LATENT),
        "upT": rows("L1_ffn_up_w").T, "downT": rows("L1_ffn_down_w").T,
    }
    arrays = {name: np.ascontiguousarray(a) for name, a in arrays.items()}
    nc = bacc.Bacc("TRN2", target_bir_lowering=False, num_devices=1)
    d = {name: nc.dram_tensor(name, a.shape, mybir.dt.from_np(a.dtype), kind="ExternalInput").ap() for name, a in arrays.items()}
    d["out"] = nc.dram_tensor("out", (TOKENS, C), F32, kind="ExternalOutput").ap()
    program(nc, d)
    got = run_bass_kernel_spmd(nc, [arrays], core_ids=[0])
    return got.results[0]["out"].reshape(BATCHES, SEQ, C)
```

```python
import concourse.bass as bass
from concourse import mybir
from contextlib import ExitStack

F32 = mybir.dt.float32
F32R = mybir.dt.float32r
BF16 = mybir.dt.bfloat16
I32 = mybir.dt.int32
U32 = mybir.dt.uint32
ALU = mybir.AluOpType
ACT = mybir.ActivationFunctionType
AX = mybir.AxisListType

P = 128
BATCHES, SEQ, C = 8, 1024, 256
TOKENS = BATCHES * SEQ
TILES = SEQ // P
CH = C // P
HALF = SEQ // 2
HTILES = HALF // P
HEADS = 32
HEAD = C // HEADS
ATTN_EPS = 1e-15
LN_EPS = 1e-5
EXPERTS = 8
REAL = EXPERTS - 1
INTER = 1024
ICH = INTER // P
CAP = TOKENS // EXPERTS
TRASH = REAL * CAP
LATENT = 128
SHARED = 1024
GROUPS = 2
GSIZE = EXPERTS // GROUPS
NORM_EPS = 1e-20
SCALE = C ** -0.5
LOWEST = -3.0e38
RSQRT_MAGIC = 0x5F3759DF
BANKS = 8


def count(i, first, each):
    if isinstance(i, int):
        return 0 if i == 0 else first + (i - 1) * each
    return i * each + (first - each)


def wait_past(eng, sem, value):
    if not isinstance(value, int) or value > 0:
        eng.wait_ge(sem, value)


class Turns:

    def __init__(self, start, offset, banks):
        self.start, self.offset, self.banks, self.n = start, offset, banks, 0

    def take(self):
        bank = self.banks[(self.offset + self.n) % len(self.banks)]
        self.n += 1
        return bank, self.start + (self.n - 1)


class Chain:

    def __init__(self, eng, sem, start):
        self.eng, self.sem, self.start, self.n = eng, sem, start, 0

    def step(self, instruction):
        self.n += 1
        instruction.then_inc(self.sem, 1)

    def wait(self):
        wait_past(self.eng, self.sem, self.start + self.n)

    def then(self, instruction_of, *args, **kw):
        self.wait()
        self.step(instruction_of(*args, **kw))


def f32(ap):
    return ap.bitcast(F32)


def across(ap, n):
    return ap.unsqueeze(2).to_broadcast([P, ap.shape[1], n])


def along(ap, n):
    return ap.unsqueeze(1).to_broadcast([P, n, ap.shape[1]])


def product(pe, out, terms):
    last = None
    for j, (lh, ll, rh, rl) in enumerate(terms):
        pe.matmul(out, lh, rh, start=(j == 0), stop=False)
        pe.matmul(out, lh, rl, start=False, stop=False)
        last = pe.matmul(out, ll, rh, start=False, stop=(j == len(terms) - 1))
    return last


def accumulate(pe, out, terms, stop=False):
    for j, (lh, ll, rh, rl) in enumerate(terms):
        pe.matmul(out, lh, rh, start=False, stop=False)
        pe.matmul(out, lh, rl, start=False, stop=False)
        last = pe.matmul(out, ll, rh, start=False, stop=(stop and j == len(terms) - 1))
    return last


def reciprocal_root(v, chain, out, x, t):
    chain.then(v.tensor_scalar, t.bitcast(I32), x.bitcast(I32), 1, None, ALU.arith_shift_right)
    chain.then(v.tensor_scalar, out.bitcast(I32), t.bitcast(I32), -1.0, float(RSQRT_MAGIC), ALU.mult, ALU.add)
    for _ in range(3):
        chain.then(v.tensor_tensor, t, out, out, ALU.mult)
        chain.then(v.tensor_tensor, t, t, x, ALU.mult)
        chain.then(v.tensor_scalar, t, t, -0.5, 1.5, ALU.mult, ALU.add)
        chain.then(v.tensor_tensor, out, out, t, ALU.mult)


RR_STEPS = 14
MEAN_STEPS = 7


def layer_norm_stats(v, chain, rows, stats, mean, rstd, tmp, n):
    for t in range(n):
        chain.step(v.bn_stats(stats[:, t, :], rows[:, t, :]))
    even, odd, var, t = stats[:, :, 1], stats[:, :, 4], tmp[:, 0, :], tmp[:, 1, :]
    chain.then(v.tensor_tensor, mean, even, odd, ALU.add)
    chain.then(v.tensor_scalar, mean, mean, 0.5, None, ALU.mult)
    chain.then(v.tensor_tensor, t, even, odd, ALU.subtract)
    chain.then(v.scalar_tensor_tensor, t, t, 0.25, t, ALU.mult, ALU.mult)
    chain.then(v.tensor_tensor, var, stats[:, :, 2], stats[:, :, 5], ALU.add)
    chain.then(v.scalar_tensor_tensor, var, var, 1.0 / C, t, ALU.mult, ALU.add)
    chain.then(v.tensor_scalar, var, var, LN_EPS, None, ALU.add)
    reciprocal_root(v, chain, rstd, var, t)
    chain.wait()


def norm_scale(v, chain, stats, scale, shift, tmp):
    even, odd, var, t = stats[:, :, 1], stats[:, :, 4], tmp[:, 0, :], tmp[:, 1, :]
    chain.then(v.tensor_tensor, shift, even, odd, ALU.add)
    chain.step(v.tensor_tensor(t, even, odd, ALU.subtract))
    chain.step(v.tensor_tensor(var, stats[:, :, 2], stats[:, :, 5], ALU.add))
    chain.then(v.tensor_scalar, var, var, 1.0 / C, LN_EPS, ALU.mult, ALU.add)
    chain.step(v.scalar_tensor_tensor(t, t, 0.25, t, ALU.mult, ALU.mult))
    chain.then(v.tensor_tensor, var, var, t, ALU.add)
    chain.then(v.tensor_scalar, t.bitcast(I32), var.bitcast(I32), 1, None, ALU.arith_shift_right)
    chain.then(v.tensor_scalar, scale.bitcast(I32), t.bitcast(I32), -1.0, float(RSQRT_MAGIC), ALU.mult, ALU.add)
    for _ in range(3):
        chain.then(v.scalar_tensor_tensor, t, scale, -0.5, scale, ALU.mult, ALU.mult)
        chain.then(v.tensor_tensor, t, t, var, ALU.mult)
        chain.then(v.scalar_tensor_tensor, scale, t, 1.5, scale, ALU.add, ALU.mult)
    chain.then(v.scalar_tensor_tensor, shift, shift, -0.5, scale, ALU.mult, ALU.mult)


NORM_STEPS = 18


def top_two(v, chain, first, second, values, falling, m, key, n):
    for out, of in ((first, values), (second, key[1])):
        if out is second:
            chain.then(v.scalar_tensor_tensor, key[1], first, LOWEST, values, ALU.mult, ALU.add)
        chain.then(v.tensor_reduce, m, of, AX.X, ALU.max)
        chain.then(v.tensor_tensor, key[0], of, across(m, EXPERTS), ALU.is_equal)
        chain.then(v.tensor_tensor, key[0], key[0], along(falling, n), ALU.mult)
        chain.then(v.tensor_reduce, m, key[0], AX.X, ALU.max)
        chain.then(v.tensor_tensor, out, key[0], across(m, EXPERTS), ALU.is_equal)


TOP_STEPS = 11


def stage_a(nc, d):
    HEAD_GROUPS = TILES + CH + 2 * CH
    LATE_GROUPS = 2 * CH + 1
    MAIN_GROUPS = 4 * CH + TILES // 2
    FIRST = HEAD_GROUPS + MAIN_GROUPS
    EACH = FIRST + LATE_GROUPS + 1
    CONSTS = 24
    LN_STEPS = TILES + MEAN_STEPS + RR_STEPS
    ROUTE_STEPS = 4 + TOP_STEPS + 10

    with ExitStack() as ctx:
        def sb(name, shape, dt=F32):
            return ctx.enter_context(nc.sbuf_tensor("a_" + name, shape, dt))

        def sem(name):
            return ctx.enter_context(nc.semaphore("a_" + name))

        ps = ctx.enter_context(nc.psum_tensor("a_ps", [P, BANKS, 512], F32))

        wkv_raw, wkv_hi, wkv_lo = sb("wkv_raw", [P, CH, 2 * C]), sb("wkv_hi", [P, CH, 2 * C], F32R), sb("wkv_lo", [P, CH, 2 * C], F32R)
        wq_raw, wq_hi, wq_lo = sb("wq_raw", [P, CH, C]), sb("wq_hi", [P, CH, C], F32R), sb("wq_lo", [P, CH, C], F32R)
        wp_raw, wp_hi, wp_lo = sb("wp_raw", [P, CH, C]), sb("wp_hi", [P, CH, C], F32R), sb("wp_lo", [P, CH, C], F32R)
        wr_raw, wr_hi, wr_lo = sb("wr_raw", [P, CH, EXPERTS]), sb("wr_hi", [P, CH, EXPERTS], F32R), sb("wr_lo", [P, CH, EXPERTS], F32R)
        bias_p, bias_r = sb("bias_p", [P, C]), sb("bias_r", [P, EXPERTS])
        zeros = sb("zeros", [P, 2 * SEQ])
        ident = sb("ident", [P, P])
        same_head = sb("same_head", [P, 2 * P])
        ones_f = sb("ones_f", [P, P])
        before, ones = sb("before", [P, P], BF16), sb("ones", [P, P], BF16)
        falling, real, slot0 = sb("falling", [P, EXPERTS]), sb("real", [P, EXPERTS]), sb("slot0", [P, EXPERTS])
        xT_raw, xT_hi, xT_lo = sb("xT_raw", [P, CH, SEQ]), sb("xT_hi", [P, CH, SEQ], F32R), sb("xT_lo", [P, CH, SEQ], F32R)
        x_rows = sb("x_rows", [P, TILES, C])
        kv_hi, kv_lo = sb("kv_hi", [P, TILES, 5 * P], F32R), sb("kv_lo", [P, TILES, 4 * P], F32R)
        vk_m, vk_hi, vk_lo = sb("vk_m", [P, CH, 2 * P]), sb("vk_hi", [P, CH, 2 * P], F32R), sb("vk_lo", [P, CH, 2 * P], F32R)
        q_hi, q_lo = sb("q_hi", [P, CH, SEQ], F32R), sb("q_lo", [P, CH, SEQ], F32R)
        den, rden, mix = sb("den", [P, HALF]), sb("rden", [P, HALF]), sb("mix", [P, 2, HALF])
        mix_hi, mix_lo = sb("mix_hi", [P, CH, SEQ], F32R), sb("mix_lo", [P, CH, SEQ], F32R)
        rows, x1, x1_copy = sb("rows", [P, TILES, C]), sb("x1", [P, TILES, C]), sb("x1_copy", [P, TILES, C])
        x1T_hi, x1T_lo = sb("x1T_hi", [P, CH, SEQ], F32R), sb("x1T_lo", [P, CH, SEQ], F32R)
        stats, mean = sb("stats", [P, TILES, 6]), sb("mean", [P, TILES])
        rstd, rr_tmp = sb("rstd", [P, TILES]), sb("rr_tmp", [P, 2, TILES])
        logit, expd, weight = (sb(n, [P, TILES, EXPERTS]) for n in ("logit", "expd", "weight"))
        first, second = sb("first", [P, TILES, EXPERTS]), sb("second", [P, TILES, EXPERTS])
        key0, key1 = sb("key0", [P, TILES, EXPERTS]), sb("key1", [P, TILES, EXPERTS])
        row_m, row_s = sb("row_m", [P, TILES]), sb("row_s", [P, TILES])
        mask = sb("mask", [P, TILES, EXPERTS], BF16)
        tile_sum, carry = sb("tile_sum", [P, EXPERTS]), sb("carry", [P, EXPERTS])
        carry_b = sb("carry_b", [P, EXPERTS], BF16)
        slot, room = sb("slot", [P, TILES, EXPERTS]), sb("room", [P, TILES, EXPERTS])
        picked = sb("picked", [P, 2, TILES])
        slots = sb("slots", [P, 2, TILES], U32)
        gates = sb("gates", [P, 3, TILES])

        weights_in, consts = sem("weights_in"), sem("consts")
        xT_in, x_in = sem("xT_in"), sem("x_in")
        zero_filled = sem("zero_filled")
        weights_hi, weights_split = sem("weights_hi"), sem("weights_split")
        xT_hi_done, xT_split = sem("xT_hi_done"), sem("xT_split")
        bank_full, bank_free = sem("bank_full"), sem("bank_free")
        kv_hi_done, q_hi_done, vk_hi_done, vk_split = sem("kv_hi_done"), sem("q_hi_done"), sem("vk_hi_done"), sem("vk_split")
        recip_done, mix_hi_done, mix_split = sem("recip_done"), sem("mix_hi_done"), sem("mix_split")
        x_biased, x1_done, x1_stored, x1_copied = sem("x_biased"), sem("x1_done"), sem("x1_stored"), sem("x1_copied")
        x1T_hi_done, logit_done, exp_done = sem("x1T_hi_done"), sem("logit_done"), sem("exp_done")
        ln_chain, route_chain, slot_chain = sem("ln_chain"), sem("route_chain"), sem("slot_chain")
        mask_done, slots_done, slots_stored, scattered = sem("mask_done"), sem("slots_done"), sem("slots_stored"), sem("scattered")
        SLOT_STEPS = 9

        def turns(i):
            return Turns(count(i, FIRST, EACH), 0 if isinstance(i, int) and i == 0 else FIRST, range(BANKS))

        block = ctx.enter_context(nc.Block())

        @block.sync
        def _(sp):
            for raw, w in ((wkv_raw, "wkvT"), (wq_raw, "wqT"), (wp_raw, "projT"), (wr_raw, "routerT")):
                sp.dma_start(raw[:], d[w].rearrange("(a p) n -> p a n", p=P)).then_inc(weights_in, 16)
            sp.dma_start(bias_p[:], d["proj_bias"].partition_broadcast(P)).then_inc(weights_in, 16)
            sp.dma_start(bias_r[:], d["router_b"].partition_broadcast(P)).then_inc(weights_in, 16)

            def load(i):
                if not (isinstance(i, int) and i == 0):
                    sp.wait_ge(xT_split, i)
                sp.dma_start(xT_raw[:], d["xT"][:, bass.ds(i * SEQ, SEQ)].rearrange("(a p) n -> p a n", p=P)).then_inc(xT_in, 16)
                if not (isinstance(i, int) and i == 0):
                    sp.wait_ge(bank_free, count(i - 1, FIRST, EACH) + (FIRST if isinstance(i, int) and i == 1 else EACH - 1))
                sp.dma_start(x_rows[:], d["x"][bass.ds(i * SEQ, SEQ), :].rearrange("(t p) c -> p t c", p=P)).then_inc(x_in, 16)

            def store(i):
                sp.wait_ge(x1_done, i + 1)
                sp.dma_start(d["x1"][bass.ds(i * SEQ, SEQ), :].rearrange("(t p) c -> p t c", p=P), x1[:]).then_inc(x1_stored, 16)

            def store_slots(i):
                sp.wait_ge(slots_done, i + 1)
                sp.dma_start(d["slots"][bass.ds(i * P, P), :], slots[:].rearrange("p a t -> p (a t)")).then_inc(slots_stored, 16)
                sp.dma_start(d["gates"][bass.ds(i * P, P), :], gates[:].rearrange("p a t -> p (a t)")).then_inc(slots_stored, 16)

            load(0)
            load(1)
            store(0)
            with sp.Fori(1, BATCHES - 1) as i:
                load(i + 1)
                store_slots(i - 1)
                store(i)
            store_slots(BATCHES - 2)
            store(BATCHES - 1)
            store_slots(BATCHES - 1)
            sp.wait_ge(x1_stored, 16 * BATCHES)
            sp.wait_ge(slots_stored, 32 * BATCHES)

        @block.gpsimd
        def _(pool):
            def const(instruction):
                instruction.then_inc(consts, 1)

            const(pool.memset(zeros[:], 0.0))
            const(pool.memset(ident[:], 0.0))
            const(pool.memset(ones_f[:], 1.0))
            const(pool.memset(same_head[:], 1.0))
            const(pool.memset(before[:], 1.0))
            const(pool.memset(ones[:], 1.0))
            const(pool.memset(real[:], 1.0))
            const(pool.memset(carry[:], 0.0))
            const(pool.memset(carry_b[:], 0.0))
            for e in range(EXPERTS):
                const(pool.memset(falling[:, e:e + 1], float(EXPERTS - e)))
            pool.wait_ge(consts, 9 + EXPERTS)
            for part in range(REAL * CAP * C // (P * 2 * SEQ)):
                pool.dma_start(d["xs"].rearrange("(a p r) c -> a p (r c)", p=P, r=2 * SEQ // C)[part, :, :], zeros[:]).then_inc(zero_filled, 16)
            pool.dma_start(d["ys"][TRASH:TRASH + P, :], zeros[:, 0:C]).then_inc(zero_filled, 16)
            ZERO_FILLS = REAL * CAP * C // (P * 2 * SEQ) + 1
            const(pool.affine_select(out=ident[:], in_=ident[:], compare_op=ALU.not_equal, fill=1.0,
                                     base=0, pattern=[[-1, P]], channel_multiplier=1))
            const(pool.affine_select(out=before[:], in_=before[:], compare_op=ALU.is_ge, fill=0.0,
                                     base=-1, pattern=[[1, P]], channel_multiplier=-1))
            heads = same_head[:].rearrange("p (a h e) -> p a h e", a=2, e=HEAD)
            const(pool.affine_select(out=heads, in_=heads, compare_op=ALU.is_ge, fill=0.0, base=0,
                                     pattern=[[0, 2], [-HEAD, P // HEAD], [0, HEAD]], channel_multiplier=1))
            pool.wait_ge(consts, 9 + EXPERTS + 3)
            const(pool.affine_select(out=heads, in_=heads, compare_op=ALU.is_ge, fill=0.0, base=HEAD - 1,
                                     pattern=[[0, 2], [HEAD, P // HEAD], [0, HEAD]], channel_multiplier=-1))
            const(pool.memset(real[:, REAL:EXPERTS], 0.0))
            const(pool.iota(slots[:].rearrange("p a t -> p (a t)").bitcast(I32)[:, 0:EXPERTS], pattern=[[CAP, EXPERTS]], base=-TRASH, channel_multiplier=0))
            pool.wait_ge(consts, 9 + EXPERTS + 6)
            const(pool.tensor_copy(slot0[:], slots[:].rearrange("p a t -> p (a t)").bitcast(I32)[:, 0:EXPERTS]))

            def bias(i):
                pool.wait_ge(x_in, 16 * i + 16)
                if isinstance(i, int) and i == 0:
                    pool.wait_ge(weights_in, 16 * 6)
                pool.tensor_tensor(x_rows[:], x_rows[:], bias_p[:].unsqueeze(1).to_broadcast([P, TILES, C]), ALU.add).then_inc(x_biased, 1)

            def late(i):
                pool.wait_ge(zero_filled, 16 * ZERO_FILLS)
                pool.wait_ge(x1_copied, i + 1)
                pool.wait_ge(slots_done, i + 1)
                for t in range(TILES):
                    for a in range(2):
                        pool.indirect_dma_start(d["xs"], bass.IndirectOffsetOnAxis(ap=slots[:, a, t:t + 1], axis=0),
                                                x1_copy[:, t, :], None, bounds_check=TRASH - 1, oob_is_err=False).then_inc(scattered, 16)

            bias(0)
            bias(1)
            late(0)
            with pool.Fori(2, BATCHES) as i:
                bias(i)
                late(i - 1)
            late(BATCHES - 1)
            pool.wait_ge(scattered, 32 * TILES * BATCHES)

        @block.scalar
        def _(act):
            act.wait_ge(weights_in, 16 * 6)
            for hi, raw in ((wkv_hi, wkv_raw), (wq_hi, wq_raw), (wp_hi, wp_raw), (wr_hi, wr_raw)):
                act.activation(hi[:], raw[:], ACT.Copy).then_inc(weights_hi, 1)
            act.wait_ge(consts, CONSTS)
            act.activation(kv_hi[:, :, 4 * P:], ones_f[:].unsqueeze(1).to_broadcast([P, TILES, P]), ACT.Copy).then_inc(weights_hi, 1)

            def split_xT(i):
                act.wait_ge(xT_in, 16 * i + 16)
                act.activation(xT_hi[:], xT_raw[:], ACT.Copy).then_inc(xT_hi_done, 1)

            def late(i, turn):
                for c in range(CH):
                    for h in range(2):
                        bank, n = turn.take()
                        act.wait_ge(bank_full, n + 1)
                        act.activation(x1T_hi[:, c, bass.ts(h, HALF)], ps[:, bank, :], ACT.Copy).then_inc(x1T_hi_done, 1)
                turn.take()
                act.wait_ge(logit_done, i + 1)
                act.activation(expd[:], logit[:], ACT.Exp).then_inc(exp_done, 1)
                if not (isinstance(i, int) and i == 0):
                    act.wait_ge(scattered, 32 * TILES * i)
                act.activation(x1_copy[:], x1[:], ACT.Copy).then_inc(x1_copied, 1)

            def body(i, start, end):
                turn = turns(i)
                for t in range(TILES):
                    bank, n = turn.take()
                    act.wait_ge(bank_full, n + 1)
                    act.activation(kv_hi[:, t, 0:4 * P], ps[:, bank, :], ACT.Relu).then_inc(kv_hi_done, 1)
                for p in range(CH):
                    bank, n = turn.take()
                    act.wait_ge(bank_free, n + 1)
                    act.activation(vk_hi[:, p, :], vk_m[:, p, :], ACT.Copy).then_inc(vk_hi_done, 1)
                for h in range(2):
                    for p in range(CH):
                        bank, n = turn.take()
                        act.wait_ge(bank_full, n + 1)
                        act.activation(q_hi[:, p, bass.ts(h, HALF)], ps[:, bank, :], ACT.Relu).then_inc(q_hi_done, 1)
                if not end:
                    split_xT(i + 1)
                if not start:
                    late(i - 1, turn)
                for h in range(2):
                    for p in range(CH):
                        turn.take()
                        bank, n = turn.take()
                        act.wait_ge(bank_free, n + 1)
                        act.activation(mix_hi[:, p, bass.ts(h, HALF)], mix[:, p, :], ACT.Copy).then_inc(mix_hi_done, 1)

            split_xT(0)
            body(0, True, False)
            with act.Fori(1, BATCHES - 1) as i:
                body(i, False, False)
            body(BATCHES - 1, False, True)
            late(BATCHES - 1, turns(BATCHES))

        @block.vector
        def _(v):
            for j, (lo, raw, hi) in enumerate(((wkv_lo, wkv_raw, wkv_hi), (wq_lo, wq_raw, wq_hi), (wp_lo, wp_raw, wp_hi), (wr_lo, wr_raw, wr_hi))):
                v.wait_ge(weights_hi, j + 1)
                v.tensor_tensor(lo[:], raw[:], f32(hi[:]), ALU.subtract).then_inc(weights_split, 1)
            v.wait_ge(consts, CONSTS)

            def split_xT(i):
                v.wait_ge(xT_hi_done, i + 1)
                v.tensor_tensor(xT_lo[:], xT_raw[:], f32(xT_hi[:]), ALU.subtract).then_inc(xT_split, 1)

            def late(i, turn):
                for c in range(CH):
                    for h in range(2):
                        bank, n = turn.take()
                        v.wait_ge(x1T_hi_done, 4 * i + 2 * c + h + 1)
                        v.tensor_tensor(x1T_lo[:, c, bass.ts(h, HALF)], ps[:, bank, :], f32(x1T_hi[:, c, bass.ts(h, HALF)]), ALU.subtract).then_inc(bank_free, 1)
                bank, n = turn.take()
                v.wait_ge(bank_full, n + 1)
                v.tensor_tensor(logit[:], ps[:, bank, 0:TILES * EXPERTS].rearrange("p (t e) -> p t e", e=EXPERTS), along(bias_r[:], TILES), ALU.add).then_inc(bank_free, 1)
                chain = Chain(v, route_chain, i * ROUTE_STEPS)
                v.wait_ge(bank_free, n + 1)
                chain.step(v.tensor_reduce(row_m[:], logit[:], AX.X, ALU.max))
                chain.wait()
                v.tensor_tensor(logit[:], logit[:], across(row_m[:], EXPERTS), ALU.subtract).then_inc(logit_done, 1)
                v.wait_ge(exp_done, i + 1)
                chain.step(v.tensor_reduce(row_s[:], expd[:], AX.X, ALU.add))
                chain.then(v.reciprocal, row_s[:], row_s[:])
                chain.then(v.tensor_tensor, weight[:], expd[:], across(row_s[:], EXPERTS), ALU.mult)
                top_two(v, chain, first[:], second[:], weight[:], falling[:], row_m[:], (key0[:], key1[:]), TILES)
                chain.then(v.tensor_scalar, key0[:], weight[:], 0.0, None, ALU.is_gt)
                chain.then(v.tensor_tensor, second[:], second[:], key0[:], ALU.mult)
                chain.then(v.tensor_tensor, first[:], first[:], key0[:], ALU.mult)
                chain.then(v.tensor_tensor, key1[:], first[:], second[:], ALU.add)
                if not (isinstance(i, int) and i == 0):
                    v.wait_ge(slots_stored, 32 * i)
                chain.then(v.tensor_tensor, key0[:], first[:], weight[:], ALU.mult)
                chain.then(v.tensor_reduce, gates[:, 0, :], key0[:], AX.X, ALU.add)
                chain.then(v.tensor_tensor, key0[:], second[:], weight[:], ALU.mult)
                chain.then(v.tensor_reduce, gates[:, 1, :], key0[:], AX.X, ALU.add)
                chain.then(v.tensor_tensor, gates[:, 2, :], key1[:, :, REAL], weight[:, :, REAL], ALU.mult)
                chain.then(v.tensor_copy, slot[:], key1[:])
                assert chain.n == ROUTE_STEPS, chain.n
                v.tensor_copy(mask[:], key1[:]).then_inc(mask_done, 1)

            def late_slots(i, turn):
                bank, n = turn.take()
                chain = Chain(v, slot_chain, i * SLOT_STEPS)
                v.wait_ge(bank_full, n + 1)
                if not (isinstance(i, int) and i == 0):
                    v.wait_ge(scattered, 32 * TILES * i)
                position = ps[:, bank, 0:TILES * EXPERTS].rearrange("p (t e) -> p t e", e=EXPERTS)
                chain.step(v.scalar_tensor_tensor(room[:], position, float(CAP), along(real[:], TILES), ALU.is_lt, ALU.mult))
                v.tensor_tensor(slot[:], position, along(slot0[:], TILES), ALU.add).then_inc(bank_free, 1)
                v.wait_ge(bank_free, n + 1)
                chain.then(v.tensor_tensor, slot[:], slot[:], room[:], ALU.mult)
                for a, chosen in ((0, first), (1, second)):
                    chain.then(v.tensor_tensor, room[:], slot[:], chosen[:], ALU.mult)
                    chain.then(v.tensor_reduce, picked[:, a, :], room[:], AX.X, ALU.add)
                chain.then(v.tensor_reduce, tile_sum[:], mask[:].rearrange("p t e -> p e t"), AX.X, ALU.add)
                chain.then(v.tensor_tensor, carry[:], carry[:], tile_sum[:], ALU.add)
                chain.then(v.tensor_copy, carry_b[:], carry[:])
                assert chain.n == SLOT_STEPS, chain.n
                chain.wait()
                v.tensor_scalar(slots[:], picked[:], float(TRASH), None, ALU.add).then_inc(slots_done, 1)

            def body(i, start, end):
                turn = turns(i)
                for t in range(TILES):
                    bank, n = turn.take()
                    v.wait_ge(kv_hi_done, TILES * i + t + 1)
                    v.scalar_tensor_tensor(kv_lo[:, t, :], ps[:, bank, :], 0.0, f32(kv_hi[:, t, 0:4 * P]), ALU.max, ALU.subtract).then_inc(bank_free, 1)
                for p in range(CH):
                    bank, n = turn.take()
                    v.wait_ge(bank_full, n + 1)
                    v.tensor_tensor(vk_m[:, p, :], ps[:, bank, 0:2 * P], same_head[:], ALU.mult).then_inc(bank_free, 1)
                for h in range(2):
                    for p in range(CH):
                        bank, n = turn.take()
                        v.wait_ge(q_hi_done, 2 * CH * i + CH * h + p + 1)
                        v.scalar_tensor_tensor(q_lo[:, p, bass.ts(h, HALF)], ps[:, bank, :], 0.0, f32(q_hi[:, p, bass.ts(h, HALF)]), ALU.max, ALU.subtract).then_inc(bank_free, 1)
                for p in range(CH):
                    v.wait_ge(vk_hi_done, CH * i + p + 1)
                    v.tensor_tensor(vk_lo[:, p, :], vk_m[:, p, :], f32(vk_hi[:, p, :]), ALU.subtract).then_inc(vk_split, 1)
                if not end:
                    split_xT(i + 1)
                if not start:
                    late(i - 1, turn)

                def split_mix(j):
                    h, p = j // CH, j % CH
                    v.wait_ge(mix_hi_done, 2 * CH * i + j + 1)
                    v.tensor_tensor(mix_lo[:, p, bass.ts(h, HALF)], mix[:, p, :], f32(mix_hi[:, p, bass.ts(h, HALF)]), ALU.subtract).then_inc(mix_split, 1)

                for j in range(2 * CH):
                    bank, n = turn.take()
                    v.wait_ge(bank_full, n + 1)
                    v.tensor_scalar(den[:], ps[:, bank, :], ATTN_EPS, None, ALU.add).then_inc(bank_free, 1)
                    v.wait_ge(bank_free, n + 1)
                    v.reciprocal(rden[:], den[:]).then_inc(recip_done, 1)
                    bank, n = turn.take()
                    v.wait_ge(bank_full, n + 1)
                    v.wait_ge(recip_done, 2 * CH * i + j + 1)
                    v.tensor_tensor(mix[:, j % CH, :], ps[:, bank, :], rden[:], ALU.mult).then_inc(bank_free, 1)
                    if j:
                        split_mix(j - 1)
                split_mix(2 * CH - 1)
                v.wait_ge(x_biased, i + 1)
                for j in range(TILES // 2):
                    bank, n = turn.take()
                    v.wait_ge(bank_full, n + 1)
                    v.tensor_tensor(rows[:, 2 * j:2 * j + 2, :], ps[:, bank, :].rearrange("p (t c) -> p t c", c=C), x_rows[:, 2 * j:2 * j + 2, :], ALU.add).then_inc(bank_free, 1)
                chain = Chain(v, ln_chain, i * LN_STEPS)
                v.wait_ge(bank_free, n + 1)
                layer_norm_stats(v, chain, rows[:], stats[:], mean[:], rstd[:], rr_tmp[:], TILES)
                assert chain.n == LN_STEPS, chain.n
                if not start:
                    v.wait_ge(x1_copied, i)
                    v.wait_ge(x1_stored, 16 * i)
                for t in range(TILES):
                    norm = v.tensor_scalar(x1[:, t, :], rows[:, t, :], mean[:, t:t + 1], rstd[:, t:t + 1], ALU.subtract, ALU.mult)
                norm.then_inc(x1_done, 1)
                if not start:
                    late_slots(i - 1, turn)

            split_xT(0)
            body(0, True, False)
            with v.Fori(1, BATCHES - 1) as i:
                body(i, False, False)
            body(BATCHES - 1, False, True)
            turn = turns(BATCHES)
            late(BATCHES - 1, turn)
            late_slots(BATCHES - 1, turn)

        @block.tensor
        def _(pe):
            def late(i, open_bank):
                pe.wait_ge(x1_done, i + 1)
                for c in range(CH):
                    for h in range(2):
                        out, n = open_bank()
                        for t in range(HTILES):
                            last = pe.transpose(out[:, bass.ts(t, P)], x1[:, HTILES * h + t, bass.ts(c, P)], ident[:])
                        last.then_inc(bank_full, 1)
                pe.wait_ge(bank_free, n + 1)
                out, n = open_bank()
                for t in range(TILES):
                    last = product(pe, out[:, bass.ts(t, EXPERTS)],
                                   [(x1T_hi[:, c, bass.ts(t, P)], x1T_lo[:, c, bass.ts(t, P)], wr_hi[:, c, :], wr_lo[:, c, :]) for c in range(CH)])
                last.then_inc(bank_full, 1)

            def late_slots(i, open_bank):
                out, n = open_bank()
                out = out[:, 0:TILES * EXPERTS].rearrange("p (t e) -> p t e", e=EXPERTS)
                pe.wait_ge(mask_done, i + 1)
                pe.matmul(out, before[:], mask[:], start=True, stop=False)
                for t in range(TILES - 1):
                    rest = TILES - 1 - t
                    pe.matmul(out[:, t + 1:, :], ones[:], along(mask[:, t, :], rest), start=False, stop=False)
                if not (isinstance(i, int) and i == 0):
                    pe.wait_ge(slots_done, i)
                pe.matmul(out, ones[:], along(carry_b[:], TILES), start=False, stop=True).then_inc(bank_full, 1)

            def body(i, start, end):
                turn = turns(i)

                def open_bank():
                    bank, n = turn.take()
                    wait_past(pe, bank_free, n + 1 - BANKS)
                    return ps[:, bank, :], n

                pe.wait_ge(xT_split, i + 1)
                for t in range(TILES):
                    out, n = open_bank()
                    product(pe, out, [(xT_hi[:, c, bass.ts(t, P)], xT_lo[:, c, bass.ts(t, P)], wkv_hi[:, c, :], wkv_lo[:, c, :])
                                      for c in range(CH)]).then_inc(bank_full, 1)
                pe.wait_ge(bank_free, n + 1)
                blocks = kv_hi[:].rearrange("p t (b n) -> p t b n", n=P)
                for p in range(CH):
                    out, n = open_bank()
                    for t in range(TILES):
                        v_ones = blocks[:, t, 2 + p::2 - p, :]
                        pe.matmul(out[:, 0:2 * P], kv_hi[:, t, bass.ts(p, P)], v_ones, start=(t == 0), stop=False)
                        pe.matmul(out[:, 0:P], kv_hi[:, t, bass.ts(p, P)], kv_lo[:, t, bass.ts(2 + p, P)], start=False, stop=False)
                        last = pe.matmul(out[:, 0:2 * P], kv_lo[:, t, bass.ts(p, P)], v_ones, start=False, stop=(t == TILES - 1))
                    last.then_inc(bank_full, 1)
                for h in range(2):
                    for p in range(CH):
                        out, q_n = open_bank()
                        product(pe, out, [(wq_hi[:, c, bass.ts(p, P)], wq_lo[:, c, bass.ts(p, P)], xT_hi[:, c, bass.ts(h, HALF)], xT_lo[:, c, bass.ts(h, HALF)])
                                          for c in range(CH)]).then_inc(bank_full, 1)
                if not start:
                    late(i - 1, open_bank)
                pe.wait_ge(bank_free, q_n + 1)
                pe.wait_ge(vk_split, CH * i + CH)
                for h in range(2):
                    for p in range(CH):
                        for part in (1, 0):
                            out, n = open_bank()
                            product(pe, out, [(vk_hi[:, p, bass.ts(part, P)], vk_lo[:, p, bass.ts(part, P)],
                                               q_hi[:, p, bass.ts(h, HALF)], q_lo[:, p, bass.ts(h, HALF)])]).then_inc(bank_full, 1)
                for j in range(TILES // 2):
                    if j % HTILES // 2 == 0 or j == HTILES // 2:
                        pe.wait_ge(mix_split, 2 * CH * i + CH * (1 + j // (HTILES // 2)))
                    out, n = open_bank()
                    for t in (2 * j, 2 * j + 1):
                        last = product(pe, out[:, bass.ts(t % 2, C)],
                                       [(mix_hi[:, p, bass.ts(t, P)], mix_lo[:, p, bass.ts(t, P)], wp_hi[:, p, :], wp_lo[:, p, :]) for p in range(CH)])
                    last.then_inc(bank_full, 1)
                if not start:
                    late_slots(i - 1, open_bank)

            pe.wait_ge(weights_split, 4)
            pe.wait_ge(weights_hi, 5)
            pe.wait_ge(consts, CONSTS)
            body(0, True, False)
            with pe.Fori(1, BATCHES - 1) as i:
                body(i, False, False)
            body(BATCHES - 1, False, True)
            turn = turns(BATCHES)

            def open_bank():
                bank, n = turn.take()
                pe.wait_ge(bank_free, n + 1 - BANKS)
                return ps[:, bank, :], n

            late(BATCHES - 1, open_bank)
            late_slots(BATCHES - 1, open_bank)


def stage_b(nc, d):
    EACH = 2 * ICH + HTILES // 2 + 2 * CH + HTILES // 2
    PROLOGUE = 2 * CH
    with ExitStack() as ctx:
        def sb(name, shape, dt=F32):
            return ctx.enter_context(nc.sbuf_tensor("b_" + name, shape, dt))

        def sem(name):
            return ctx.enter_context(nc.semaphore("b_" + name))

        ps = ctx.enter_context(nc.psum_tensor("b_ps", [P, BANKS, 512], F32))
        ident = sb("ident", [P, P])
        xs = sb("xs", [P, TILES, C])
        xsT_hi, xsT_lo = sb("xsT_hi", [P, CH, CAP], F32R), sb("xsT_lo", [P, CH, CAP], F32R)
        win_raw, win_hi, win_lo = sb("win_raw", [P, CH, INTER]), sb("win_hi", [P, CH, INTER], F32R), sb("win_lo", [P, CH, INTER], F32R)
        wout_raw, wout_hi, wout_lo = sb("wout_raw", [P, ICH, C]), sb("wout_hi", [P, ICH, C], F32R), sb("wout_lo", [P, ICH, C], F32R)
        hT_hi, hT_lo = sb("hT_hi", [P, 2, ICH, HALF], F32R), sb("hT_lo", [P, 2, ICH, HALF], F32R)
        results = sb("results", [P, TILES, C])

        ident_done, xs_in, win_in, wout_in = sem("ident_done"), sem("xs_in"), sem("win_in"), sem("wout_in")
        win_hi_done, win_split = sem("win_hi_done"), sem("win_split")
        wout_hi_done, wout_split = sem("wout_hi_done"), sem("wout_split")
        bank_full, bank_free = sem("bank_full"), sem("bank_free")
        xsT_hi_done, hT_hi_done, results_stored = sem("xsT_hi_done"), sem("hT_hi_done"), sem("results_stored")

        def group(i, n):
            return PROLOGUE + i * EACH + n

        def turns(i):
            return Turns(group(i, 0), PROLOGUE, range(BANKS))

        OUT_A, ROWS, OUT_B = 2 * ICH, 2 * ICH + HTILES // 2, 2 * ICH + HTILES // 2 + 2 * CH
        block = ctx.enter_context(nc.Block())

        @block.sync
        def _(sp):
            def load_rows(e):
                sp.dma_start(xs[:], d["xs"][bass.ds(e * CAP, CAP), :].rearrange("(t p) c -> p t c", p=P)).then_inc(xs_in, 16)

            def load_in(e):
                sp.dma_start(win_raw[:], d["w_in"][bass.ds(e * C, C), :].rearrange("(a p) n -> p a n", p=P)).then_inc(win_in, 16)

            def load_out(e):
                sp.dma_start(wout_raw[:], d["w_out"][bass.ds(e * INTER, INTER), :].rearrange("(a p) n -> p a n", p=P)).then_inc(wout_in, 16)

            def body(e, end):
                if not end:
                    sp.wait_ge(bank_full, PROLOGUE if isinstance(e, int) and e == 0 else group(e - 1, OUT_B))
                    load_rows(e + 1)
                    sp.wait_ge(win_split, e + 1)
                    load_in(e + 1)
                    sp.wait_ge(wout_split, e + 1)
                    load_out(e + 1)
                for h, at in ((0, ROWS), (1, EACH)):
                    sp.wait_ge(bank_free, group(e, at) if h == 0 or not end else group(e, EACH - 2 * CH))
                    sp.dma_start(d["ys"][bass.ds(e * CAP + h * HALF, HALF), :].rearrange("(t p) c -> p t c", p=P),
                                 results[:, bass.ts(h, HTILES), :]).then_inc(results_stored, 16)

            load_rows(0)
            load_in(0)
            load_out(0)
            body(0, False)
            with sp.Fori(1, REAL - 1) as e:
                body(e, False)
            body(REAL - 1, True)
            sp.wait_ge(results_stored, 32 * REAL)

        @block.gpsimd
        def _(pool):
            pool.memset(ident[:], 0.0).then_inc(ident_done, 1)
            pool.wait_ge(ident_done, 1)
            pool.affine_select(out=ident[:], in_=ident[:], compare_op=ALU.not_equal, fill=1.0,
                               base=0, pattern=[[-1, P]], channel_multiplier=1).then_inc(ident_done, 1)

        @block.scalar
        def _(act):
            def split_in(e):
                act.wait_ge(win_in, 16 * e + 16)
                act.activation(win_hi[:], win_raw[:], ACT.Copy).then_inc(win_hi_done, 1)

            def split_out(e):
                act.wait_ge(wout_in, 16 * e + 16)
                act.activation(wout_hi[:], wout_raw[:], ACT.Copy).then_inc(wout_hi_done, 1)

            def split_rows(turn):
                for c in range(CH):
                    for h in range(2):
                        bank, n = turn.take()
                        act.wait_ge(bank_full, n + 1)
                        act.activation(xsT_hi[:, c, bass.ts(h, HALF)], ps[:, bank, :], ACT.Copy).then_inc(xsT_hi_done, 1)

            def body(e, end):
                turn = turns(e)
                if not (isinstance(e, int) and e == 0):
                    act.wait_ge(bank_full, group(e - 1, EACH))
                split_out(e)
                for h in range(2):
                    for k in range(ICH):
                        bank, n = turn.take()
                        act.wait_ge(bank_full, n + 1)
                        act.activation(hT_hi[:, h, k, :], ps[:, bank, :], ACT.Relu).then_inc(hT_hi_done, 1)
                if not end:
                    split_in(e + 1)
                    for _ in range(HTILES // 2):
                        turn.take()
                    split_rows(turn)

            split_in(0)
            split_rows(Turns(0, 0, range(BANKS)))
            body(0, False)
            with act.Fori(1, REAL - 1) as e:
                body(e, False)
            body(REAL - 1, True)

        @block.vector
        def _(v):
            def split_in(e):
                v.wait_ge(win_hi_done, e + 1)
                v.tensor_tensor(win_lo[:], win_raw[:], f32(win_hi[:]), ALU.subtract).then_inc(win_split, 1)

            def split_out(e):
                v.wait_ge(wout_hi_done, e + 1)
                v.tensor_tensor(wout_lo[:], wout_raw[:], f32(wout_hi[:]), ALU.subtract).then_inc(wout_split, 1)

            def split_rows(e, turn):
                for c in range(CH):
                    for h in range(2):
                        bank, n = turn.take()
                        v.wait_ge(xsT_hi_done, 2 * CH * e + 2 * c + h + 1)
                        v.tensor_tensor(xsT_lo[:, c, bass.ts(h, HALF)], ps[:, bank, :], f32(xsT_hi[:, c, bass.ts(h, HALF)]), ALU.subtract).then_inc(bank_free, 1)

            def store_pairs(e, h, turn):
                if not (isinstance(e, int) and e == 0):
                    v.wait_ge(results_stored, 32 * e)
                for j in range(HTILES // 2):
                    bank, n = turn.take()
                    v.wait_ge(bank_full, n + 1)
                    t = HTILES * h + 2 * j
                    v.tensor_copy(results[:, t:t + 2, :], ps[:, bank, :].rearrange("p (t c) -> p t c", c=C)).then_inc(bank_free, 1)

            def body(e, end):
                turn = turns(e)
                split_out(e)
                for h in range(2):
                    for k in range(ICH):
                        bank, n = turn.take()
                        v.wait_ge(hT_hi_done, 2 * ICH * e + ICH * h + k + 1)
                        v.scalar_tensor_tensor(hT_lo[:, h, k, :], ps[:, bank, :], 0.0, f32(hT_hi[:, h, k, :]), ALU.max, ALU.subtract).then_inc(bank_free, 1)
                if not end:
                    split_in(e + 1)
                store_pairs(e, 0, turn)
                if not end:
                    split_rows(e + 1, turn)
                store_pairs(e, 1, turn)

            split_in(0)
            split_rows(0, Turns(0, 0, range(BANKS)))
            body(0, False)
            with v.Fori(1, REAL - 1) as e:
                body(e, False)
            body(REAL - 1, True)

        @block.tensor
        def _(pe):
            def opener(turn):
                def open_bank():
                    bank, n = turn.take()
                    wait_past(pe, bank_free, n + 1 - BANKS)
                    return ps[:, bank, :], n
                return open_bank

            def turn_rows(e, open_bank):
                pe.wait_ge(xs_in, 16 * e + 16)
                for c in range(CH):
                    for h in range(2):
                        out, n = open_bank()
                        for t in range(HTILES):
                            last = pe.transpose(out[:, bass.ts(t, P)], xs[:, HTILES * h + t, bass.ts(c, P)], ident[:])
                        last.then_inc(bank_full, 1)

            def hidden(e, h, open_bank):
                for k in range(ICH):
                    out, n = open_bank()
                    product(pe, out, [(win_hi[:, c, bass.ts(k, P)], win_lo[:, c, bass.ts(k, P)],
                                       xsT_hi[:, c, bass.ts(h, HALF)], xsT_lo[:, c, bass.ts(h, HALF)]) for c in range(CH)]).then_inc(bank_full, 1)
                return n

            def result(h, open_bank):
                for j in range(HTILES // 2):
                    out, n = open_bank()
                    for t in (2 * j, 2 * j + 1):
                        last = product(pe, out[:, bass.ts(t % 2, C)],
                                       [(hT_hi[:, h, k, bass.ts(t, P)], hT_lo[:, h, k, bass.ts(t, P)], wout_hi[:, k, :], wout_lo[:, k, :])
                                        for k in range(ICH)])
                    last.then_inc(bank_full, 1)

            def body(e, end):
                open_bank = opener(turns(e))
                pe.wait_ge(win_split, e + 1)
                pe.wait_ge(bank_free, PROLOGUE if isinstance(e, int) and e == 0 else group(e - 1, OUT_B))
                last_a = hidden(e, 0, open_bank)
                last_b = hidden(e, 1, open_bank)
                pe.wait_ge(wout_split, e + 1)
                pe.wait_ge(bank_free, last_a + 1)
                result(0, open_bank)
                if not end:
                    turn_rows(e + 1, open_bank)
                pe.wait_ge(bank_free, last_b + 1)
                result(1, open_bank)

            pe.wait_ge(ident_done, 2)
            turn_rows(0, opener(Turns(0, 0, range(BANKS))))
            body(0, False)
            with pe.Fori(1, REAL - 1) as e:
                body(e, False)
            body(REAL - 1, True)


def stage_c(nc, d):
    HALVES = 2
    PARTS = 2
    CHUNKS = EXPERTS // PARTS
    ORDER = [("q", j) for j in range(4)] + [("k", j) for j in range(4)] + [("score", 0)] + [("v", j) for j in range(4)]
    BESIDE = {0: [("tail", 0)], 1: [("combine", 0), ("combine", 1)], 2: [("combine", 2), ("combine", 3)], 3: [("combine", 4)],
              4: [("ln3", 0)], 5: [("norm3", 0), ("combine", 5), ("combine", 6)], 6: [("x3T", 0), ("combine", 7)], 7: [("gate", 0), ("ln2", 0)]}
    for s in range(TILES):
        ORDER += [("score", s + 1)] if s + 1 < TILES else []
        ORDER += [("mix", s - 1)] if s else []
        ORDER += [("turn", s)] + BESIDE[s]
    ORDER += [("mix", TILES - 1), ("gateT", 0), ("ln3", 1), ("up", (0, 0)), ("scoreT", 0), ("norm3", 1), ("latent", 0)]
    ORDER += [("up", (0, 1)), ("x3T", 1), ("expert", (0, 0)), ("gate", 1), ("expert", (0, 1)), ("gateT", 1), ("comb", 0)]
    ORDER += [("up", (1, 0)), ("scoreT", 1), ("out", 0), ("latent", 1), ("up", (1, 1)), ("ln4", 0)]
    ORDER += [("expert", (1, 0)), ("expert", (1, 1)), ("x2T", 0), ("comb", 1), ("x2T", 1), ("out", 1)]

    V_COUNT = {"q": 1, "k": 1, "v": 1, "mix": 1, "turn": 2, "x3T": 2, "gate": 1, "gateT": 1, "scoreT": 1, "latent": 1, "x2T": 2, "comb": 1, "out": 2}
    HI_KINDS = ("q", "k", "v", "turn", "x3T", "latent", "comb", "x2T")
    V_AT, V_BANK, HI_EACH = {}, [], 0
    second_layer = False
    for kind, j in ORDER:
        second_layer = second_layer or kind == "up"
        V_AT[kind, j] = len(V_BANK)
        for g in range(V_COUNT.get(kind, 0)):
            V_BANK.append(6 + g if kind == "out" else 4 + len(V_BANK) % (2 if second_layer else 4))
        HI_EACH += V_COUNT[kind] if kind in HI_KINDS else 0
    V_EACH = len(V_BANK)
    PROLOGUE = 2 * V_COUNT["x2T"]
    S_BANKS = 4
    S_COUNT = {"score": 2, "up": CHUNKS, "expert": CHUNKS}
    S_AT, S_EACH = {}, 0
    for unit in ORDER:
        S_AT[unit] = S_EACH
        S_EACH += S_COUNT.get(unit[0], 0)
    HIDDEN = 2 * EXPERTS
    RELU_RING, RING = 2, 4
    GATHER = 2
    PRE_STEPS = TILES + NORM_STEPS
    ROUTE_STEPS = 2 + 8 + 3 + TOP_STEPS + 5
    CONSTS = 3 + EXPERTS

    with ExitStack() as ctx:
        def sb(name, shape, dt=F32):
            return ctx.enter_context(nc.sbuf_tensor("c_" + name, shape, dt))

        def pair(name, shape):
            return sb(name + "_hi", shape, F32R), sb(name + "_lo", shape, F32R)

        def sem(name):
            return ctx.enter_context(nc.semaphore("c_" + name))

        ps = ctx.enter_context(nc.psum_tensor("c_ps", [P, BANKS, 512], F32))
        wq_hi, wq_lo = pair("wq", [P, CH, C])
        wk_hi, wk_lo = pair("wk", [P, CH, C])
        wv_hi, wv_lo = pair("wv", [P, CH, C])
        gate_hi, gate_lo = pair("gate", [P, CH, EXPERTS])
        fc1_hi, fc1_lo = pair("fc1", [P, CH, LATENT])
        fc2_hi, fc2_lo = pair("fc2", [P, 1, C])
        w1_hi, w1_lo = pair("w1", [P, EXPERTS, P])
        w2_hi, w2_lo = pair("w2", [P, EXPERTS, LATENT])
        up_hi, up_lo = pair("up", [P, CH, SHARED])
        down_hi, down_lo = pair("down", [P, SHARED // P, C])
        bias_q, bias_k, bias_qs = sb("bias_q", [P, CH]), sb("bias_k", [P, CH]), sb("bias_qs", [P, CH])
        bias_v, bias_corr = sb("bias_v", [P, C]), sb("bias_corr", [P, EXPERTS])
        ident, falling = sb("ident", [P, P]), sb("falling", [P, EXPERTS])
        zeros = sb("zeros", [P, 512], BF16)
        pre, x2, x3 = sb("pre", [P, TILES, C]), sb("x2", [P, TILES, C]), sb("x3", [P, TILES, C])
        x2T = sb("x2T", [P, 2, CH, SEQ], F32R)
        x2T_hi, x2T_lo = x2T[:, 0], x2T[:, 1]
        score_rows = x2T[:].rearrange("p a c s -> p (a c s)").bitcast(F32)
        place = sb("place", [P, 16 * SEQ], F32R)
        q_hi, q_lo, k_hi, k_lo = (place[:, j * CH * SEQ:(j + 1) * CH * SEQ].rearrange("p (c s) -> p c s", c=CH) for j in range(4))
        v_hi, v_lo = (place[:, (8 + 2 * j) * SEQ:(10 + 2 * j) * SEQ].rearrange("p (t c) -> p t c", c=C) for j in range(2))
        probT_hi, probT_lo = (place[:, (12 + j) * SEQ:(13 + j) * SEQ].rearrange("p (t s) -> p t s", s=P) for j in range(2))
        hid_hi, hid_lo = (place[:, 8 * j * SEQ:8 * (j + 1) * SEQ].rearrange("p (k s) -> p k s", s=HALF) for j in range(2))
        shared_place = sb("shared_place", [P, (RELU_RING + RING) * HALF])
        prob = shared_place[:, 0:2 * SEQ].rearrange("p (r s) -> p r s", r=2)
        relu = shared_place[:, 0:RELU_RING * HALF].rearrange("p (r s) -> p r s", s=HALF)
        square = shared_place[:, RELU_RING * HALF:].rearrange("p (r s) -> p r s", s=HALF)
        neg_max, row_sum, row_inv = sb("neg_max", [P, TILES]), sb("row_sum", [P, TILES]), sb("row_inv", [P, TILES])
        x3T_hi, x3T_lo = pair("x3T", [P, CH, HALF])
        lat_hi, lat_lo = pair("lat", [P, HALF])
        comb_hi, comb_lo = pair("comb", [P, HALF])
        logit = sb("logit", [EXPERTS, HALF])
        gathered = sb("gathered", [P, GATHER, 2, C])
        slots, gates = sb("slots", [P, 2, TILES], U32), sb("gates", [P, 3, TILES])
        stats, scale, shift, tmp = sb("stats", [P, TILES, 6]), sb("scale", [P, TILES]), sb("shift", [P, TILES]), sb("tmp", [P, 2, TILES])
        pre_stats, pre_scale, pre_shift = sb("pre_stats", [P, TILES, 6]), sb("pre_scale", [P, TILES]), sb("pre_shift", [P, TILES])
        expd, score, choice = (sb(n, [P, HTILES, EXPERTS]) for n in ("expd", "score", "choice"))
        first, second, key0, key1 = (sb(n, [P, HTILES, EXPERTS]) for n in ("first", "second", "key0", "key1"))
        row_m, row_s = sb("row_m", [P, HTILES]), sb("row_s", [P, HTILES])
        group_m, group_n = sb("group_m", [P, HTILES, GROUPS]), sb("group_n", [P, HTILES, GROUPS])
        score_et, scoreT = sb("score_et", [P, EXPERTS, HTILES]), sb("scoreT", [EXPERTS * HTILES, P])

        consts, biases_in = sem("consts"), sem("biases_in")
        weight_in = [sem("weight_in0"), sem("weight_in1")]
        weight_hi, weight_split = sem("weight_hi"), sem("weight_split")
        v_full, v_free = sem("v_full"), sem("v_free")
        s_full, s_free = sem("s_full"), sem("s_free")
        slots_in, gates_in, x1_in = sem("slots_in"), sem("gates_in"), sem("x1_in")
        rows_in = [sem(f"rows_in{j}") for j in range(GATHER)]
        combine_chain, combined, x2_done, bias_added = sem("combine_chain"), sem("combined"), sem("x2_done"), sem("bias_added")
        pre_chain, ln_chain, route_chain = sem("pre_chain"), sem("ln_chain"), sem("route_chain")
        stats_done = sem("stats_done")
        hi_done = sem("hi_done")
        max_done, inv_done, x3_done = sem("max_done"), sem("inv_done"), sem("x3_done")
        exp_done, score_done, scores_stored = sem("exp_done"), sem("score_done"), sem("scores_stored")
        scores_in = [sem(f"scores_in{j}") for j in range(EXPERTS // 2)]
        scaled, squared, hid_hi_done, hid_split = sem("scaled"), sem("squared"), sem("hid_hi_done"), sem("hid_split")
        out_done, out_stored = sem("out_done"), sem("out_stored")

        WEIGHTS = [("wq", wq_hi, wq_lo, 0, CH, SCALE), ("wk", wk_hi, wk_lo, 0, CH, 1.0), ("wv", wv_hi, wv_lo, 0, CH, 1.0),
                   ("gateT", gate_hi, gate_lo, 0, CH, 1.0), ("fc1T", fc1_hi, fc1_lo, 0, CH, 1.0),
                   ("upT", up_hi, up_lo, 0, 1, 1.0), ("upT", up_hi, up_lo, 1, 2, 1.0),
                   ("w1T", w1_hi, w1_lo, 0, EXPERTS, 1.0), ("w2T", w2_hi, w2_lo, 0, EXPERTS, 1.0),
                   ("fc2T", fc2_hi, fc2_lo, 0, 1, 1.0),
                   ("downT", down_hi, down_lo, 0, 4, 1.0), ("downT", down_hi, down_lo, 4, 8, 1.0)]

        def staged(j):
            _, hi, _, a, b, _ = WEIGHTS[j]
            return prob[:, j % 2, 0:(b - a) * hi.shape[2]].rearrange("p (k n) -> p k n", k=b - a)

        def is_first(b):
            return isinstance(b, int) and b == 0

        def v_number(b, at):
            skipped = sum(V_COUNT["x2T"] for j in range(2) if at > V_AT["x2T", j]) if isinstance(b, int) and b == BATCHES - 1 else 0
            return PROLOGUE + b * V_EACH + at - skipped

        def v_upto(b, unit):
            return v_number(b, V_AT[unit] + V_COUNT[unit[0]] - 1) + 1

        def v_bank(unit, g=0):
            return V_BANK[V_AT[unit] + g]

        def v_open(pe, b, unit, g=0):
            at = V_AT[unit] + g
            skipped = [V_AT["x2T", c] + h for c in range(CH) for h in range(2)] if isinstance(b, int) and b == BATCHES - 1 else []
            before = [a for a in range(at) if V_BANK[a] == V_BANK[at] and a not in skipped]
            if before:
                pe.wait_ge(v_free, v_number(b, before[-1]) + 1)
            elif not is_first(b):
                pe.wait_ge(v_free, v_number(b - 1, max(a for a in range(V_EACH) if V_BANK[a] == V_BANK[at])) + 1)
            return ps[:, V_BANK[at], :]

        def s_upto(b, unit, k):
            return b * S_EACH + S_AT[unit] + k + 1

        def s_bank(unit, k=0):
            return (S_AT[unit] + k) % S_BANKS

        def hidden(b, kind, j, k):
            place = (0 if kind == "up" else EXPERTS) + CHUNKS * j[1] + k
            return HIDDEN * (HALVES * b + j[0]) + place, place

        def order(b):
            return [unit for unit in ORDER
                    if not (isinstance(b, int) and b == BATCHES - 1 and unit[0] in ("combine", "ln2", "x2T"))
                    and not (is_first(b) and unit[0] == "tail")]

        block = ctx.enter_context(nc.Block())

        @block.sync
        def _(sp):
            def load(b):
                sp.dma_start(slots[:].rearrange("p a t -> p (a t)"), d["slots"][bass.ds(b * P, P), :]).then_inc(slots_in, 16)
                sp.dma_start(gates[:].rearrange("p a t -> p (a t)"), d["gates"][bass.ds(b * P, P), :]).then_inc(gates_in, 16)
                sp.dma_start(pre[:], d["x1"][bass.ds(b * SEQ, SEQ), :].rearrange("(t p) c -> p t c", p=P)).then_inc(x1_in, 16)

            def spread_scores(b, h):
                sp.wait_ge(v_free, v_upto(b, ("scoreT", h)))
                sp.dma_start(d["score_rows"][bass.ds(2 * b + h, 1), :].rearrange("a (r s) -> (a r) s", s=P), scoreT[:]).then_inc(scores_stored, 16)
                sp.wait_ge(scores_stored, 32 * b + 16 * h + 16)
                for j in range(EXPERTS // 2):
                    if h == 1:
                        sp.wait_ge(scaled, 2 * EXPERTS * b + 2 * j + 2)
                    sp.dma_start(score_rows[:, bass.ts(j, 2 * HALF)],
                                 d["score_rows"][bass.ds(2 * b + h, 1), bass.ts(j, 2 * HALF)].to_broadcast([P, 2 * HALF])).then_inc(scores_in[j], 16)

            def store(b, h):
                sp.wait_ge(out_done, 2 * b + h + 1)
                sp.dma_start(d["out"][bass.ds(b * SEQ + h * HALF, HALF), :].rearrange("(t p) c -> p t c", p=P),
                             x3[:, bass.ts(h, HTILES), :]).then_inc(out_stored, 16)

            def body(b, end):
                if not end:
                    sp.wait_ge(x2_done, b + 1)
                    load(b + 1)
                if not is_first(b):
                    store(b - 1, 1)
                spread_scores(b, 0)
                spread_scores(b, 1)
                store(b, 0)

            load(0)
            sp.dma_start(bias_q[:], d["bq"]).then_inc(biases_in, 16)
            sp.dma_start(bias_k[:], d["bk"]).then_inc(biases_in, 16)
            sp.dma_start(bias_v[:], d["bv"].partition_broadcast(P)).then_inc(biases_in, 16)
            sp.dma_start(bias_corr[:], d["corr"].partition_broadcast(P)).then_inc(biases_in, 16)
            for j, (w, _, _, a, b, _) in enumerate(WEIGHTS):
                wait_past(sp, weight_split, j - 1)
                sp.dma_start(staged(j), d[w].rearrange("(k p) n -> p k n", p=P)[:, a:b, :] if w not in ("w1T", "w2T")
                             else d[w].rearrange("p (k n) -> p k n", k=EXPERTS)).then_inc(weight_in[j % 2], 16)
            body(0, False)
            with sp.Fori(1, BATCHES - 1) as b:
                body(b, False)
            body(BATCHES - 1, True)
            store(BATCHES - 1, 1)
            sp.wait_ge(out_stored, 32 * BATCHES)

        @block.gpsimd
        def _(pool):
            pool.memset(ident[:], 0.0).then_inc(consts, 1)
            pool.memset(zeros[:], 0.0).then_inc(consts, 1)
            for e in range(EXPERTS):
                pool.memset(falling[:, e:e + 1], float(EXPERTS - e)).then_inc(consts, 1)
            pool.wait_ge(consts, 1)
            pool.affine_select(out=ident[:], in_=ident[:], compare_op=ALU.not_equal, fill=1.0,
                               base=0, pattern=[[-1, P]], channel_multiplier=1).then_inc(consts, 1)

            def gather(b):
                for t in range(TILES):
                    producer, upto = (slots_in, 16 * b + 16) if t < GATHER else (combined, TILES * b + t - GATHER + 1)
                    if not isinstance(upto, int):
                        pool.to_reg(upto)
                    pool.wait_ge(biases_in, 64)
                    pool.wait_ge(producer, upto)
                    for a in range(2):
                        pool.indirect_dma_start(gathered[:, t % GATHER, a, :], None, d["ys"],
                                                bass.IndirectOffsetOnAxis(ap=slots[:, a, t:t + 1], axis=0),
                                                bounds_check=TRASH + P - 1, oob_is_err=False).then_inc(rows_in[t % GATHER], 16)

            def add_bias(b):
                pool.wait_ge(v_full, PROLOGUE if is_first(b) else v_upto(b - 1, ("x2T", 1)))
                pool.tensor_tensor(x2[:], x2[:], bias_v[:].unsqueeze(1).to_broadcast([P, TILES, C]), ALU.add).then_inc(bias_added, 1)

            def body(b, end):
                if not end:
                    gather(b + 1)
                for kind, j in order(b):
                    if kind not in ("up", "expert"):
                        continue
                    for k in range(CHUNKS):
                        n, place = hidden(b, kind, j, k)
                        pool.wait_ge(s_free, s_upto(b, (kind, j), k))
                        wait_past(pool, hid_split, n - RING + 1)
                        t = relu[:, place % RELU_RING, :]
                        if kind == "up":
                            pool.tensor_tensor(square[:, place % RING, :], t, t, ALU.mult).then_inc(squared, 1)
                        else:
                            e = place - EXPERTS
                            pool.wait_ge(scores_in[e // 2], 16 * (HALVES * b + j[0] + 1))
                            pool.tensor_tensor(square[:, place % RING, :], t, score_rows[:, bass.ts(e, HALF)], ALU.mult).then_inc(scaled, 1)
                if not end:
                    add_bias(b + 1)

            gather(0)
            add_bias(0)
            body(0, False)
            with pool.Fori(1, BATCHES - 1) as b:
                body(b, False)
            body(BATCHES - 1, True)

        @block.scalar
        def _(act):
            def split_weights():
                for j, (_, hi, _, a, b, scale_w) in enumerate(WEIGHTS):
                    act.wait_ge(weight_in[j % 2], 16 * (j // 2) + 16)
                    act.activation(hi[:, a:b, :], staged(j), ACT.Copy, scale=scale_w).then_inc(weight_hi, 1)

            def normed(out, rows, t, scales, shifts):
                return act.activation(out[:, t, :], rows[:, t, :], ACT.Identity, scale=scales[:, t:t + 1], bias=shifts[:, t:t + 1])

            def norm_x2(b, t):
                if t == 0:
                    act.wait_ge(pre_chain, (b + 1) * PRE_STEPS)
                    wait_past(act, x3_done, 2 * b)
                norm = normed(x2, pre, t, pre_scale, pre_shift)
                if t == TILES - 1:
                    norm.then_inc(x2_done, 1)

            def turn_rows(c, first_n):
                for h in range(2):
                    act.wait_ge(v_full, first_n + h + 1)
                    act.activation(x2T_hi[:, c, bass.ts(h, HALF)], ps[:, v_bank(("x2T", c), h), :], ACT.Copy).then_inc(hi_done, 1)

            def tail(b):
                act.wait_ge(ln_chain, (4 * b + 4) * NORM_STEPS)
                for t in range(HTILES, TILES):
                    last = normed(x3, x3, t, scale, shift)
                last.then_inc(out_done, 1)

            def norm4(b, t):
                if t == 0:
                    act.wait_ge(ln_chain, (4 * b + 3) * NORM_STEPS)
                norm = normed(x3, x3, t, scale, shift)
                if t == HTILES - 1:
                    norm.then_inc(out_done, 1)

            def body(b, end):
                def copy_hi(unit, g, out, func=ACT.Copy, **kw):
                    act.wait_ge(v_full, v_number(b, V_AT[unit] + g) + 1)
                    act.activation(out, ps[:, v_bank(unit, g), :], func, **kw).then_inc(hi_done, 1)

                for unit in order(b):
                    kind, j = unit
                    if kind in ("q", "k"):
                        hi, bias = (q_hi, bias_qs) if kind == "q" else (k_hi, bias_k)
                        copy_hi(unit, 0, hi[:, j % CH, bass.ts(j // CH, HALF)], ACT.Identity, bias=bias[:, j % CH:j % CH + 1])
                    elif kind == "v":
                        copy_hi(unit, 0, v_hi[:, 2 * j:2 * j + 2, :].rearrange("p t c -> p (t c)"))
                    elif kind == "score":
                        bank = s_bank(unit)
                        act.wait_ge(max_done, TILES * b + j + 1)
                        if j == 0 and not is_first(b):
                            act.wait_ge(hid_hi_done, HALVES * HIDDEN * b)
                        act.activation(prob[:, j % 2, :], ps[:, bank:bank + 2, :].rearrange("p a n -> p (a n)"), ACT.Exp,
                                       bias=neg_max[:, j:j + 1], accum_out=row_sum[:, j:j + 1]).then_inc(s_free, 2)
                    elif kind == "turn":
                        for g in range(2):
                            copy_hi(unit, g, probT_hi[:, 4 * g:4 * g + 4, :].rearrange("p t s -> p (t s)"))
                    elif kind == "norm3":
                        act.wait_ge(ln_chain, (4 * b + j + 1) * NORM_STEPS)
                        if not is_first(b):
                            act.wait_ge(out_stored, 32 * b)
                        for t in range(HTILES * j, HTILES * (j + 1)):
                            last = normed(x3, x2, t, scale, shift)
                        last.then_inc(x3_done, 1)
                    elif kind == "x3T":
                        for c in range(CH):
                            copy_hi(unit, c, x3T_hi[:, c, :])
                    elif kind == "gateT":
                        act.wait_ge(v_full, v_number(b, V_AT[unit]) + 1)
                        wait_past(act, score_done, 2 * b + j)
                        act.activation(expd[:].rearrange("p t e -> p (t e)"), ps[:, v_bank(unit), 0:HTILES * EXPERTS], ACT.Exp, scale=-1.0).then_inc(exp_done, 1)
                    elif kind == "latent":
                        copy_hi(unit, 0, lat_hi[:])
                    elif kind == "comb":
                        copy_hi(unit, 0, comb_hi[:])
                    elif kind == "x2T":
                        act.wait_ge(scaled, 2 * EXPERTS * (b + 1))
                        turn_rows(j, v_number(b, V_AT[unit]))
                    elif kind == "tail":
                        tail(b - 1)
                    elif kind in ("up", "expert"):
                        lag = 1 if kind == "up" else 2
                        for k in range(CHUNKS + lag):
                            if k < CHUNKS:
                                n, place = hidden(b, kind, j, k)
                                act.wait_ge(s_full, s_upto(b, unit, k))
                                wait_past(act, squared, n - RELU_RING + 1)
                                if kind == "up" or k < RELU_RING:
                                    wait_past(act, hid_hi_done, n - RELU_RING + 1)
                                act.activation(relu[:, place % RELU_RING, :], ps[:, s_bank(unit, k), :], ACT.Relu).then_inc(s_free, 1)
                            if k >= lag:
                                n, place = hidden(b, kind, j, k - lag)
                                if kind == "up":
                                    act.wait_ge(s_free, s_upto(b, unit, k - lag))
                                    act.activation(hid_hi[:, place, :], relu[:, place % RELU_RING, :], ACT.Square).then_inc(hid_hi_done, 1)
                                else:
                                    act.wait_ge(squared, n + 1)
                                    act.activation(hid_hi[:, place, :], square[:, place % RING, :], ACT.Copy).then_inc(hid_hi_done, 1)
                            if k < CHUNKS and kind == "expert" and j[0] == 0 and not end:
                                norm_x2(b + 1, CHUNKS * j[1] + k)
                            elif k < CHUNKS and unit == ("expert", (1, 0)):
                                norm4(b, k)

            split_weights()
            act.wait_ge(biases_in, 64)
            for t in range(TILES):
                norm_x2(0, t)
            for c in range(CH):
                turn_rows(c, 2 * c)
            act.wait_ge(weight_split, len(WEIGHTS) + 1)
            body(0, False)
            with act.Fori(1, BATCHES - 1) as b:
                body(b, False)
            body(BATCHES - 1, True)
            tail(BATCHES - 1)

        @block.vector
        def _(v):
            def split_weights():
                for j, (_, hi, lo, a, b, scale_w) in enumerate(WEIGHTS):
                    v.wait_ge(weight_hi, j + 1)
                    v.scalar_tensor_tensor(lo[:, a:b, :], staged(j), scale_w, f32(hi[:, a:b, :]), ALU.mult, ALU.subtract).then_inc(weight_split, 1)

            def split_rows(c, hi_n):
                for h in range(2):
                    v.wait_ge(hi_done, hi_n + h + 1)
                    at = (slice(None), c, bass.ts(h, HALF))
                    v.tensor_tensor(x2T_lo[at], ps[:, v_bank(("x2T", c), h), :], f32(x2T_hi[at]), ALU.subtract).then_inc(v_free, 1)

            def combine(b, t):
                chain = Chain(v, combine_chain, 2 * (TILES * b + t))
                rows, place = pre[:, t, :], gathered[:, t % GATHER]
                if t == 0:
                    v.wait_ge(x1_in, 16 * b + 16)
                    v.wait_ge(gates_in, 16 * b + 16)
                chain.step(v.scalar_tensor_tensor(rows, rows, gates[:, 2, t:t + 1], rows, ALU.mult, ALU.add))
                v.wait_ge(rows_in[t % GATHER], 32 * (TILES // GATHER * b + t // GATHER + 1))
                chain.then(v.scalar_tensor_tensor, rows, place[:, 0, :], gates[:, 0, t:t + 1], rows, ALU.mult, ALU.add)
                chain.wait()
                v.scalar_tensor_tensor(rows, place[:, 1, :], gates[:, 1, t:t + 1], rows, ALU.mult, ALU.add).then_inc(combined, 1)
                v.wait_ge(combined, TILES * b + t + 1)
                v.bn_stats(pre_stats[:, t, :], rows).then_inc(pre_chain, 1)

            def scale_pre(b):
                chain = Chain(v, pre_chain, b * PRE_STEPS)
                chain.n = TILES
                norm_scale(v, chain, pre_stats[:], pre_scale[:], pre_shift[:], tmp[:])
                assert chain.n == PRE_STEPS, chain.n

            def scale_half(b, which, h):
                chain = Chain(v, ln_chain, (4 * b + which) * NORM_STEPS)
                half = bass.ts(h, HTILES)
                v.wait_ge(stats_done, HTILES * (4 * b + which + 1))
                norm_scale(v, chain, stats[:, half, :], scale[:, half], shift[:, half], tmp[:, :, half])
                assert chain.n == NORM_STEPS, chain.n

            def tail(b):
                scale_half(b, 3, 1)

            def route(b, h, n):
                chain = Chain(v, route_chain, (2 * b + h) * ROUTE_STEPS)
                v.wait_ge(exp_done, 2 * b + h + 1)
                v.tensor_scalar(expd[:], expd[:], 1.0, None, ALU.add).then_inc(v_free, 1)
                v.wait_ge(v_free, n + 1)
                chain.step(v.reciprocal(score[:], expd[:]))
                chain.then(v.tensor_tensor, choice[:], score[:], along(bias_corr[:], HTILES), ALU.add)
                groups = choice[:].rearrange("p t (g e) -> p (t g) e", g=GROUPS)
                keys = key0[:].rearrange("p t (g e) -> p (t g) e", g=GROUPS)
                keys1 = key1[:].rearrange("p t (g e) -> p (t g) e", g=GROUPS)
                marks, seconds = group_m[:].rearrange("p t g -> p (t g)"), group_n[:].rearrange("p t g -> p (t g)")
                chain.then(v.tensor_reduce, marks, groups, AX.X, ALU.max)
                chain.then(v.tensor_tensor, keys, groups, across(marks, GSIZE), ALU.is_equal)
                chain.then(v.tensor_tensor, keys, keys, along(falling[:, 0:GSIZE], HTILES * GROUPS), ALU.mult)
                chain.then(v.tensor_reduce, seconds, keys, AX.X, ALU.max)
                chain.then(v.tensor_tensor, keys, keys, across(seconds, GSIZE), ALU.is_equal)
                chain.then(v.scalar_tensor_tensor, keys1, keys, LOWEST, groups, ALU.mult, ALU.add)
                chain.then(v.tensor_reduce, seconds, keys1, AX.X, ALU.max)
                chain.then(v.tensor_tensor, group_m[:], group_m[:], group_n[:], ALU.add)
                chain.then(v.tensor_tensor, group_n[:, :, 0], group_m[:, :, 0], group_m[:, :, 1], ALU.is_ge)
                chain.then(v.tensor_scalar, group_n[:, :, 1], group_n[:, :, 0], -1.0, 1.0, ALU.mult, ALU.add)
                chain.then(v.tensor_tensor, groups, groups, across(seconds, GSIZE), ALU.mult)
                top_two(v, chain, first[:], second[:], choice[:], falling[:], row_m[:], (key0[:], key1[:]), HTILES)
                chain.then(v.tensor_tensor, first[:], first[:], second[:], ALU.add)
                chain.then(v.tensor_tensor, score[:], score[:], first[:], ALU.mult)
                chain.then(v.tensor_reduce, row_s[:], score[:], AX.X, ALU.add)
                chain.then(v.tensor_scalar, row_s[:], row_s[:], NORM_EPS, None, ALU.add)
                chain.then(v.reciprocal, row_s[:], row_s[:])
                chain.wait()
                v.tensor_tensor(score_et[:].rearrange("p e t -> p t e"), score[:], across(row_s[:], EXPERTS), ALU.mult).then_inc(score_done, 1)
                assert chain.n == ROUTE_STEPS, chain.n

            def body(b, end):
                hi_n = [b * HI_EACH + PROLOGUE]

                def split_lo(unit, g, hi, lo, bias=None):
                    hi_n[0] = hi_n[0] + 1
                    bank = ps[:, v_bank(unit, g), :]
                    v.wait_ge(hi_done, hi_n[0])
                    if bias is None:
                        v.tensor_tensor(lo, bank, f32(hi), ALU.subtract).then_inc(v_free, 1)
                    else:
                        v.scalar_tensor_tensor(lo, bank, bias, f32(hi), ALU.add, ALU.subtract).then_inc(v_free, 1)

                for unit in order(b):
                    kind, j = unit
                    n = v_number(b, V_AT[unit])
                    if kind in ("q", "k"):
                        hi, lo, bias = (q_hi, q_lo, bias_qs) if kind == "q" else (k_hi, k_lo, bias_k)
                        at = (slice(None), j % CH, bass.ts(j // CH, HALF))
                        split_lo(unit, 0, hi[at], lo[at], bias[:, j % CH:j % CH + 1])
                    elif kind == "v":
                        split_lo(unit, 0, v_hi[:, 2 * j:2 * j + 2, :].rearrange("p t c -> p (t c)"), v_lo[:, 2 * j:2 * j + 2, :].rearrange("p t c -> p (t c)"))
                    elif kind == "score":
                        bank = s_bank(unit)
                        v.wait_ge(s_full, s_upto(b, unit, 1))
                        v.tensor_reduce(neg_max[:, j:j + 1], ps[:, bank:bank + 2, :].rearrange("p a n -> p (a n)"), AX.X, ALU.max, negate=True).then_inc(max_done, 1)
                    elif kind == "turn":
                        for g in range(2):
                            at = (slice(None), slice(4 * g, 4 * g + 4))
                            split_lo(unit, g, probT_hi[at].rearrange("p t s -> p (t s)"), probT_lo[at].rearrange("p t s -> p (t s)"))
                    elif kind == "mix":
                        v.wait_ge(s_free, s_upto(b, ("score", j), 1))
                        v.reciprocal(row_inv[:, j:j + 1], row_sum[:, j:j + 1]).then_inc(inv_done, 1)
                        v.wait_ge(v_full, n + 1)
                        v.wait_ge(bias_added, b + 1)
                        v.wait_ge(inv_done, TILES * b + j + 1)
                        v.scalar_tensor_tensor(x2[:, j, :], ps[:, v_bank(unit), 0:C], row_inv[:, j:j + 1], x2[:, j, :], ALU.mult, ALU.add).then_inc(v_free, 1)
                        v.wait_ge(v_free, n + 1)
                        v.bn_stats(stats[:, j, :], x2[:, j, :]).then_inc(stats_done, 1)
                    elif kind == "ln3":
                        if not is_first(b):
                            v.wait_ge(out_done, 2 * b)
                        scale_half(b, j, j)
                    elif kind == "x3T":
                        for c in range(CH):
                            split_lo(unit, c, x3T_hi[:, c, :], x3T_lo[:, c, :])
                    elif kind == "gate":
                        v.wait_ge(v_full, n + 1)
                        v.tensor_copy(logit[:], ps[0:EXPERTS, v_bank(unit), :]).then_inc(v_free, 1)
                    elif kind == "gateT":
                        route(b, j, n)
                    elif kind == "scoreT":
                        v.wait_ge(v_full, n + 1)
                        wait_past(v, scores_stored, 32 * b + 16 * j)
                        v.tensor_copy(scoreT[:], ps[0:EXPERTS * HTILES, v_bank(unit), 0:P]).then_inc(v_free, 1)
                    elif kind == "latent":
                        split_lo(unit, 0, lat_hi[:], lat_lo[:])
                    elif kind == "comb":
                        split_lo(unit, 0, comb_hi[:], comb_lo[:])
                    elif kind == "combine":
                        combine(b + 1, j)
                    elif kind == "ln2":
                        scale_pre(b + 1)
                    elif kind == "x2T":
                        split_rows(j, hi_n[0])
                        hi_n[0] = hi_n[0] + V_COUNT["x2T"]
                    elif kind == "tail":
                        tail(b - 1)
                    elif kind in ("up", "expert"):
                        lag = 0 if kind == "up" else 1
                        for k in range(CHUNKS + lag):
                            if lag and k < CHUNKS:
                                n, place = hidden(b, kind, j, k)
                                v.wait_ge(scaled, EXPERTS * (HALVES * b + j[0]) + place - EXPERTS + 1)
                                v.tensor_tensor(square[:, place % RING, :], square[:, place % RING, :], relu[:, place % RELU_RING, :], ALU.mult).then_inc(squared, 1)
                            if k >= lag:
                                n, place = hidden(b, kind, j, k - lag)
                                v.wait_ge(squared, n + 1)
                                v.wait_ge(hid_hi_done, n + 1)
                                v.tensor_tensor(hid_lo[:, place, :], square[:, place % RING, :], f32(hid_hi[:, place, :]), ALU.subtract).then_inc(hid_split, 1)
                    elif kind == "out":
                        for g in range(2):
                            at = HTILES * j + 2 * g
                            v.wait_ge(v_full, n + g + 1)
                            v.tensor_tensor(x3[:, at:at + 2, :], ps[:, v_bank(unit, g), :].rearrange("p (t c) -> p t c", c=C), x3[:, at:at + 2, :], ALU.add).then_inc(v_free, 1)
                        for t in range(HTILES):
                            v.wait_ge(v_free, n + t // 2 + 1)
                            v.bn_stats(stats[:, HTILES * j + t, :], x3[:, HTILES * j + t, :]).then_inc(stats_done, 1)
                    elif kind == "ln4":
                        v.wait_ge(x3_done, 2 * b + 2)
                        scale_half(b, 2, 0)

            v.wait_ge(consts, CONSTS)
            split_weights()
            v.wait_ge(biases_in, 64)
            v.tensor_scalar(bias_qs[:], bias_q[:], SCALE, None, ALU.mult).then_inc(weight_split, 1)
            for t in range(TILES):
                combine(0, t)
            scale_pre(0)
            for c in range(CH):
                split_rows(c, 2 * c)
            v.wait_ge(weight_split, len(WEIGHTS) + 1)
            body(0, False)
            with v.Fori(1, BATCHES - 1) as b:
                body(b, False)
            body(BATCHES - 1, True)
            tail(BATCHES - 1)

        @block.tensor
        def _(pe):
            def turn_rows(b, c, opened):
                pe.wait_ge(x2_done, b + 1)
                for h in range(2):
                    out = opened(h)
                    for t in range(HTILES):
                        last = pe.transpose(out[:, bass.ts(t, P)], x2[:, HTILES * h + t, bass.ts(c, P)], ident[:])
                    last.then_inc(v_full, 1)

            def body(b, end):
                def s_open(unit, k):
                    wait_past(pe, s_free, s_upto(b, unit, k) - S_BANKS)
                    return ps[:, s_bank(unit, k), :]

                pe.wait_ge(v_free, PROLOGUE if is_first(b) else v_upto(b - 1, ("x2T", 1)))
                for unit in order(b):
                    kind, j = unit
                    if kind in ("q", "k"):
                        w_hi, w_lo = (wq_hi, wq_lo) if kind == "q" else (wk_hi, wk_lo)
                        h, p = j // CH, j % CH
                        product(pe, v_open(pe, b, unit), [(w_hi[:, c, bass.ts(p, P)], w_lo[:, c, bass.ts(p, P)], x2T_hi[:, c, bass.ts(h, HALF)], x2T_lo[:, c, bass.ts(h, HALF)])
                                                          for c in range(CH)]).then_inc(v_full, 1)
                    elif kind == "v":
                        out = v_open(pe, b, unit)
                        for t in (2 * j, 2 * j + 1):
                            last = product(pe, out[:, bass.ts(t % 2, C)],
                                           [(x2T_hi[:, c, bass.ts(t, P)], x2T_lo[:, c, bass.ts(t, P)], wv_hi[:, c, :], wv_lo[:, c, :]) for c in range(CH)])
                        last.then_inc(v_full, 1)
                    elif kind == "score":
                        pe.wait_ge(v_free, v_upto(b, ("k", 3)))
                        for h in range(2):
                            product(pe, s_open(unit, h), [(q_hi[:, c, bass.ts(j, P)], q_lo[:, c, bass.ts(j, P)], k_hi[:, c, bass.ts(h, HALF)], k_lo[:, c, bass.ts(h, HALF)])
                                                          for c in range(CH)]).then_inc(s_full, 1)
                    elif kind == "turn":
                        pe.wait_ge(s_free, s_upto(b, ("score", j), 1))
                        for g in range(2):
                            out = v_open(pe, b, unit, g)
                            for t in range(4):
                                last = pe.transpose(out[:, bass.ts(t, P)], prob[:, j % 2, bass.ts(4 * g + t, P)], ident[:])
                            last.then_inc(v_full, 1)
                    elif kind == "mix":
                        pe.wait_ge(v_free, v_upto(b, ("turn", j)))
                        product(pe, v_open(pe, b, unit)[:, 0:C], [(probT_hi[:, t, :], probT_lo[:, t, :], v_hi[:, t, :], v_lo[:, t, :]) for t in range(TILES)]).then_inc(v_full, 1)
                    elif kind == "x3T":
                        pe.wait_ge(x3_done, 2 * b + j + 1)
                        for c in range(CH):
                            out = v_open(pe, b, unit, c)
                            for t in range(HTILES):
                                last = pe.transpose(out[:, bass.ts(t, P)], x3[:, HTILES * j + t, bass.ts(c, P)], ident[:])
                            last.then_inc(v_full, 1)
                    elif kind == "gate":
                        pe.wait_ge(v_free, v_upto(b, ("x3T", j)))
                        product(pe, v_open(pe, b, unit)[0:EXPERTS, :], [(gate_hi[:, c, :], gate_lo[:, c, :], x3T_hi[:, c, :], x3T_lo[:, c, :]) for c in range(CH)]).then_inc(v_full, 1)
                    elif kind == "gateT":
                        logit_there = v_upto(b, ("gate", j))
                        if not isinstance(b, int):
                            pe.to_reg(logit_there)
                        pe.wait_ge(weight_split, len(WEIGHTS) + 1)
                        pe.wait_ge(v_free, logit_there)
                        out = ps[:, v_bank(unit), :]
                        for t in range(HTILES):
                            last = pe.transpose(out[:, bass.ts(t, EXPERTS)], logit[:, bass.ts(t, P)], ident[0:EXPERTS, 0:EXPERTS])
                        last.then_inc(v_full, 1)
                    elif kind == "scoreT":
                        pe.wait_ge(score_done, 2 * b + j + 1)
                        pe.transpose(v_open(pe, b, unit)[0:EXPERTS * HTILES, 0:P], score_et[:].rearrange("p e t -> p (e t)"), ident[:]).then_inc(v_full, 1)
                    elif kind == "latent":
                        pe.wait_ge(v_free, v_upto(b, ("x3T", j)))
                        product(pe, v_open(pe, b, unit), [(fc1_hi[:, c, :], fc1_lo[:, c, :], x3T_hi[:, c, :], x3T_lo[:, c, :]) for c in range(CH)]).then_inc(v_full, 1)
                    elif kind == "up":
                        pe.wait_ge(v_free, v_upto(b, ("x3T", j[0])))
                        for k in range(CHUNKS):
                            n = CHUNKS * j[1] + k
                            product(pe, s_open(unit, k), [(up_hi[:, c, bass.ts(n, P)], up_lo[:, c, bass.ts(n, P)], x3T_hi[:, c, :], x3T_lo[:, c, :])
                                                          for c in range(CH)]).then_inc(s_full, 1)
                    elif kind == "expert":
                        h, part = j
                        pe.wait_ge(v_free, v_upto(b, ("latent", h)))
                        for k in range(CHUNKS):
                            e = CHUNKS * part + k
                            product(pe, s_open(unit, k), [(w1_hi[:, e, :], w1_lo[:, e, :], lat_hi[:], lat_lo[:])]).then_inc(s_full, 1)
                            t, some = 2 * part + k // 2, range(4 * (k % 2), 4 * (k % 2) + 4)
                            pe.wait_ge(hid_split, hidden(b, "up", (h, k % 2), CHUNKS - 1)[0] + 1)
                            out = ps[:, v_bank(("out", h), part), :]
                            if k == 0:
                                pe.matmul(v_open(pe, b, ("out", h), part), zeros[:, 0:P], zeros[:], start=True, stop=False)
                            accumulate(pe, out[:, bass.ts(t % 2, C)], [(hid_hi[:, m, bass.ts(t, P)], hid_lo[:, m, bass.ts(t, P)], down_hi[:, m, :], down_lo[:, m, :])
                                                                       for m in some])
                    elif kind == "x2T":
                        turn_rows(b + 1, j, lambda h: v_open(pe, b, unit, h))
                    elif kind == "comb":
                        pe.wait_ge(hid_split, HIDDEN * (HALVES * b + j + 1))
                        product(pe, v_open(pe, b, unit), [(w2_hi[:, e, :], w2_lo[:, e, :], hid_hi[:, EXPERTS + e, :], hid_lo[:, EXPERTS + e, :])
                                                          for e in range(EXPERTS)]).then_inc(v_full, 1)
                    elif kind == "out":
                        pe.wait_ge(v_free, v_upto(b, ("comb", j)))
                        for t in range(HTILES):
                            last = accumulate(pe, ps[:, v_bank(unit, t // 2), bass.ts(t % 2, C)],
                                              [(comb_hi[:, bass.ts(t, P)], comb_lo[:, bass.ts(t, P)], fc2_hi[:, 0, :], fc2_lo[:, 0, :])], stop=(t % 2 == 1))
                            if t % 2:
                                last.then_inc(v_full, 1)

            pe.wait_ge(consts, CONSTS)

            for c in range(CH):
                wait_past(pe, v_free, 2 * c)
                turn_rows(0, c, lambda h: ps[:, v_bank(("x2T", c), h), :])
            pe.wait_ge(weight_split, len(WEIGHTS) + 1)
            body(0, False)
            with pe.Fori(1, BATCHES - 1) as b:
                body(b, False)
            body(BATCHES - 1, True)


def program(nc, d):
    d["x1"] = nc.dram_tensor("x1_rows", (TOKENS, C), F32).ap()
    d["xs"] = nc.dram_tensor("expert_rows", (REAL * CAP, C), F32).ap()
    d["ys"] = nc.dram_tensor("expert_results", (REAL * CAP + P, C), F32).ap()
    d["slots"] = nc.dram_tensor("slot_rows", (BATCHES * P, 2 * TILES), U32).ap()
    d["gates"] = nc.dram_tensor("gate_rows", (BATCHES * P, 3 * TILES), F32).ap()
    d["score_rows"] = nc.dram_tensor("score_rows", (2 * BATCHES, EXPERTS * HALF), F32).ap()
    stage_a(nc, d)
    stage_b(nc, d)
    stage_c(nc, d)


def kernel(**inputs):
    import numpy as np
    import concourse.bacc as bacc
    from concourse.bass_utils import run_bass_kernel_spmd

    def rows(name):
        a = np.asarray(inputs[name])
        return a.reshape(-1, a.shape[-1])

    qkv = rows("L0_attn_qkv_weight")
    arrays = {
        "x": rows("L0_attn_x"), "xT": rows("L0_attn_x").T,
        "wqT": qkv[:C].T, "wkvT": qkv[C:].T, "projT": rows("L0_attn_proj_weight").T, "proj_bias": inputs["L0_attn_proj_bias"],
        "routerT": rows("L0_ffn_router_w").T, "router_b": inputs["L0_ffn_router_b"],
        "w_in": rows("L0_ffn_experts_inter"), "w_out": rows("L0_ffn_experts_out"),
        "wq": rows("L1_attn_W_q"), "wk": rows("L1_attn_W_k"), "wv": rows("L1_attn_W_v"),
        "bq": np.asarray(inputs["L1_attn_b_q"]).reshape(CH, P).T, "bk": np.asarray(inputs["L1_attn_b_k"]).reshape(CH, P).T, "bv": inputs["L1_attn_b_v"],
        "gateT": rows("L1_ffn_gate").T, "corr": inputs["L1_ffn_corr_bias"],
        "fc1T": rows("L1_ffn_fc1_w").T, "fc2T": rows("L1_ffn_fc2_w").T,
        "w1T": rows("L1_ffn_w1").T, "w2T": rows("L1_ffn_w2").reshape(EXPERTS, LATENT, -1).transpose(2, 0, 1).reshape(-1, EXPERTS * LATENT),
        "upT": rows("L1_ffn_up_w").T, "downT": rows("L1_ffn_down_w").T,
    }
    arrays = {name: np.ascontiguousarray(a) for name, a in arrays.items()}
    nc = bacc.Bacc("TRN2", target_bir_lowering=False, num_devices=1)
    d = {name: nc.dram_tensor(name, a.shape, mybir.dt.from_np(a.dtype), kind="ExternalInput").ap() for name, a in arrays.items()}
    d["out"] = nc.dram_tensor("out", (TOKENS, C), F32, kind="ExternalOutput").ap()
    program(nc, d)
    got = run_bass_kernel_spmd(nc, [arrays], core_ids=[0])
    return got.results[0]["out"].reshape(BATCHES, SEQ, C)
```

```python
import concourse.bass as bass
from concourse import mybir
from contextlib import ExitStack

F32 = mybir.dt.float32
F32R = mybir.dt.float32r
BF16 = mybir.dt.bfloat16
I32 = mybir.dt.int32
U32 = mybir.dt.uint32
ALU = mybir.AluOpType
ACT = mybir.ActivationFunctionType
AX = mybir.AxisListType

P = 128
BATCHES, SEQ, C = 8, 1024, 256
TOKENS = BATCHES * SEQ
TILES = SEQ // P
CH = C // P
HALF = SEQ // 2
HTILES = HALF // P
HEADS = 32
HEAD = C // HEADS
ATTN_EPS = 1e-15
LN_EPS = 1e-5
EXPERTS = 8
REAL = EXPERTS - 1
INTER = 1024
ICH = INTER // P
CAP = TOKENS // EXPERTS
TRASH = REAL * CAP
LATENT = 128
SHARED = 1024
GROUPS = 2
GSIZE = EXPERTS // GROUPS
NORM_EPS = 1e-20
SCALE = C ** -0.5
LOWEST = -3.0e38
RSQRT_MAGIC = 0x5F3759DF
ROOT_BITS = 4
BANKS = 8


def wait_past(eng, sem, value):
    if not isinstance(value, int) or value > 0:
        eng.wait_ge(sem, value)


class Turns:

    def __init__(self, start, offset, banks):
        self.start, self.offset, self.banks, self.n = start, offset, banks, 0

    def take(self):
        bank = self.banks[(self.offset + self.n) % len(self.banks)]
        self.n += 1
        return bank, self.start + (self.n - 1)


class Chain:

    def __init__(self, eng, sem, start):
        self.eng, self.sem, self.start, self.n = eng, sem, start, 0

    def step(self, instruction):
        self.n += 1
        instruction.then_inc(self.sem, 1)

    def wait(self):
        wait_past(self.eng, self.sem, self.start + self.n)

    def then(self, instruction_of, *args, **kw):
        self.wait()
        self.step(instruction_of(*args, **kw))


def f32(ap):
    return ap.bitcast(F32)


def across(ap, n):
    return ap.unsqueeze(2).to_broadcast([P, ap.shape[1], n])


def along(ap, n):
    return ap.unsqueeze(1).to_broadcast([P, n, ap.shape[1]])


def product(pe, out, terms):
    last = None
    for j, (lh, ll, rh, rl) in enumerate(terms):
        pe.matmul(out, lh, rh, start=(j == 0), stop=False)
        pe.matmul(out, lh, rl, start=False, stop=False)
        last = pe.matmul(out, ll, rh, start=False, stop=(j == len(terms) - 1))
    return last


def accumulate(pe, out, terms, stop=False):
    for j, (lh, ll, rh, rl) in enumerate(terms):
        pe.matmul(out, lh, rh, start=False, stop=False)
        pe.matmul(out, lh, rl, start=False, stop=False)
        last = pe.matmul(out, ll, rh, start=False, stop=(stop and j == len(terms) - 1))
    return last


def norm_scale(v, chain, stats, scale, shift, tmp):
    even, odd, var, t = stats[:, :, 1], stats[:, :, 4], tmp[:, 0, :], tmp[:, 1, :]
    chain.wait()
    chain.step(v.tensor_tensor(t, even, odd, ALU.subtract))
    chain.step(v.tensor_tensor(shift, even, odd, ALU.add))
    chain.step(v.scalar_tensor_tensor(var, stats[:, :, 2], C * LN_EPS, stats[:, :, 5], ALU.add, ALU.add))
    chain.then(v.scalar_tensor_tensor, t, t, 0.25 * C, t, ALU.mult, ALU.mult)
    chain.then(v.tensor_tensor, var, var, t, ALU.add)
    chain.then(v.tensor_scalar, t.bitcast(I32), var.bitcast(I32), 1, None, ALU.arith_shift_right)
    chain.then(v.tensor_scalar, scale.bitcast(I32), t.bitcast(I32), -1.0, float(RSQRT_MAGIC + (ROOT_BITS << 23)), ALU.mult, ALU.add)
    chain.then(v.scalar_tensor_tensor, t, scale, 1.0 / C, scale, ALU.mult, ALU.mult)
    chain.then(v.tensor_tensor, t, t, var, ALU.mult)
    chain.then(v.scalar_tensor_tensor, t, t, -10.0 / 3.0, t, ALU.add, ALU.mult)
    chain.then(v.tensor_scalar, t, t, 0.375, 1.875, ALU.mult, ALU.add)
    chain.then(v.tensor_tensor, scale, t, scale, ALU.mult)
    chain.then(v.scalar_tensor_tensor, t, scale, -0.5 / C, scale, ALU.mult, ALU.mult)
    chain.then(v.tensor_tensor, t, t, var, ALU.mult)
    chain.then(v.scalar_tensor_tensor, scale, t, 1.5, scale, ALU.add, ALU.mult)
    chain.then(v.scalar_tensor_tensor, shift, shift, -0.5, scale, ALU.mult, ALU.mult)


NORM_STEPS = 16


def top_two(v, chain, first, second, values, falling, largest, m, key):
    n = values.shape[1]
    for out, of, value in ((first, values, largest[0]), (second, key[1], largest[1])):
        if out is second:
            chain.then(v.scalar_tensor_tensor, key[1], first, LOWEST, values, ALU.mult, ALU.add)
        chain.then(v.tensor_reduce, value, of, AX.X, ALU.max)
        chain.then(v.tensor_tensor, key[0], of, across(value, EXPERTS), ALU.is_equal)
        chain.then(v.tensor_tensor, key[0], key[0], along(falling, n), ALU.mult)
        chain.then(v.tensor_reduce, m, key[0], AX.X, ALU.max)
        chain.then(v.tensor_tensor, out, key[0], across(m, EXPERTS), ALU.is_equal)


TOP_STEPS = 11


def stage_a(nc, d):
    NDT = 2
    BESIDE_V = P // HEAD
    WIDE = P + BESIDE_V
    NEXT, LATE = ("kv", "vk", "q", "split"), ("ln", "norm", "x1T", "logit", "logitT", "slots", "copy")
    ORDER = [("nd", 0), ("ln", 0), ("nd", 1), ("kv", 0), ("kv", 1), ("norm", 0), ("kv", 2), ("kv", 3), ("nd", 2), ("norm", 1), ("mixT", 0),
             ("kv", 4), ("x1T", 0), ("kv", 5), ("x1T", 1), ("proj", 0), ("kv", 6), ("kv", 7), ("nd", 3), ("logit", 0), ("logit", 1),
             ("proj", 1), ("logitT", 0), ("vk", 0), ("vk", 1), ("q", 0), ("q", 1), ("mixT", 1), ("q", 2), ("slots", 0), ("q", 3),
             ("split", 0), ("copy", 0), ("proj", 2), ("proj", 3)]
    PIECES = 4
    START = [unit for unit in ORDER if unit[0] in NEXT]
    COUNT = {"kv": 1, "nd": NDT, "mixT": 2, "proj": 1, "vk": 1, "q": 1, "x1T": 2, "logit": 1, "logitT": 1, "slots": 3}

    def fills(units):
        return sum(COUNT.get(kind, 0) for kind, _ in units)

    PROLOGUE, EACH = fills(START), fills(ORDER)
    FIRST = EACH - sum(COUNT.get(kind, 0) for kind, _ in ORDER if kind in LATE)
    assert EACH % BANKS == 0
    CONSTS = 26
    ROUTE_STEPS = 4 + TOP_STEPS + 2
    SLOT_STEPS = 9

    def order(i):
        if not isinstance(i, int):
            return ORDER
        if i < 0:
            return START
        if i == BATCHES:
            return [unit for unit in ORDER if unit[0] in LATE]
        return [unit for unit in ORDER if not (i == 0 and unit[0] in LATE) and not (i == BATCHES - 1 and unit[0] in NEXT)]

    def number(i, unit):
        units = order(i)
        at = fills(units[:units.index(unit)])
        if isinstance(i, int) and i < 0:
            return at
        if isinstance(i, int) and i == 0:
            return PROLOGUE + at
        if isinstance(i, int) and i == BATCHES:
            return FIRST + (BATCHES - 1) * EACH + at
        return PROLOGUE + FIRST + (i - 1) * EACH + at

    def bank_of(i, unit, g=0):
        if isinstance(i, int):
            return (number(i, unit) + g) % BANKS
        return (PROLOGUE + FIRST + fills(ORDER[:ORDER.index(unit)]) + g) % BANKS

    with ExitStack() as ctx:
        def sb(name, shape, dt=F32):
            return ctx.enter_context(nc.sbuf_tensor("a_" + name, shape, dt))

        def pair(name, shape):
            return sb(name + "_hi", shape, F32R), sb(name + "_lo", shape, F32R)

        def sem(name):
            return ctx.enter_context(nc.semaphore("a_" + name))

        ps = ctx.enter_context(nc.psum_tensor("a_ps", [P, BANKS, 512], F32))

        wkv_raw, wq_raw, wp_raw, wr_raw = (sb(n, [P, CH, w]) for n, w in (("wkv_raw", 2 * C), ("wq_raw", C), ("wp_raw", C), ("wr_raw", EXPERTS)))
        wkv_hi, wkv_lo = pair("wkv", [P, CH, 2 * C])
        wq_hi, wq_lo = pair("wq", [P, CH, C])
        wp_hi, wp_lo = pair("wp", [P, CH, C])
        wr_hi, wr_lo = pair("wr", [P, CH, EXPERTS])
        bias_p, bias_r = sb("bias_p", [P, C]), sb("bias_r", [P, EXPERTS])
        zeros = sb("zeros", [P, 2 * SEQ])
        ident = sb("ident", [P, P])
        same_head = sb("same_head", [P, WIDE])
        ones_f = sb("ones_f", [P, TILES * CH * BESIDE_V])
        before, ones = sb("before", [P, P], BF16), sb("ones", [P, P], BF16)
        falling, real, slot0 = sb("falling", [P, EXPERTS]), sb("real", [P, EXPERTS]), sb("slot0", [P, EXPERTS])
        xT_raw = sb("xT_raw", [P, CH, SEQ])
        xT_hi, xT_lo = pair("xT", [P, CH, SEQ])
        x_rows = sb("x_rows", [P, TILES, C])
        kv_hi, kv_lo = sb("kv_hi", [P, TILES, 4, WIDE], F32R), sb("kv_lo", [P, TILES, 4, P], F32R)
        vk_m = sb("vk_m", [P, CH, WIDE])
        vk_hi, vk_lo = pair("vk", [P, CH, WIDE])
        q_hi, q_lo = pair("q", [P, CH, SEQ])
        den, rden = sb("den", [P, NDT, CH, BESIDE_V]), sb("rden", [P, NDT, CH, BESIDE_V])
        mix = sb("mix", [P, TILES, C])
        mix_hi, mix_lo = pair("mix", [P, CH, SEQ])
        rows, x1, x1_copy = sb("rows", [P, TILES, C]), sb("x1", [P, TILES, C]), sb("x1_copy", [P, TILES, C])
        x1T_hi, x1T_lo = pair("x1T", [P, CH, SEQ])
        stats, scale, shift, tmp = sb("stats", [P, TILES, 6]), sb("scale", [P, TILES]), sb("shift", [P, TILES]), sb("tmp", [P, 2, TILES])
        logit_e, freed = sb("logit_e", [EXPERTS, SEQ]), sb("freed", [1, 2])
        logit, expd, weight = (sb(n, [P, TILES, EXPERTS]) for n in ("logit", "expd", "weight"))
        first, second = sb("first", [P, TILES, EXPERTS]), sb("second", [P, TILES, EXPERTS])
        key0, key1 = sb("key0", [P, TILES, EXPERTS]), sb("key1", [P, TILES, EXPERTS])
        row_m, row_s = sb("row_m", [P, TILES]), sb("row_s", [P, TILES])
        mask = sb("mask", [P, TILES, EXPERTS], BF16)
        tile_sum, carry = sb("tile_sum", [P, EXPERTS]), sb("carry", [P, EXPERTS])
        carry_b = sb("carry_b", [P, EXPERTS], BF16)
        slot, room = sb("slot", [P, TILES, EXPERTS]), sb("room", [P, TILES, EXPERTS])
        picked = sb("picked", [P, 2, TILES])
        slots = sb("slots", [P, 2, TILES], U32)
        gates = sb("gates", [P, 3, TILES])

        wkv_in, weights_in, consts = sem("wkv_in"), sem("weights_in"), sem("consts")
        xT_in, x_in = sem("xT_in"), sem("x_in")
        zero_filled = sem("zero_filled")
        weights_hi, weights_split = sem("weights_hi"), sem("weights_split")
        xT_hi_done, xT_split = sem("xT_hi_done"), sem("xT_split")
        bank_full, bank_free = sem("bank_full"), sem("bank_free")
        hi_done, vk_hi_done, vk_split = sem("hi_done"), sem("vk_hi_done"), sem("vk_split")
        den_chain, stats_done = sem("den_chain"), sem("stats_done")
        x_biased, x1_done, x1_stored, x1_copied = sem("x_biased"), sem("x1_done"), sem("x1_stored"), sem("x1_copied")
        logit_copied, logit_done, exp_done = sem("logit_copied"), sem("logit_done"), sem("exp_done")
        ln_chain, route_chain, slot_chain = sem("ln_chain"), sem("route_chain"), sem("slot_chain")
        mask_done, slots_done, slots_stored, scattered = sem("mask_done"), sem("slots_done"), sem("slots_stored"), sem("scattered")

        HI_KINDS = ("kv", "q", "mixT", "x1T")

        def hi_halves(units):
            return sum(COUNT[kind] for kind, _ in units if kind in HI_KINDS)

        def hi_before(i):
            if isinstance(i, int):
                return sum(hi_halves(order(k)) for k in range(-1, i))
            return hi_halves(order(-1)) + hi_halves(order(0)) + (i - 1) * hi_halves(ORDER)

        block = ctx.enter_context(nc.Block())

        @block.sync
        def _(sp):
            def load_xT(i):
                wait_past(sp, xT_split, PIECES * i)
                sp.dma_start(xT_raw[:], d["xT"][:, bass.ds(i * SEQ, SEQ)].rearrange("(a p) n -> p a n", p=P)).then_inc(xT_in, 16)

            def load_x(i):
                if not (isinstance(i, int) and i == 0):
                    sp.wait_ge(bank_free, number(i - 1, ("proj", 3)) + 1)
                sp.dma_start(x_rows[:], d["x"][bass.ds(i * SEQ, SEQ), :].rearrange("(t p) c -> p t c", p=P)).then_inc(x_in, 16)

            def store(i):
                sp.wait_ge(x1_done, 2 * i + 2)
                sp.dma_start(d["x1"][bass.ds(i * SEQ, SEQ), :].rearrange("(t p) c -> p t c", p=P), x1[:]).then_inc(x1_stored, 16)

            def store_slots(i):
                sp.wait_ge(slots_done, i + 1)
                sp.dma_start(d["slots"][bass.ds(i * P, P), :], slots[:].rearrange("p a t -> p (a t)")).then_inc(slots_stored, 16)
                sp.dma_start(d["gates"][bass.ds(i * P, P), :], gates[:].rearrange("p a t -> p (a t)")).then_inc(slots_stored, 16)

            sp.dma_start(wkv_raw[:], d["wkvT"].rearrange("(a p) n -> p a n", p=P)).then_inc(wkv_in, 16)
            load_xT(0)
            for raw, w in ((wq_raw, "wqT"), (wp_raw, "projT"), (wr_raw, "routerT")):
                sp.dma_start(raw[:], d[w].rearrange("(a p) n -> p a n", p=P)).then_inc(weights_in, 16)
            sp.dma_start(bias_p[:], d["proj_bias"].partition_broadcast(P)).then_inc(weights_in, 16)
            sp.dma_start(bias_r[:], d["router_b"].partition_broadcast(P)).then_inc(weights_in, 16)
            load_x(0)
            load_xT(1)
            load_xT(2)
            load_x(1)
            with sp.Fori(1, BATCHES - 2) as i:
                load_xT(i + 2)
                store(i - 1)
                store_slots(i - 1)
                load_x(i + 1)
            store(BATCHES - 3)
            store_slots(BATCHES - 3)
            load_x(BATCHES - 1)
            for i in (BATCHES - 2, BATCHES - 1):
                store(i)
                store_slots(i)
            sp.wait_ge(x1_stored, 16 * BATCHES)
            sp.wait_ge(slots_stored, 32 * BATCHES)

        @block.gpsimd
        def _(pool):
            def const(instruction):
                instruction.then_inc(consts, 1)

            const(pool.memset(zeros[:], 0.0))
            const(pool.memset(ident[:], 0.0))
            const(pool.memset(ones_f[:], 1.0))
            const(pool.memset(same_head[:], 1.0))
            const(pool.memset(before[:], 1.0))
            const(pool.memset(ones[:], 1.0))
            const(pool.memset(real[:], 1.0))
            const(pool.memset(carry[:], 0.0))
            const(pool.memset(carry_b[:], 0.0))
            for e in range(EXPERTS):
                const(pool.memset(falling[:, e:e + 1], float(EXPERTS - e)))
            pool.wait_ge(consts, 9 + EXPERTS)
            const(pool.affine_select(out=ident[:], in_=ident[:], compare_op=ALU.not_equal, fill=1.0,
                                     base=0, pattern=[[-1, P]], channel_multiplier=1))
            const(pool.affine_select(out=before[:], in_=before[:], compare_op=ALU.is_ge, fill=0.0,
                                     base=-1, pattern=[[1, P]], channel_multiplier=-1))
            heads, sums = same_head[:, 0:P].rearrange("p (h e) -> p h e", e=HEAD), same_head[:, P:WIDE]
            const(pool.affine_select(out=heads, in_=heads, compare_op=ALU.is_ge, fill=0.0, base=0,
                                     pattern=[[-HEAD, P // HEAD], [0, HEAD]], channel_multiplier=1))
            const(pool.affine_select(out=sums, in_=sums, compare_op=ALU.is_ge, fill=0.0, base=0,
                                     pattern=[[-HEAD, P // HEAD]], channel_multiplier=1))
            pool.wait_ge(consts, 9 + EXPERTS + 4)
            const(pool.affine_select(out=heads, in_=heads, compare_op=ALU.is_ge, fill=0.0, base=HEAD - 1,
                                     pattern=[[HEAD, P // HEAD], [0, HEAD]], channel_multiplier=-1))
            const(pool.affine_select(out=sums, in_=sums, compare_op=ALU.is_ge, fill=0.0, base=HEAD - 1,
                                     pattern=[[HEAD, P // HEAD]], channel_multiplier=-1))
            const(pool.memset(real[:, REAL:EXPERTS], 0.0))
            const(pool.iota(slots[:].rearrange("p a t -> p (a t)").bitcast(I32)[:, 0:EXPERTS], pattern=[[CAP, EXPERTS]], base=-TRASH, channel_multiplier=0))
            pool.wait_ge(consts, 9 + EXPERTS + 8)
            const(pool.tensor_copy(slot0[:], slots[:].rearrange("p a t -> p (a t)").bitcast(I32)[:, 0:EXPERTS]))

            def split_xT(i):
                for j in range(PIECES):
                    at = (slice(None), slice(None), bass.ts(j, SEQ // PIECES))
                    pool.wait_ge(xT_hi_done, PIECES * i + j + 1)
                    pool.tensor_tensor(xT_lo[at], xT_raw[at], f32(xT_hi[at]), ALU.subtract).then_inc(xT_split, 1)

            def bias(i):
                pool.wait_ge(x_in, 16 * i + 16)
                if isinstance(i, int) and i == 0:
                    pool.wait_ge(weights_in, 16 * 5)
                pool.tensor_tensor(x_rows[:], x_rows[:], bias_p[:].unsqueeze(1).to_broadcast([P, TILES, C]), ALU.add).then_inc(x_biased, 1)

            ZERO_FILLS = REAL * CAP * C // (P * 2 * SEQ) + 1

            def fill_zeros():
                for part in range(ZERO_FILLS - 1):
                    pool.dma_start(d["xs"].rearrange("(a p r) c -> a p (r c)", p=P, r=2 * SEQ // C)[part, :, :], zeros[:]).then_inc(zero_filled, 16)
                pool.dma_start(d["ys"][TRASH:TRASH + P, :], zeros[:, 0:C]).then_inc(zero_filled, 16)

            def scatter(i):
                pool.wait_ge(zero_filled, 16 * ZERO_FILLS)
                pool.wait_ge(x1_copied, i + 1)
                pool.wait_ge(slots_done, i + 1)
                for t in range(TILES):
                    for a in range(2):
                        pool.indirect_dma_start(d["xs"], bass.IndirectOffsetOnAxis(ap=slots[:, a, t:t + 1], axis=0),
                                                x1_copy[:, t, :], None, bounds_check=TRASH - 1, oob_is_err=False).then_inc(scattered, 16)

            split_xT(0)
            bias(0)
            split_xT(1)
            fill_zeros()
            split_xT(2)
            bias(1)
            with pool.Fori(1, BATCHES - 2) as i:
                split_xT(i + 2)
                bias(i + 1)
                scatter(i - 1)
            bias(BATCHES - 1)
            for i in range(BATCHES - 3, BATCHES):
                scatter(i)
            pool.wait_ge(scattered, 32 * TILES * BATCHES)

        @block.scalar
        def _(act):
            def split_xT(i):
                act.wait_ge(xT_in, 16 * i + 16)
                for j in range(PIECES):
                    at = (slice(None), slice(None), bass.ts(j, SEQ // PIECES))
                    act.activation(xT_hi[at], xT_raw[at], ACT.Copy).then_inc(xT_hi_done, 1)

            def body(i):
                def copy_hi(unit, g, out, func):
                    act.wait_ge(bank_full, number(i, unit) + g + 1)
                    return act.activation(out, ps[:, bank_of(i, unit, g), :], func).then_inc(hi_done, 1)

                for unit in order(i):
                    kind, j = unit
                    if kind == "kv":
                        act.wait_ge(bank_full, number(i, unit) + 1)
                        act.activation(kv_hi[:, j, :, 0:P], ps[:, bank_of(i, unit), :].rearrange("p (b n) -> p b n", n=P), ACT.Relu).then_inc(hi_done, 1)
                    elif kind == "q":
                        copy_hi(unit, 0, q_hi[:, j % CH, bass.ts(j // CH, HALF)], ACT.Relu)
                    elif kind == "vk":
                        act.wait_ge(bank_free, number(i, unit) + 1)
                        act.activation(vk_hi[:, j, :], vk_m[:, j, :], ACT.Copy).then_inc(vk_hi_done, 1)
                    elif kind == "mixT":
                        for p in range(CH):
                            copy_hi(unit, p, mix_hi[:, p, bass.ts(j, HALF)], ACT.Copy)
                    elif kind == "norm":
                        act.wait_ge(ln_chain, i * NORM_STEPS)
                        if not (isinstance(i, int) and i == 1):
                            act.wait_ge(x1_copied, i - 1)
                            act.wait_ge(x1_stored, 16 * (i - 1))
                        for t in range(HTILES * j, HTILES * (j + 1)):
                            last = act.activation(x1[:, t, :], rows[:, t, :], ACT.Identity, scale=scale[:, t:t + 1], bias=shift[:, t:t + 1])
                        last.then_inc(x1_done, 1)
                    elif kind == "split":
                        if isinstance(i, int):
                            if i + 2 < BATCHES:
                                split_xT(i + 2)
                        else:
                            split_xT(i + 2)
                    elif kind == "x1T":
                        for c in range(CH):
                            copy_hi(unit, c, x1T_hi[:, c, bass.ts(j, HALF)], ACT.Copy)
                    elif kind == "logit":
                        act.wait_ge(bank_full, number(i, unit) + 1)
                        act.activation(logit_e[:, bass.ts(j, HALF)], ps[0:EXPERTS, bank_of(i, unit), :], ACT.Copy).then_inc(logit_copied, 1)
                    elif kind == "logitT":
                        act.wait_ge(logit_done, i)
                        act.activation(expd[:], logit[:], ACT.Exp).then_inc(exp_done, 1)
                    elif kind == "copy":
                        if not (isinstance(i, int) and i == 1):
                            act.wait_ge(scattered, 32 * TILES * (i - 1))
                        act.wait_ge(x1_done, 2 * i)
                        act.activation(x1_copy[:], x1[:], ACT.Copy).then_inc(x1_copied, 1)

            act.wait_ge(wkv_in, 16)
            act.activation(wkv_hi[:], wkv_raw[:], ACT.Copy).then_inc(weights_hi, 1)
            split_xT(0)
            act.wait_ge(weights_in, 16 * 5)
            for hi, raw in ((wq_hi, wq_raw), (wp_hi, wp_raw), (wr_hi, wr_raw)):
                act.activation(hi[:], raw[:], ACT.Copy).then_inc(weights_hi, 1)
            act.wait_ge(consts, CONSTS)
            act.activation(kv_hi[:, :, 2:4, P:WIDE], ones_f[:].rearrange("p (t a h) -> p t a h", t=TILES, a=CH), ACT.Copy).then_inc(weights_hi, 1)
            body(-1)
            body(0)
            with act.Fori(1, BATCHES - 2) as i:
                body(i)
            body(BATCHES - 2)
            body(BATCHES - 1)
            body(BATCHES)

        @block.vector
        def _(v):
            for j, (lo, raw, hi) in enumerate(((wkv_lo, wkv_raw, wkv_hi), (wq_lo, wq_raw, wq_hi), (wp_lo, wp_raw, wp_hi), (wr_lo, wr_raw, wr_hi))):
                v.wait_ge(weights_hi, j + 1)
                v.tensor_tensor(lo[:], raw[:], f32(hi[:]), ALU.subtract).then_inc(weights_split, 1)
            v.wait_ge(consts, CONSTS)

            def route(i, bank, n):
                v.wait_ge(bank_full, n + 1)
                v.tensor_tensor(logit[:], bank[:, 0:TILES * EXPERTS].rearrange("p (t e) -> p t e", e=EXPERTS), along(bias_r[:], TILES), ALU.add).then_inc(bank_free, 1)
                chain = Chain(v, route_chain, i * ROUTE_STEPS)
                v.wait_ge(bank_free, n + 1)
                chain.step(v.tensor_reduce(row_m[:], logit[:], AX.X, ALU.max))
                chain.wait()
                v.tensor_tensor(logit[:], logit[:], across(row_m[:], EXPERTS), ALU.subtract).then_inc(logit_done, 1)
                v.wait_ge(exp_done, i + 1)
                chain.step(v.tensor_reduce(row_s[:], expd[:], AX.X, ALU.add))
                chain.then(v.reciprocal, row_s[:], row_s[:])
                chain.then(v.tensor_tensor, weight[:], expd[:], across(row_s[:], EXPERTS), ALU.mult)
                if not (isinstance(i, int) and i == 0):
                    v.wait_ge(slots_stored, 32 * i)
                top_two(v, chain, first[:], second[:], weight[:], falling[:], (gates[:, 0, :], gates[:, 1, :]), row_m[:], (key0[:], key1[:]))
                chain.then(v.scalar_tensor_tensor, second[:], weight[:], 0.0, second[:], ALU.is_gt, ALU.mult)
                chain.wait()
                v.tensor_tensor(mask[:], first[:], second[:], ALU.add).then_inc(mask_done, 1)
                v.wait_ge(mask_done, i + 1)
                chain.step(v.tensor_tensor(gates[:, 2, :], mask[:, :, REAL], weight[:, :, REAL], ALU.mult))
                assert chain.n == ROUTE_STEPS, chain.n

            def find_slots(i, bank, n):
                chain = Chain(v, slot_chain, i * SLOT_STEPS)
                v.wait_ge(bank_full, n + 1)
                if not (isinstance(i, int) and i == 0):
                    v.wait_ge(scattered, 32 * TILES * i)
                position = bank[:, 0:TILES * EXPERTS].rearrange("p (t e) -> p t e", e=EXPERTS)
                chain.step(v.scalar_tensor_tensor(room[:], position, float(CAP), along(real[:], TILES), ALU.is_lt, ALU.mult))
                v.tensor_tensor(slot[:], position, along(slot0[:], TILES), ALU.add).then_inc(bank_free, COUNT["slots"])
                v.wait_ge(bank_free, n + COUNT["slots"])
                chain.then(v.tensor_tensor, slot[:], slot[:], room[:], ALU.mult)
                for a, chosen in ((0, first), (1, second)):
                    chain.then(v.tensor_tensor, room[:], slot[:], chosen[:], ALU.mult)
                    chain.then(v.tensor_reduce, picked[:, a, :], room[:], AX.X, ALU.add)
                chain.then(v.tensor_reduce, tile_sum[:], mask[:].rearrange("p t e -> p e t"), AX.X, ALU.add)
                chain.then(v.tensor_tensor, carry[:], carry[:], tile_sum[:], ALU.add)
                chain.then(v.tensor_copy, carry_b[:], carry[:])
                assert chain.n == SLOT_STEPS, chain.n
                chain.wait()
                v.tensor_scalar(slots[:], picked[:], float(TRASH), None, ALU.add).then_inc(slots_done, 1)

            def body(i):
                hi_n = [hi_before(i)]

                def split_lo(unit, g, hi, lo, relu=False):
                    hi_n[0] = hi_n[0] + 1
                    v.wait_ge(hi_done, hi_n[0])
                    bank = ps[:, bank_of(i, unit, g), :]
                    if relu:
                        v.scalar_tensor_tensor(lo, bank.rearrange("p (b n) -> p b n", n=P) if len(lo.shape) == 3 else bank, 0.0, f32(hi), ALU.max, ALU.subtract).then_inc(bank_free, 1)
                    else:
                        v.tensor_tensor(lo, bank, f32(hi), ALU.subtract).then_inc(bank_free, 1)

                for unit in order(i):
                    kind, j = unit
                    n = number(i, unit)
                    if kind == "kv":
                        split_lo(unit, 0, kv_hi[:, j, :, 0:P], kv_lo[:, j, :, :], True)
                    elif kind == "q":
                        at = (slice(None), j % CH, bass.ts(j // CH, HALF))
                        split_lo(unit, 0, q_hi[at], q_lo[at], True)
                        if j == 0:
                            for p in range(CH):
                                v.wait_ge(vk_hi_done, CH * (i + 1) + p + 1)
                                v.tensor_tensor(vk_lo[:, p, :], vk_m[:, p, :], f32(vk_hi[:, p, :]), ALU.subtract).then_inc(vk_split, 1)
                    elif kind == "vk":
                        v.wait_ge(bank_full, n + 1)
                        v.tensor_tensor(vk_m[:, j, :], ps[:, bank_of(i, unit), 0:WIDE], same_head[:], ALU.mult).then_inc(bank_free, 1)
                    elif kind == "nd":
                        before_nd = 2 * TILES * i + 2 * NDT * j
                        bank = bank_of(i, unit)
                        parts = [(0, NDT)] if bank + NDT <= BANKS else [(g, g + 1) for g in range(NDT)]
                        v.wait_ge(bank_full, n + NDT)
                        if j:
                            v.wait_ge(bank_free, number(i, ("nd", j - 1)) + NDT)
                        for g, end in parts:
                            sums = ps[:, (bank + g) % BANKS:(bank + g) % BANKS + end - g, 0:CH * WIDE].rearrange("p t (a n) -> p t a n", n=WIDE)[:, :, :, P:WIDE]
                            v.tensor_scalar(den[:, g:end], sums, ATTN_EPS, None, ALU.add).then_inc(den_chain, end - g)
                        v.wait_ge(den_chain, before_nd + NDT)
                        v.reciprocal(rden[:], den[:]).then_inc(den_chain, NDT)
                        v.wait_ge(den_chain, before_nd + 2 * NDT)
                        for g in range(NDT):
                            both = ps[:, bank_of(i, unit, g), 0:CH * WIDE].rearrange("p (a n) -> p a n", n=WIDE)[:, :, 0:P]
                            v.tensor_tensor(mix[:, NDT * j + g, :].rearrange("p (a h e) -> p a h e", a=CH, e=HEAD), both.rearrange("p a (h e) -> p a h e", e=HEAD),
                                            rden[:, g].unsqueeze(3).to_broadcast([P, CH, BESIDE_V, HEAD]), ALU.mult).then_inc(bank_free, 1)
                    elif kind == "mixT":
                        for p in range(CH):
                            at = (slice(None), p, bass.ts(j, HALF))
                            split_lo(unit, p, mix_hi[at], mix_lo[at])
                    elif kind == "proj":
                        two = slice(2 * j, 2 * j + 2)
                        v.wait_ge(bank_full, n + 1)
                        if j == 0:
                            v.wait_ge(x_biased, i + 1)
                            if not (isinstance(i, int) and i == 0):
                                v.wait_ge(x1_done, 2 * i)
                        v.tensor_tensor(rows[:, two, :], ps[:, bank_of(i, unit), :].rearrange("p (t c) -> p t c", c=C), x_rows[:, two, :], ALU.add).then_inc(bank_free, 1)
                        v.wait_ge(bank_free, n + 1)
                        for t in (2 * j, 2 * j + 1):
                            v.bn_stats(stats[:, t, :], rows[:, t, :]).then_inc(stats_done, 1)
                    elif kind == "ln":
                        chain = Chain(v, ln_chain, (i - 1) * NORM_STEPS)
                        v.wait_ge(stats_done, TILES * i)
                        norm_scale(v, chain, stats[:], scale[:], shift[:], tmp[:])
                        assert chain.n == NORM_STEPS, chain.n
                    elif kind == "x1T":
                        for c in range(CH):
                            at = (slice(None), c, bass.ts(j, HALF))
                            split_lo(unit, c, x1T_hi[at], x1T_lo[at])
                    elif kind == "logit":
                        v.wait_ge(logit_copied, 2 * (i - 1) + j + 1)
                        v.memset(freed[:, j:j + 1], 0.0).then_inc(bank_free, 1)
                    elif kind == "logitT":
                        route(i - 1, ps[:, bank_of(i, unit), :], n)
                    elif kind == "slots":
                        find_slots(i - 1, ps[:, bank_of(i, unit), :], n)

            body(-1)
            body(0)
            with v.Fori(1, BATCHES - 2) as i:
                body(i)
            body(BATCHES - 2)
            body(BATCHES - 1)
            body(BATCHES)

        @block.tensor
        def _(pe):
            def body(i):
                def opened(unit, g=0):
                    wait_past(pe, bank_free, number(i, unit) + g + 1 - BANKS)
                    return ps[:, bank_of(i, unit, g), :]

                for unit in order(i):
                    kind, j = unit
                    if kind == "kv":
                        if j % (TILES // PIECES) == 0:
                            pe.wait_ge(xT_split, PIECES * (i + 1) + j * PIECES // TILES + 1)
                        product(pe, opened(unit), [(xT_hi[:, c, bass.ts(j, P)], xT_lo[:, c, bass.ts(j, P)], wkv_hi[:, c, :], wkv_lo[:, c, :])
                                                   for c in range(CH)]).then_inc(bank_full, 1)
                    elif kind == "vk":
                        if j == 0:
                            if isinstance(i, int) and i < 0:
                                pe.wait_ge(weights_split, 4)
                                pe.wait_ge(weights_hi, 5)
                            pe.wait_ge(bank_free, number(i, ("kv", TILES - 1)) + 1)
                        out = opened(unit)
                        for t in range(TILES):
                            v_ones = kv_hi[:, t, 2 + j, :]
                            pe.matmul(out[:, 0:WIDE], kv_hi[:, t, j, 0:P], v_ones, start=(t == 0), stop=False)
                            pe.matmul(out[:, 0:P], kv_hi[:, t, j, 0:P], kv_lo[:, t, 2 + j, :], start=False, stop=False)
                            last = pe.matmul(out[:, 0:WIDE], kv_lo[:, t, j, :], v_ones, start=False, stop=(t == TILES - 1))
                        last.then_inc(bank_full, 1)
                    elif kind == "q":
                        h, p = j // CH, j % CH
                        product(pe, opened(unit), [(wq_hi[:, c, bass.ts(p, P)], wq_lo[:, c, bass.ts(p, P)], xT_hi[:, c, bass.ts(h, HALF)], xT_lo[:, c, bass.ts(h, HALF)])
                                                   for c in range(CH)]).then_inc(bank_full, 1)
                    elif kind == "nd":
                        if j == 0:
                            pe.wait_ge(bank_free, number(i - 1, ("q", 3)) + 1)
                            pe.wait_ge(vk_split, CH * i + CH)
                        for g in range(NDT):
                            t, out = NDT * j + g, opened(unit, g)
                            for p in range(CH):
                                last = product(pe, out[:, bass.ts(p, WIDE)], [(q_hi[:, p, bass.ts(t, P)], q_lo[:, p, bass.ts(t, P)], vk_hi[:, p, :], vk_lo[:, p, :])])
                            last.then_inc(bank_full, 1)
                    elif kind == "mixT":
                        pe.wait_ge(bank_free, number(i, ("nd", HTILES // NDT * (j + 1) - 1)) + NDT)
                        for p in range(CH):
                            out = opened(unit, p)
                            for t in range(HTILES):
                                last = pe.transpose(out[:, bass.ts(t, P)], mix[:, HTILES * j + t, bass.ts(p, P)], ident[:])
                            last.then_inc(bank_full, 1)
                    elif kind == "proj":
                        pe.wait_ge(bank_free, number(i, ("mixT", j // 2)) + CH)
                        out = opened(unit)
                        for t in (2 * j, 2 * j + 1):
                            last = product(pe, out[:, bass.ts(t % 2, C)],
                                           [(mix_hi[:, p, bass.ts(t, P)], mix_lo[:, p, bass.ts(t, P)], wp_hi[:, p, :], wp_lo[:, p, :]) for p in range(CH)])
                        last.then_inc(bank_full, 1)
                    elif kind == "x1T":
                        pe.wait_ge(x1_done, 2 * (i - 1) + j + 1)
                        for c in range(CH):
                            out = opened(unit, c)
                            for t in range(HTILES):
                                last = pe.transpose(out[:, bass.ts(t, P)], x1[:, HTILES * j + t, bass.ts(c, P)], ident[:])
                            last.then_inc(bank_full, 1)
                    elif kind == "logit":
                        if j == 0:
                            pe.wait_ge(bank_free, number(i, ("x1T", 1)) + CH)
                        product(pe, opened(unit)[0:EXPERTS, :], [(wr_hi[:, c, :], wr_lo[:, c, :], x1T_hi[:, c, bass.ts(j, HALF)], x1T_lo[:, c, bass.ts(j, HALF)])
                                                                 for c in range(CH)]).then_inc(bank_full, 1)
                    elif kind == "logitT":
                        logit_there = number(i, ("logit", 1)) + 1
                        if not isinstance(logit_there, int):
                            pe.to_reg(logit_there)
                        pe.wait_ge(weights_hi, 5)
                        pe.wait_ge(bank_free, logit_there)
                        out = ps[:, bank_of(i, unit), :]
                        for t in range(TILES):
                            last = pe.transpose(out[:, bass.ts(t, EXPERTS)], logit_e[:, bass.ts(t, P)], ident[0:EXPERTS, 0:EXPERTS])
                        last.then_inc(bank_full, 1)
                    elif kind == "slots":
                        out = opened(unit)[:, 0:TILES * EXPERTS].rearrange("p (t e) -> p t e", e=EXPERTS)
                        pe.wait_ge(mask_done, i)
                        pe.matmul(out, before[:], mask[:], start=True, stop=False)
                        for t in range(TILES - 1):
                            pe.matmul(out[:, t + 1:, :], ones[:], along(mask[:, t, :], TILES - 1 - t), start=False, stop=False)
                        if not (isinstance(i, int) and i == 1):
                            pe.wait_ge(slots_done, i - 1)
                        pe.matmul(out, ones[:], along(carry_b[:], TILES), start=False, stop=True).then_inc(bank_full, COUNT["slots"])

            pe.wait_ge(weights_split, 1)
            pe.wait_ge(consts, CONSTS)
            body(-1)
            body(0)
            with pe.Fori(1, BATCHES - 2) as i:
                body(i)
            body(BATCHES - 2)
            body(BATCHES - 1)
            body(BATCHES)


def stage_b(nc, d, later):
    EACH = 2 * ICH + HTILES // 2 + 2 * CH + HTILES // 2
    PROLOGUE = 2 * CH
    with ExitStack() as ctx:
        def sb(name, shape, dt=F32):
            return ctx.enter_context(nc.sbuf_tensor("b_" + name, shape, dt))

        def sem(name):
            return ctx.enter_context(nc.semaphore("b_" + name))

        ps = ctx.enter_context(nc.psum_tensor("b_ps", [P, BANKS, 512], F32))
        ident = sb("ident", [P, P])
        xs = sb("xs", [P, TILES, C])
        xsT_hi, xsT_lo = sb("xsT_hi", [P, CH, CAP], F32R), sb("xsT_lo", [P, CH, CAP], F32R)
        win_raw, win_hi, win_lo = sb("win_raw", [P, CH, INTER]), sb("win_hi", [P, CH, INTER], F32R), sb("win_lo", [P, CH, INTER], F32R)
        wout_raw, wout_hi, wout_lo = sb("wout_raw", [P, ICH, C]), sb("wout_hi", [P, ICH, C], F32R), sb("wout_lo", [P, ICH, C], F32R)
        hT_hi, hT_lo = sb("hT_hi", [P, 2, ICH, HALF], F32R), sb("hT_lo", [P, 2, ICH, HALF], F32R)
        results = sb("results", [P, TILES, C])

        ident_done, xs_in, win_in, wout_in = sem("ident_done"), sem("xs_in"), sem("win_in"), sem("wout_in")
        win_hi_done, win_split = sem("win_hi_done"), sem("win_split")
        wout_hi_done, wout_split = sem("wout_hi_done"), sem("wout_split")
        bank_full, bank_free = sem("bank_full"), sem("bank_free")
        later_in = [sem(f"later_in{j}") for j in range(6)]
        later_hi, later_split = sem("later_hi"), sem("later_split")
        xsT_hi_done, hT_hi_done, results_stored = sem("xsT_hi_done"), sem("hT_hi_done"), sem("results_stored")

        PIECE = 1024
        pieces = []
        for w, hi, lo, factor in later:
            blocks = w.rearrange("(k p) n -> p k n" if w.shape[0] == P * hi.shape[1] else "p (k n) -> p k n", k=hi.shape[1])
            each = max(1, min(hi.shape[1], PIECE // hi.shape[2]))
            pieces += [(blocks[:, k:k + each, :], hi[:, k:k + each, :], lo[:, k:k + each, :], factor) for k in range(0, hi.shape[1], each)]
        assert len(pieces) <= 2 * ICH
        places = [whole[:].rearrange("p k n -> p (k n)")[:, bass.ts(j, PIECE)] for whole in (win_raw, xs, wout_raw) for j in range(2)]

        def waiting(k):
            _, hi, _, _ = pieces[k]
            return places[k % len(places)][:, 0:hi.shape[1] * hi.shape[2]].rearrange("p (k n) -> p k n", k=hi.shape[1])

        def group(i, n):
            return PROLOGUE + i * EACH + n

        def turns(i):
            return Turns(group(i, 0), PROLOGUE, range(BANKS))

        OUT_A, ROWS, OUT_B = 2 * ICH, 2 * ICH + HTILES // 2, 2 * ICH + HTILES // 2 + 2 * CH
        block = ctx.enter_context(nc.Block())

        @block.sync
        def _(sp):
            def load_rows(e):
                sp.dma_start(xs[:], d["xs"][bass.ds(e * CAP, CAP), :].rearrange("(t p) c -> p t c", p=P)).then_inc(xs_in, 16)

            def load_in(e):
                sp.dma_start(win_raw[:], d["w_in"][bass.ds(e * C, C), :].rearrange("(a p) n -> p a n", p=P)).then_inc(win_in, 16)

            def load_out(e):
                sp.dma_start(wout_raw[:], d["w_out"][bass.ds(e * INTER, INTER), :].rearrange("(a p) n -> p a n", p=P)).then_inc(wout_in, 16)

            def load_later():
                sp.wait_ge(win_split, REAL)
                sp.wait_ge(bank_full, group(REAL - 2, OUT_B))
                for k, (w, _, _, _) in enumerate(pieces):
                    if k == 4:
                        sp.wait_ge(wout_split, REAL)
                    if k >= len(places):
                        sp.wait_ge(later_split, k - len(places) + 1)
                    sp.dma_start(waiting(k), w).then_inc(later_in[k % len(places)], 16)

            def body(e, end):
                if end:
                    load_later()
                else:
                    sp.wait_ge(bank_full, PROLOGUE if isinstance(e, int) and e == 0 else group(e - 1, OUT_B))
                    load_rows(e + 1)
                    sp.wait_ge(win_split, e + 1)
                    load_in(e + 1)
                    sp.wait_ge(wout_split, e + 1)
                    load_out(e + 1)
                for h, at in ((0, ROWS), (1, EACH)):
                    sp.wait_ge(bank_free, group(e, at) if h == 0 or not end else group(e, EACH - 2 * CH))
                    sp.dma_start(d["ys"][bass.ds(e * CAP + h * HALF, HALF), :].rearrange("(t p) c -> p t c", p=P),
                                 results[:, bass.ts(h, HTILES), :]).then_inc(results_stored, 16)

            load_in(0)
            load_rows(0)
            load_out(0)
            body(0, False)
            with sp.Fori(1, REAL - 1) as e:
                body(e, False)
            body(REAL - 1, True)
            sp.wait_ge(results_stored, 32 * REAL)

        @block.gpsimd
        def _(pool):
            pool.memset(ident[:], 0.0).then_inc(ident_done, 1)
            pool.wait_ge(ident_done, 1)
            pool.affine_select(out=ident[:], in_=ident[:], compare_op=ALU.not_equal, fill=1.0,
                               base=0, pattern=[[-1, P]], channel_multiplier=1).then_inc(ident_done, 1)

        @block.scalar
        def _(act):
            def split_in(e):
                act.wait_ge(win_in, 16 * e + 16)
                act.activation(win_hi[:], win_raw[:], ACT.Copy).then_inc(win_hi_done, 1)

            def split_out(e):
                act.wait_ge(wout_in, 16 * e + 16)
                act.activation(wout_hi[:], wout_raw[:], ACT.Copy).then_inc(wout_hi_done, 1)

            def split_rows(turn):
                for c in range(CH):
                    for h in range(2):
                        bank, n = turn.take()
                        act.wait_ge(bank_full, n + 1)
                        act.activation(xsT_hi[:, c, bass.ts(h, HALF)], ps[:, bank, :], ACT.Copy).then_inc(xsT_hi_done, 1)

            def body(e, end):
                turn = turns(e)
                if not (isinstance(e, int) and e == 0):
                    act.wait_ge(bank_full, group(e - 1, EACH))
                split_out(e)
                for h in range(2):
                    for k in range(ICH):
                        bank, n = turn.take()
                        act.wait_ge(bank_full, n + 1)
                        act.activation(hT_hi[:, h, k, :], ps[:, bank, :], ACT.Relu).then_inc(hT_hi_done, 1)
                        if end and ICH * h + k < len(pieces):
                            m = ICH * h + k
                            _, hi, _, factor = pieces[m]
                            act.wait_ge(later_in[m % len(places)], 16 * (m // len(places)) + 16)
                            act.activation(hi, waiting(m), ACT.Copy, scale=factor).then_inc(later_hi, 1)
                if not end:
                    split_in(e + 1)
                    for _ in range(HTILES // 2):
                        turn.take()
                    split_rows(turn)

            split_in(0)
            split_rows(Turns(0, 0, range(BANKS)))
            body(0, False)
            with act.Fori(1, REAL - 1) as e:
                body(e, False)
            body(REAL - 1, True)

        @block.vector
        def _(v):
            def split_in(e):
                v.wait_ge(win_hi_done, e + 1)
                v.tensor_tensor(win_lo[:], win_raw[:], f32(win_hi[:]), ALU.subtract).then_inc(win_split, 1)

            def split_out(e):
                v.wait_ge(wout_hi_done, e + 1)
                v.tensor_tensor(wout_lo[:], wout_raw[:], f32(wout_hi[:]), ALU.subtract).then_inc(wout_split, 1)

            def split_rows(e, turn):
                for c in range(CH):
                    for h in range(2):
                        bank, n = turn.take()
                        v.wait_ge(xsT_hi_done, 2 * CH * e + 2 * c + h + 1)
                        v.tensor_tensor(xsT_lo[:, c, bass.ts(h, HALF)], ps[:, bank, :], f32(xsT_hi[:, c, bass.ts(h, HALF)]), ALU.subtract).then_inc(bank_free, 1)

            def store_pairs(e, h, turn):
                if not (isinstance(e, int) and e == 0):
                    v.wait_ge(results_stored, 32 * e)
                for j in range(HTILES // 2):
                    bank, n = turn.take()
                    v.wait_ge(bank_full, n + 1)
                    t = HTILES * h + 2 * j
                    v.tensor_copy(results[:, t:t + 2, :], ps[:, bank, :].rearrange("p (t c) -> p t c", c=C)).then_inc(bank_free, 1)

            def body(e, end):
                turn = turns(e)
                split_out(e)
                for h in range(2):
                    for k in range(ICH):
                        bank, n = turn.take()
                        v.wait_ge(hT_hi_done, 2 * ICH * e + ICH * h + k + 1)
                        v.scalar_tensor_tensor(hT_lo[:, h, k, :], ps[:, bank, :], 0.0, f32(hT_hi[:, h, k, :]), ALU.max, ALU.subtract).then_inc(bank_free, 1)
                        if end and ICH * h + k < len(pieces):
                            m = ICH * h + k
                            _, hi, lo, factor = pieces[m]
                            v.wait_ge(later_hi, m + 1)
                            v.scalar_tensor_tensor(lo, waiting(m), factor, f32(hi), ALU.mult, ALU.subtract).then_inc(later_split, 1)
                if not end:
                    split_in(e + 1)
                store_pairs(e, 0, turn)
                if not end:
                    split_rows(e + 1, turn)
                store_pairs(e, 1, turn)

            split_in(0)
            split_rows(0, Turns(0, 0, range(BANKS)))
            body(0, False)
            with v.Fori(1, REAL - 1) as e:
                body(e, False)
            body(REAL - 1, True)

        @block.tensor
        def _(pe):
            def opener(turn):
                def open_bank():
                    bank, n = turn.take()
                    wait_past(pe, bank_free, n + 1 - BANKS)
                    return ps[:, bank, :], n
                return open_bank

            def turn_rows(e, open_bank):
                pe.wait_ge(xs_in, 16 * e + 16)
                for c in range(CH):
                    for h in range(2):
                        out, n = open_bank()
                        for t in range(HTILES):
                            last = pe.transpose(out[:, bass.ts(t, P)], xs[:, HTILES * h + t, bass.ts(c, P)], ident[:])
                        last.then_inc(bank_full, 1)

            def hidden(e, h, open_bank):
                for k in range(ICH):
                    out, n = open_bank()
                    product(pe, out, [(win_hi[:, c, bass.ts(k, P)], win_lo[:, c, bass.ts(k, P)],
                                       xsT_hi[:, c, bass.ts(h, HALF)], xsT_lo[:, c, bass.ts(h, HALF)]) for c in range(CH)]).then_inc(bank_full, 1)
                return n

            def result(h, open_bank):
                for j in range(HTILES // 2):
                    out, n = open_bank()
                    for t in (2 * j, 2 * j + 1):
                        last = product(pe, out[:, bass.ts(t % 2, C)],
                                       [(hT_hi[:, h, k, bass.ts(t, P)], hT_lo[:, h, k, bass.ts(t, P)], wout_hi[:, k, :], wout_lo[:, k, :])
                                        for k in range(ICH)])
                    last.then_inc(bank_full, 1)

            def body(e, end):
                open_bank = opener(turns(e))
                pe.wait_ge(win_split, e + 1)
                pe.wait_ge(bank_free, PROLOGUE if isinstance(e, int) and e == 0 else group(e - 1, OUT_B))
                last_a = hidden(e, 0, open_bank)
                last_b = hidden(e, 1, open_bank)
                pe.wait_ge(wout_split, e + 1)
                pe.wait_ge(bank_free, last_a + 1)
                result(0, open_bank)
                if not end:
                    turn_rows(e + 1, open_bank)
                pe.wait_ge(bank_free, last_b + 1)
                result(1, open_bank)

            pe.wait_ge(ident_done, 2)
            turn_rows(0, opener(Turns(0, 0, range(BANKS))))
            body(0, False)
            with pe.Fori(1, REAL - 1) as e:
                body(e, False)
            body(REAL - 1, True)


def stage_c(nc, d, weights):
    HALVES = 2
    PARTS = 2
    CHUNKS = EXPERTS // PARTS
    ORDER = [("q", 0), ("q", 1), ("q", 2), ("q", 3), ("keep", 0), ("k", 0), ("k", 1), ("k", 2), ("k", 3), ("v", 0), ("v", 1), ("keep", 1),
             ("score", 0), ("v", 2), ("v", 3), ("turn", 0), ("score", 1), ("tail", 0), ("mix", 0), ("combine", 0), ("turn", 1),
             ("score", 2), ("score", 3), ("mix", 1), ("turn", 2), ("combine", 1), ("score", 4), ("mix", 2), ("turn", 3), ("combine", 2),
             ("score", 5), ("mix", 3), ("turn", 4), ("ln3", 0), ("score", 6), ("mix", 4), ("turn", 5), ("combine", 3), ("norm3", 0),
             ("score", 7), ("mix", 5), ("turn", 6), ("x3T", 0), ("combine", 4), ("mix", 6), ("turn", 7), ("gate", 0), ("combine", 5),
             ("gateT", 0), ("mix", 7), ("ln3", 1), ("latent", 0), ("up", (0, 0)), ("scoreT", 0), ("combine", 6), ("norm3", 1),
             ("combine", 7), ("up", (0, 1)), ("ln2", 0), ("x3T", 1), ("expert", (0, 0)), ("gate", 1), ("expert", (0, 1)), ("gateT", 1),
             ("comb", 0), ("up", (1, 0)), ("scoreT", 1), ("out", 0), ("latent", 1), ("up", (1, 1)), ("ln4", 0), ("expert", (1, 0)),
             ("expert", (1, 1)), ("comb", 1), ("x2T", 0), ("x2T", 1), ("out", 1)]

    V_COUNT = {"q": 1, "k": 1, "v": 1, "mix": 1, "turn": 2, "x3T": 2, "gate": 1, "gateT": 1, "scoreT": 1, "latent": 1, "x2T": 2, "comb": 1, "out": 2}
    HI_KINDS = ("q", "k", "v", "turn", "x3T", "latent", "comb", "x2T")
    V_AT, V_BANK, HI_EACH = {}, [], 0
    second_layer = False
    for kind, j in ORDER:
        second_layer = second_layer or kind == "up"
        V_AT[kind, j] = len(V_BANK)
        for g in range(V_COUNT.get(kind, 0)):
            V_BANK.append(6 + g if kind == "out" else 2 * j + g if kind == "x2T" else 4 + len(V_BANK) % (2 if second_layer else 4))
        HI_EACH += V_COUNT[kind] if kind in HI_KINDS else 0
    V_EACH = len(V_BANK)
    PROLOGUE = 2 * V_COUNT["x2T"]
    S_BANKS = 4
    S_COUNT = {"score": 2, "up": CHUNKS, "expert": CHUNKS}
    S_AT, S_EACH = {}, 0
    for unit in ORDER:
        S_AT[unit] = S_EACH
        S_EACH += S_COUNT.get(unit[0], 0)
    HIDDEN = 2 * EXPERTS
    RELU_RING, RING = 2, 4
    GATHER = 2
    PRE_STEPS = TILES + NORM_STEPS
    ROUTE_STEPS = 2 + 8 + 3 + TOP_STEPS + 5
    CONSTS = 3 + EXPERTS

    with ExitStack() as ctx:
        def sb(name, shape, dt=F32):
            return ctx.enter_context(nc.sbuf_tensor("c_" + name, shape, dt))

        def pair(name, shape):
            return sb(name + "_hi", shape, F32R), sb(name + "_lo", shape, F32R)

        def sem(name):
            return ctx.enter_context(nc.semaphore("c_" + name))

        ps = ctx.enter_context(nc.psum_tensor("c_ps", [P, BANKS, 512], F32))
        (wq_hi, wq_lo), (wk_hi, wk_lo), (wv_hi, wv_lo) = weights["wq"], weights["wk"], weights["wv"]
        (gate_hi, gate_lo), (fc1_hi, fc1_lo), (fc2_hi, fc2_lo) = weights["gateT"], weights["fc1T"], weights["fc2T"]
        (w1_hi, w1_lo), (up_hi, up_lo), (down_hi, down_lo) = weights["w1T"], weights["upT"], weights["downT"]
        w2_hi, w2_lo = pair("w2", [P, EXPERTS, LATENT])
        bias_q, bias_k, bias_qs = sb("bias_q", [P, CH]), sb("bias_k", [P, CH]), sb("bias_qs", [P, CH])
        bias_v, bias_corr = sb("bias_v", [P, C]), sb("bias_corr", [P, EXPERTS])
        ident, falling = sb("ident", [P, P]), sb("falling", [P, EXPERTS])
        zeros = sb("zeros", [P, 512], BF16)
        pre, x2, x3 = sb("pre", [P, TILES, C]), sb("x2", [P, TILES, C]), sb("x3", [P, TILES, C])
        x2T = sb("x2T", [P, 2, CH, SEQ], F32R)
        x2T_hi, x2T_lo = x2T[:, 0], x2T[:, 1]
        score_rows = x2T[:].rearrange("p a c s -> p (a c s)").bitcast(F32)
        place = sb("place", [P, 16 * SEQ], F32R)
        q_hi, q_lo, k_hi, k_lo = (place[:, j * CH * SEQ:(j + 1) * CH * SEQ].rearrange("p (c s) -> p c s", c=CH) for j in range(4))
        v_hi, v_lo = (place[:, (8 + 2 * j) * SEQ:(10 + 2 * j) * SEQ].rearrange("p (t c) -> p t c", c=C) for j in range(2))
        probT_hi, probT_lo = (place[:, (12 + j) * SEQ:(13 + j) * SEQ].rearrange("p (t s) -> p t s", s=P) for j in range(2))
        hid_hi, hid_lo = (place[:, 8 * j * SEQ:8 * (j + 1) * SEQ].rearrange("p (k s) -> p k s", s=HALF) for j in range(2))
        shared_place = sb("shared_place", [P, (RELU_RING + RING) * HALF])
        prob = shared_place[:, 0:2 * SEQ].rearrange("p (r s) -> p r s", r=2)
        relu = shared_place[:, 0:RELU_RING * HALF].rearrange("p (r s) -> p r s", s=HALF)
        square = shared_place[:, RELU_RING * HALF:].rearrange("p (r s) -> p r s", s=HALF)
        neg_max, row_sum, row_inv = sb("neg_max", [P, TILES]), sb("row_sum", [P, TILES]), sb("row_inv", [P, TILES])
        x3T_hi, x3T_lo = pair("x3T", [P, CH, HALF])
        lat_hi, lat_lo = pair("lat", [P, HALF])
        comb_hi, comb_lo = pair("comb", [P, HALF])
        logit = sb("logit", [EXPERTS, HALF])
        gathered = sb("gathered", [P, GATHER, 2, C])
        slots, gates = sb("slots", [P, 2, TILES], U32), sb("gates", [P, 3, TILES])
        stats, scale, shift, tmp = sb("stats", [P, TILES, 6]), sb("scale", [P, TILES]), sb("shift", [P, TILES]), sb("tmp", [P, 2, TILES])
        pre_stats, pre_scale, pre_shift = sb("pre_stats", [P, TILES, 6]), sb("pre_scale", [P, TILES]), sb("pre_shift", [P, TILES])
        expd, score, choice = (sb(n, [P, HTILES, EXPERTS]) for n in ("expd", "score", "choice"))
        first, second, key0, key1 = (sb(n, [P, HTILES, EXPERTS]) for n in ("first", "second", "key0", "key1"))
        row_m, row_s = sb("row_m", [P, HTILES]), sb("row_s", [P, HTILES])
        group_m, group_n = sb("group_m", [P, HTILES, GROUPS]), sb("group_n", [P, HTILES, GROUPS])
        score_et, scoreT = sb("score_et", [P, EXPERTS, HTILES]), sb("scoreT", [EXPERTS * HTILES, P])

        consts, biases_in = sem("consts"), sem("biases_in")
        w2_in, w2_hi_done, w2_split = sem("w2_in"), sem("w2_hi_done"), sem("w2_split")
        v_full, v_free = sem("v_full"), sem("v_free")
        s_full, s_free = sem("s_full"), sem("s_free")
        slots_in, gates_in, x1_in = sem("slots_in"), sem("gates_in"), sem("x1_in")
        first_in = [sem(f"first_in{t}") for t in range(TILES)]
        rows_in = [sem(f"rows_in{j}") for j in range(GATHER)]
        combine_chain, combined, factor_done, kept, x2_done, bias_added = sem("combine_chain"), sem("combined"), sem("factor_done"), sem("kept"), sem("x2_done"), sem("bias_added")
        pre_chain, ln_chain, route_chain = sem("pre_chain"), sem("ln_chain"), sem("route_chain")
        stats_done = sem("stats_done")
        hi_done = sem("hi_done")
        max_done, inv_done, x3_done = sem("max_done"), sem("inv_done"), sem("x3_done")
        exp_done, score_done, scores_stored = sem("exp_done"), sem("score_done"), sem("scores_stored")
        scores_in = [sem(f"scores_in{j}") for j in range(EXPERTS // 2)]
        scaled, squared, hid_hi_done, hid_split = sem("scaled"), sem("squared"), sem("hid_hi_done"), sem("hid_split")
        out_done, out_stored = sem("out_done"), sem("out_stored")

        w2_raw = prob[:, 0, :].rearrange("p (k n) -> p k n", k=EXPERTS)

        def is_first(b):
            return isinstance(b, int) and b == 0

        def rows_of(b, t):
            if is_first(b):
                return (x2, x3)[t // HTILES][:].rearrange("p (t a) c -> p t a c", a=2)[:, t % HTILES], first_in[t]
            return gathered[:, t % GATHER], rows_in[t % GATHER]

        def v_number(b, at):
            skipped = sum(V_COUNT["x2T"] for j in range(2) if at > V_AT["x2T", j]) if isinstance(b, int) and b == BATCHES - 1 else 0
            return PROLOGUE + b * V_EACH + at - skipped

        def v_upto(b, unit):
            return v_number(b, V_AT[unit] + V_COUNT[unit[0]] - 1) + 1

        def v_bank(unit, g=0):
            return V_BANK[V_AT[unit] + g]

        def v_open(pe, b, unit, g=0):
            at = V_AT[unit] + g
            skipped = [V_AT["x2T", c] + h for c in range(CH) for h in range(2)] if isinstance(b, int) and b == BATCHES - 1 else []
            before = [a for a in range(at) if V_BANK[a] == V_BANK[at] and a not in skipped]
            if before:
                pe.wait_ge(v_free, v_number(b, before[-1]) + 1)
            elif not is_first(b):
                pe.wait_ge(v_free, v_number(b - 1, max(a for a in range(V_EACH) if V_BANK[a] == V_BANK[at])) + 1)
            return ps[:, V_BANK[at], :]

        def s_upto(b, unit, k):
            return b * S_EACH + S_AT[unit] + k + 1

        def s_bank(unit, k=0):
            return (S_AT[unit] + k) % S_BANKS

        def hidden(b, kind, j, k):
            place = (0 if kind == "up" else EXPERTS) + CHUNKS * j[1] + k
            return HIDDEN * (HALVES * b + j[0]) + place, place

        def order(b):
            return [unit for unit in ORDER
                    if not (isinstance(b, int) and b == BATCHES - 1 and unit[0] in ("keep", "combine", "ln2", "x2T"))
                    and not (is_first(b) and unit[0] == "tail")]

        block = ctx.enter_context(nc.Block())

        @block.sync
        def _(sp):
            def load(b):
                sp.dma_start(slots[:].rearrange("p a t -> p (a t)"), d["slots"][bass.ds(b * P, P), :]).then_inc(slots_in, 16)
                sp.dma_start(gates[:].rearrange("p a t -> p (a t)"), d["gates"][bass.ds(b * P, P), :]).then_inc(gates_in, 16)
                sp.dma_start(pre[:], d["x1"][bass.ds(b * SEQ, SEQ), :].rearrange("(t p) c -> p t c", p=P)).then_inc(x1_in, 16)

            def spread_scores(b, h):
                sp.wait_ge(v_free, v_upto(b, ("scoreT", h)))
                sp.dma_start(d["score_rows"][bass.ds(2 * b + h, 1), :].rearrange("a (r s) -> (a r) s", s=P), scoreT[:]).then_inc(scores_stored, 16)
                sp.wait_ge(scores_stored, 32 * b + 16 * h + 16)
                for j in range(EXPERTS // 2):
                    if h == 1:
                        sp.wait_ge(scaled, 2 * EXPERTS * b + 2 * j + 2)
                    sp.dma_start(score_rows[:, bass.ts(j, 2 * HALF)],
                                 d["score_rows"][bass.ds(2 * b + h, 1), bass.ts(j, 2 * HALF)].to_broadcast([P, 2 * HALF])).then_inc(scores_in[j], 16)

            def store(b, h):
                sp.wait_ge(out_done, 2 * b + h + 1)
                sp.dma_start(d["out"][bass.ds(b * SEQ + h * HALF, HALF), :].rearrange("(t p) c -> p t c", p=P),
                             x3[:, bass.ts(h, HTILES), :]).then_inc(out_stored, 16)

            def body(b, end):
                if not end:
                    sp.wait_ge(x2_done, HALVES * (b + 1))
                    load(b + 1)
                if not is_first(b):
                    store(b - 1, 1)
                spread_scores(b, 0)
                spread_scores(b, 1)
                store(b, 0)

            load(0)
            sp.dma_start(bias_q[:], d["bq"]).then_inc(biases_in, 16)
            sp.dma_start(bias_k[:], d["bk"]).then_inc(biases_in, 16)
            sp.dma_start(bias_v[:], d["bv"].partition_broadcast(P)).then_inc(biases_in, 16)
            sp.dma_start(bias_corr[:], d["corr"].partition_broadcast(P)).then_inc(biases_in, 16)
            sp.dma_start(w2_raw, d["w2T"].rearrange("p (k n) -> p k n", k=EXPERTS)).then_inc(w2_in, 16)
            body(0, False)
            with sp.Fori(1, BATCHES - 1) as b:
                body(b, False)
            body(BATCHES - 1, True)
            store(BATCHES - 1, 1)
            sp.wait_ge(out_stored, 32 * BATCHES)

        @block.gpsimd
        def _(pool):
            pool.memset(ident[:], 0.0).then_inc(consts, 1)
            pool.memset(zeros[:], 0.0).then_inc(consts, 1)
            for e in range(EXPERTS):
                pool.memset(falling[:, e:e + 1], float(EXPERTS - e)).then_inc(consts, 1)
            pool.wait_ge(consts, 1)
            pool.affine_select(out=ident[:], in_=ident[:], compare_op=ALU.not_equal, fill=1.0,
                               base=0, pattern=[[-1, P]], channel_multiplier=1).then_inc(consts, 1)

            def gather(b):
                for t in range(TILES):
                    rows, arrived = rows_of(b, t)
                    producer, upto = (slots_in, 16 * b + 16) if t < GATHER or is_first(b) else (combined, TILES * b + t - GATHER + 1)
                    if not isinstance(upto, int):
                        pool.to_reg(upto)
                    pool.wait_ge(consts, CONSTS)
                    pool.wait_ge(producer, upto)
                    for a in range(2):
                        pool.indirect_dma_start(rows[:, a, :], None, d["ys"],
                                                bass.IndirectOffsetOnAxis(ap=slots[:, a, t:t + 1], axis=0),
                                                bounds_check=TRASH + P - 1, oob_is_err=False).then_inc(arrived, 16)

            def add_bias(b):
                pool.wait_ge(v_full, PROLOGUE if is_first(b) else v_upto(b - 1, ("x2T", 1)))
                pool.tensor_tensor(x2[:], x2[:], bias_v[:].unsqueeze(1).to_broadcast([P, TILES, C]), ALU.add).then_inc(bias_added, 1)

            def body(b, end):
                if not end:
                    gather(b + 1)
                for kind, j in order(b):
                    if kind not in ("up", "expert"):
                        continue
                    for k in range(CHUNKS):
                        n, place = hidden(b, kind, j, k)
                        pool.wait_ge(s_free, s_upto(b, (kind, j), k))
                        wait_past(pool, hid_split, n - RING + 1)
                        t = relu[:, place % RELU_RING, :]
                        if kind == "up":
                            pool.tensor_tensor(square[:, place % RING, :], t, t, ALU.mult).then_inc(squared, 1)
                        else:
                            e = place - EXPERTS
                            pool.wait_ge(scores_in[e // 2], 16 * (HALVES * b + j[0] + 1))
                            pool.tensor_tensor(square[:, place % RING, :], t, score_rows[:, bass.ts(e, HALF)], ALU.mult).then_inc(scaled, 1)
                if not end:
                    add_bias(b + 1)

            gather(0)
            add_bias(0)
            body(0, False)
            with pool.Fori(1, BATCHES - 1) as b:
                body(b, False)
            body(BATCHES - 1, True)

        @block.scalar
        def _(act):
            def normed(out, rows, t, scales, shifts):
                return act.activation(out[:, t, :], rows[:, t, :], ACT.Identity, scale=scales[:, t:t + 1], bias=shifts[:, t:t + 1])

            def keep(b, h):
                if h == 0:
                    act.wait_ge(factor_done, b + 1)
                    act.wait_ge(x1_in, 16 * b + 16)
                for t in range(HTILES * h, HTILES * (h + 1)):
                    last = act.activation(pre[:, t, :], pre[:, t, :], ACT.Copy, scale=gates[:, 2, t:t + 1])
                last.then_inc(kept, 1)

            def norm_x2(b, t):
                if is_first(b) and t % HTILES == 0:
                    act.wait_ge(pre_chain, (t // HTILES + 1) * (HTILES + NORM_STEPS))
                elif t == 0:
                    act.wait_ge(pre_chain, (b + 1) * PRE_STEPS + NORM_STEPS)
                    wait_past(act, x3_done, 2 * b)
                norm = normed(x2, pre, t, pre_scale, pre_shift)
                if t % HTILES == HTILES - 1:
                    norm.then_inc(x2_done, 1)

            def turn_rows(h, first_n):
                for c in range(CH):
                    act.wait_ge(v_full, first_n + c + 1)
                    act.activation(x2T_hi[:, c, bass.ts(h, HALF)], ps[:, v_bank(("x2T", h), c), :], ACT.Copy).then_inc(hi_done, 1)

            def tail(b):
                act.wait_ge(ln_chain, (4 * b + 4) * NORM_STEPS)
                for t in range(HTILES, TILES):
                    last = normed(x3, x3, t, scale, shift)
                last.then_inc(out_done, 1)

            def norm4(b, t):
                if t == 0:
                    act.wait_ge(ln_chain, (4 * b + 3) * NORM_STEPS)
                norm = normed(x3, x3, t, scale, shift)
                if t == HTILES - 1:
                    norm.then_inc(out_done, 1)

            def body(b, end):
                def copy_hi(unit, g, out, func=ACT.Copy, **kw):
                    act.wait_ge(v_full, v_number(b, V_AT[unit] + g) + 1)
                    act.activation(out, ps[:, v_bank(unit, g), :], func, **kw).then_inc(hi_done, 1)

                for unit in order(b):
                    kind, j = unit
                    if kind in ("q", "k"):
                        hi, bias = (q_hi, bias_qs) if kind == "q" else (k_hi, bias_k)
                        copy_hi(unit, 0, hi[:, j % CH, bass.ts(j // CH, HALF)], ACT.Identity, bias=bias[:, j % CH:j % CH + 1])
                    elif kind == "v":
                        copy_hi(unit, 0, v_hi[:, 2 * j:2 * j + 2, :].rearrange("p t c -> p (t c)"))
                    elif kind == "score":
                        bank = s_bank(unit)
                        act.wait_ge(max_done, TILES * b + j + 1)
                        if j == 0 and not is_first(b):
                            act.wait_ge(hid_hi_done, HALVES * HIDDEN * b)
                        act.activation(prob[:, j % 2, :], ps[:, bank:bank + 2, :].rearrange("p a n -> p (a n)"), ACT.Exp,
                                       bias=neg_max[:, j:j + 1], accum_out=row_sum[:, j:j + 1]).then_inc(s_free, 2)
                    elif kind == "turn":
                        for g in range(2):
                            copy_hi(unit, g, probT_hi[:, 4 * g:4 * g + 4, :].rearrange("p t s -> p (t s)"))
                    elif kind == "norm3":
                        act.wait_ge(ln_chain, (4 * b + j + 1) * NORM_STEPS)
                        if not is_first(b):
                            act.wait_ge(out_stored, 32 * b)
                        for t in range(HTILES * j, HTILES * (j + 1)):
                            last = normed(x3, x2, t, scale, shift)
                        last.then_inc(x3_done, 1)
                    elif kind == "x3T":
                        for c in range(CH):
                            copy_hi(unit, c, x3T_hi[:, c, :])
                    elif kind == "gateT":
                        act.wait_ge(v_full, v_number(b, V_AT[unit]) + 1)
                        wait_past(act, score_done, 2 * b + j)
                        act.activation(expd[:].rearrange("p t e -> p (t e)"), ps[:, v_bank(unit), 0:HTILES * EXPERTS], ACT.Exp, scale=-1.0).then_inc(exp_done, 1)
                    elif kind == "latent":
                        copy_hi(unit, 0, lat_hi[:])
                    elif kind == "comb":
                        copy_hi(unit, 0, comb_hi[:])
                    elif kind == "x2T":
                        act.wait_ge(scaled, 2 * EXPERTS * (b + 1))
                        turn_rows(j, v_number(b, V_AT[unit]))
                    elif kind == "tail":
                        tail(b - 1)
                    elif kind == "keep":
                        keep(b + 1, j)
                    elif kind in ("up", "expert"):
                        lag = 1 if kind == "up" else 2
                        for k in range(CHUNKS + lag):
                            if k < CHUNKS:
                                n, place = hidden(b, kind, j, k)
                                act.wait_ge(s_full, s_upto(b, unit, k))
                                wait_past(act, squared, n - RELU_RING + 1)
                                if kind == "up" or k < RELU_RING:
                                    wait_past(act, hid_hi_done, n - RELU_RING + 1)
                                act.activation(relu[:, place % RELU_RING, :], ps[:, s_bank(unit, k), :], ACT.Relu).then_inc(s_free, 1)
                            if k >= lag:
                                n, place = hidden(b, kind, j, k - lag)
                                if kind == "up":
                                    act.wait_ge(s_free, s_upto(b, unit, k - lag))
                                    act.activation(hid_hi[:, place, :], relu[:, place % RELU_RING, :], ACT.Square).then_inc(hid_hi_done, 1)
                                else:
                                    act.wait_ge(squared, n + 1)
                                    act.activation(hid_hi[:, place, :], square[:, place % RING, :], ACT.Copy).then_inc(hid_hi_done, 1)
                            if k < CHUNKS and unit in (("expert", (0, 1)), ("expert", (1, 0))) and not end:
                                norm_x2(b + 1, CHUNKS * j[0] + k)
                            elif k < CHUNKS and unit == ("expert", (1, 1)):
                                norm4(b, k)

            for h in range(HALVES):
                keep(0, h)
            act.wait_ge(biases_in, 64)
            for t in range(TILES):
                norm_x2(0, t)
            for h in range(HALVES):
                turn_rows(h, CH * h)
            act.wait_ge(w2_in, 16)
            act.activation(w2_hi[:], w2_raw, ACT.Copy).then_inc(w2_hi_done, 1)
            act.wait_ge(w2_split, 2)
            body(0, False)
            with act.Fori(1, BATCHES - 1) as b:
                body(b, False)
            body(BATCHES - 1, True)
            tail(BATCHES - 1)

        @block.vector
        def _(v):
            def split_rows(h, hi_n):
                for c in range(CH):
                    v.wait_ge(hi_done, hi_n + c + 1)
                    at = (slice(None), c, bass.ts(h, HALF))
                    v.tensor_tensor(x2T_lo[at], ps[:, v_bank(("x2T", h), c), :], f32(x2T_hi[at]), ALU.subtract).then_inc(v_free, 1)

            def add_kept(b):
                v.wait_ge(gates_in, 16 * b + 16)
                v.tensor_scalar(gates[:, 2, :], gates[:, 2, :], 1.0, None, ALU.add).then_inc(factor_done, 1)

            def combine(b, t):
                chain = Chain(v, combine_chain, TILES * b + t)
                rows = pre[:, t, :]
                place, arrived = rows_of(b, t)
                if t % HTILES == 0:
                    v.wait_ge(kept, 2 * b + t // HTILES + 1)
                v.wait_ge(arrived, 32 if is_first(b) else 32 * (TILES // GATHER * (b - 1) + t // GATHER + 1))
                chain.step(v.scalar_tensor_tensor(rows, place[:, 0, :], gates[:, 0, t:t + 1], rows, ALU.mult, ALU.add))
                chain.wait()
                v.scalar_tensor_tensor(rows, place[:, 1, :], gates[:, 1, t:t + 1], rows, ALU.mult, ALU.add).then_inc(combined, 1)
                v.wait_ge(combined, TILES * b + t + 1)
                v.bn_stats(pre_stats[:, t, :], rows).then_inc(pre_chain, 1)

            def scale_pre(b):
                chain = Chain(v, pre_chain, b * PRE_STEPS + NORM_STEPS)
                chain.n = TILES
                norm_scale(v, chain, pre_stats[:], pre_scale[:], pre_shift[:], tmp[:])
                assert chain.n == PRE_STEPS, chain.n

            def scale_first(h):
                chain = Chain(v, pre_chain, HTILES * (h + 1) + NORM_STEPS * h)
                half = bass.ts(h, HTILES)
                norm_scale(v, chain, pre_stats[:, half, :], pre_scale[:, half], pre_shift[:, half], tmp[:, :, half])

            def scale_half(b, which, h):
                chain = Chain(v, ln_chain, (4 * b + which) * NORM_STEPS)
                half = bass.ts(h, HTILES)
                v.wait_ge(stats_done, HTILES * (4 * b + which + 1))
                norm_scale(v, chain, stats[:, half, :], scale[:, half], shift[:, half], tmp[:, :, half])
                assert chain.n == NORM_STEPS, chain.n

            def tail(b):
                scale_half(b, 3, 1)

            def route(b, h, n):
                chain = Chain(v, route_chain, (2 * b + h) * ROUTE_STEPS)
                v.wait_ge(exp_done, 2 * b + h + 1)
                v.tensor_scalar(expd[:], expd[:], 1.0, None, ALU.add).then_inc(v_free, 1)
                v.wait_ge(v_free, n + 1)
                chain.step(v.reciprocal(score[:], expd[:]))
                chain.then(v.tensor_tensor, choice[:], score[:], along(bias_corr[:], HTILES), ALU.add)
                groups = choice[:].rearrange("p t (g e) -> p (t g) e", g=GROUPS)
                keys = key0[:].rearrange("p t (g e) -> p (t g) e", g=GROUPS)
                keys1 = key1[:].rearrange("p t (g e) -> p (t g) e", g=GROUPS)
                marks, seconds = group_m[:].rearrange("p t g -> p (t g)"), group_n[:].rearrange("p t g -> p (t g)")
                chain.then(v.tensor_reduce, marks, groups, AX.X, ALU.max)
                chain.then(v.tensor_tensor, keys, groups, across(marks, GSIZE), ALU.is_equal)
                chain.then(v.tensor_tensor, keys, keys, along(falling[:, 0:GSIZE], HTILES * GROUPS), ALU.mult)
                chain.then(v.tensor_reduce, seconds, keys, AX.X, ALU.max)
                chain.then(v.tensor_tensor, keys, keys, across(seconds, GSIZE), ALU.is_equal)
                chain.then(v.scalar_tensor_tensor, keys1, keys, LOWEST, groups, ALU.mult, ALU.add)
                chain.then(v.tensor_reduce, seconds, keys1, AX.X, ALU.max)
                chain.then(v.tensor_tensor, group_m[:], group_m[:], group_n[:], ALU.add)
                chain.then(v.tensor_tensor, group_n[:, :, 0], group_m[:, :, 0], group_m[:, :, 1], ALU.is_ge)
                chain.then(v.tensor_scalar, group_n[:, :, 1], group_n[:, :, 0], -1.0, 1.0, ALU.mult, ALU.add)
                chain.then(v.tensor_tensor, groups, groups, across(seconds, GSIZE), ALU.mult)
                top_two(v, chain, first[:], second[:], choice[:], falling[:], (row_m[:], row_s[:]), row_m[:], (key0[:], key1[:]))
                chain.then(v.tensor_tensor, first[:], first[:], second[:], ALU.add)
                chain.then(v.tensor_tensor, score[:], score[:], first[:], ALU.mult)
                chain.then(v.tensor_reduce, row_s[:], score[:], AX.X, ALU.add)
                chain.then(v.tensor_scalar, row_s[:], row_s[:], NORM_EPS, None, ALU.add)
                chain.then(v.reciprocal, row_s[:], row_s[:])
                chain.wait()
                v.tensor_tensor(score_et[:].rearrange("p e t -> p t e"), score[:], across(row_s[:], EXPERTS), ALU.mult).then_inc(score_done, 1)
                assert chain.n == ROUTE_STEPS, chain.n

            def body(b, end):
                hi_n = [b * HI_EACH + PROLOGUE]

                def split_lo(unit, g, hi, lo, bias=None):
                    hi_n[0] = hi_n[0] + 1
                    bank = ps[:, v_bank(unit, g), :]
                    v.wait_ge(hi_done, hi_n[0])
                    if bias is None:
                        v.tensor_tensor(lo, bank, f32(hi), ALU.subtract).then_inc(v_free, 1)
                    else:
                        v.scalar_tensor_tensor(lo, bank, bias, f32(hi), ALU.add, ALU.subtract).then_inc(v_free, 1)

                for unit in order(b):
                    kind, j = unit
                    n = v_number(b, V_AT[unit])
                    if kind in ("q", "k"):
                        hi, lo, bias = (q_hi, q_lo, bias_qs) if kind == "q" else (k_hi, k_lo, bias_k)
                        at = (slice(None), j % CH, bass.ts(j // CH, HALF))
                        split_lo(unit, 0, hi[at], lo[at], bias[:, j % CH:j % CH + 1])
                    elif kind == "v":
                        split_lo(unit, 0, v_hi[:, 2 * j:2 * j + 2, :].rearrange("p t c -> p (t c)"), v_lo[:, 2 * j:2 * j + 2, :].rearrange("p t c -> p (t c)"))
                    elif kind == "score":
                        bank = s_bank(unit)
                        v.wait_ge(s_full, s_upto(b, unit, 1))
                        v.tensor_reduce(neg_max[:, j:j + 1], ps[:, bank:bank + 2, :].rearrange("p a n -> p (a n)"), AX.X, ALU.max, negate=True).then_inc(max_done, 1)
                    elif kind == "turn":
                        for g in range(2):
                            at = (slice(None), slice(4 * g, 4 * g + 4))
                            split_lo(unit, g, probT_hi[at].rearrange("p t s -> p (t s)"), probT_lo[at].rearrange("p t s -> p (t s)"))
                    elif kind == "mix":
                        v.wait_ge(s_free, s_upto(b, ("score", j), 1))
                        v.reciprocal(row_inv[:, j:j + 1], row_sum[:, j:j + 1]).then_inc(inv_done, 1)
                        v.wait_ge(v_full, n + 1)
                        v.wait_ge(bias_added, b + 1)
                        v.wait_ge(inv_done, TILES * b + j + 1)
                        v.scalar_tensor_tensor(x2[:, j, :], ps[:, v_bank(unit), 0:C], row_inv[:, j:j + 1], x2[:, j, :], ALU.mult, ALU.add).then_inc(v_free, 1)
                        v.wait_ge(v_free, n + 1)
                        v.bn_stats(stats[:, j, :], x2[:, j, :]).then_inc(stats_done, 1)
                    elif kind == "ln3":
                        if not is_first(b):
                            v.wait_ge(out_done, 2 * b)
                        scale_half(b, j, j)
                    elif kind == "x3T":
                        for c in range(CH):
                            split_lo(unit, c, x3T_hi[:, c, :], x3T_lo[:, c, :])
                    elif kind == "gate":
                        v.wait_ge(v_full, n + 1)
                        v.tensor_copy(logit[:], ps[0:EXPERTS, v_bank(unit), :]).then_inc(v_free, 1)
                    elif kind == "gateT":
                        route(b, j, n)
                    elif kind == "scoreT":
                        v.wait_ge(v_full, n + 1)
                        wait_past(v, scores_stored, 32 * b + 16 * j)
                        v.tensor_copy(scoreT[:], ps[0:EXPERTS * HTILES, v_bank(unit), 0:P]).then_inc(v_free, 1)
                    elif kind == "latent":
                        split_lo(unit, 0, lat_hi[:], lat_lo[:])
                    elif kind == "comb":
                        split_lo(unit, 0, comb_hi[:], comb_lo[:])
                    elif kind == "keep" and j == 0:
                        add_kept(b + 1)
                    elif kind == "combine":
                        combine(b + 1, j)
                    elif kind == "ln2":
                        scale_pre(b + 1)
                    elif kind == "x2T":
                        split_rows(j, hi_n[0])
                        hi_n[0] = hi_n[0] + V_COUNT["x2T"]
                    elif kind == "tail":
                        tail(b - 1)
                    elif kind in ("up", "expert"):
                        lag = 0 if kind == "up" else 1
                        for k in range(CHUNKS + lag):
                            if lag and k < CHUNKS:
                                n, place = hidden(b, kind, j, k)
                                v.wait_ge(scaled, EXPERTS * (HALVES * b + j[0]) + place - EXPERTS + 1)
                                v.tensor_tensor(square[:, place % RING, :], square[:, place % RING, :], relu[:, place % RELU_RING, :], ALU.mult).then_inc(squared, 1)
                            if k >= lag:
                                n, place = hidden(b, kind, j, k - lag)
                                v.wait_ge(squared, n + 1)
                                v.wait_ge(hid_hi_done, n + 1)
                                v.tensor_tensor(hid_lo[:, place, :], square[:, place % RING, :], f32(hid_hi[:, place, :]), ALU.subtract).then_inc(hid_split, 1)
                    elif kind == "out":
                        for g in range(2):
                            at = HTILES * j + 2 * g
                            v.wait_ge(v_full, n + g + 1)
                            v.tensor_tensor(x3[:, at:at + 2, :], ps[:, v_bank(unit, g), :].rearrange("p (t c) -> p t c", c=C), x3[:, at:at + 2, :], ALU.add).then_inc(v_free, 1)
                        for t in range(HTILES):
                            v.wait_ge(v_free, n + t // 2 + 1)
                            v.bn_stats(stats[:, HTILES * j + t, :], x3[:, HTILES * j + t, :]).then_inc(stats_done, 1)
                    elif kind == "ln4":
                        v.wait_ge(x3_done, 2 * b + 2)
                        scale_half(b, 2, 0)

            v.wait_ge(consts, CONSTS)
            add_kept(0)
            v.wait_ge(biases_in, 64)
            v.tensor_scalar(bias_qs[:], bias_q[:], SCALE, None, ALU.mult).then_inc(w2_split, 1)
            for h in range(HALVES):
                for t in range(HTILES * h, HTILES * (h + 1)):
                    combine(0, t)
                scale_first(h)
            for h in range(HALVES):
                split_rows(h, CH * h)
            v.wait_ge(w2_hi_done, 1)
            v.tensor_tensor(w2_lo[:], w2_raw, f32(w2_hi[:]), ALU.subtract).then_inc(w2_split, 1)
            v.wait_ge(w2_split, 2)
            body(0, False)
            with v.Fori(1, BATCHES - 1) as b:
                body(b, False)
            body(BATCHES - 1, True)
            tail(BATCHES - 1)

        @block.tensor
        def _(pe):
            def turn_rows(b, h, opened):
                pe.wait_ge(x2_done, HALVES * b + h + 1)
                for c in range(CH):
                    out = opened(c)
                    for t in range(HTILES):
                        last = pe.transpose(out[:, bass.ts(t, P)], x2[:, HTILES * h + t, bass.ts(c, P)], ident[:])
                    last.then_inc(v_full, 1)

            def body(b, end):
                def s_open(unit, k):
                    wait_past(pe, s_free, s_upto(b, unit, k) - S_BANKS)
                    return ps[:, s_bank(unit, k), :]

                pe.wait_ge(v_free, V_COUNT["x2T"] if is_first(b) else v_upto(b - 1, ("x2T", 0)))
                for unit in order(b):
                    kind, j = unit
                    if kind in ("q", "k"):
                        w_hi, w_lo = (wq_hi, wq_lo) if kind == "q" else (wk_hi, wk_lo)
                        h, p = j // CH, j % CH
                        if (kind, j) == ("q", CH):
                            pe.wait_ge(v_free, PROLOGUE if is_first(b) else v_upto(b - 1, ("x2T", 1)))
                        product(pe, v_open(pe, b, unit), [(w_hi[:, c, bass.ts(p, P)], w_lo[:, c, bass.ts(p, P)], x2T_hi[:, c, bass.ts(h, HALF)], x2T_lo[:, c, bass.ts(h, HALF)])
                                                          for c in range(CH)]).then_inc(v_full, 1)
                    elif kind == "v":
                        out = v_open(pe, b, unit)
                        for t in (2 * j, 2 * j + 1):
                            last = product(pe, out[:, bass.ts(t % 2, C)],
                                           [(x2T_hi[:, c, bass.ts(t, P)], x2T_lo[:, c, bass.ts(t, P)], wv_hi[:, c, :], wv_lo[:, c, :]) for c in range(CH)])
                        last.then_inc(v_full, 1)
                    elif kind == "score":
                        pe.wait_ge(v_free, v_upto(b, ("k", 3)))
                        for h in range(2):
                            product(pe, s_open(unit, h), [(q_hi[:, c, bass.ts(j, P)], q_lo[:, c, bass.ts(j, P)], k_hi[:, c, bass.ts(h, HALF)], k_lo[:, c, bass.ts(h, HALF)])
                                                          for c in range(CH)]).then_inc(s_full, 1)
                    elif kind == "turn":
                        pe.wait_ge(s_free, s_upto(b, ("score", j), 1))
                        for g in range(2):
                            out = v_open(pe, b, unit, g)
                            for t in range(4):
                                last = pe.transpose(out[:, bass.ts(t, P)], prob[:, j % 2, bass.ts(4 * g + t, P)], ident[:])
                            last.then_inc(v_full, 1)
                    elif kind == "mix":
                        pe.wait_ge(v_free, v_upto(b, ("turn", j)))
                        product(pe, v_open(pe, b, unit)[:, 0:C], [(probT_hi[:, t, :], probT_lo[:, t, :], v_hi[:, t, :], v_lo[:, t, :]) for t in range(TILES)]).then_inc(v_full, 1)
                    elif kind == "x3T":
                        pe.wait_ge(x3_done, 2 * b + j + 1)
                        for c in range(CH):
                            out = v_open(pe, b, unit, c)
                            for t in range(HTILES):
                                last = pe.transpose(out[:, bass.ts(t, P)], x3[:, HTILES * j + t, bass.ts(c, P)], ident[:])
                            last.then_inc(v_full, 1)
                    elif kind == "gate":
                        pe.wait_ge(v_free, v_upto(b, ("x3T", j)))
                        product(pe, v_open(pe, b, unit)[0:EXPERTS, :], [(gate_hi[:, c, :], gate_lo[:, c, :], x3T_hi[:, c, :], x3T_lo[:, c, :]) for c in range(CH)]).then_inc(v_full, 1)
                    elif kind == "gateT":
                        logit_there = v_upto(b, ("gate", j))
                        if not isinstance(b, int):
                            pe.to_reg(logit_there)
                        pe.wait_ge(w2_split, 2)
                        pe.wait_ge(v_free, logit_there)
                        out = ps[:, v_bank(unit), :]
                        for t in range(HTILES):
                            last = pe.transpose(out[:, bass.ts(t, EXPERTS)], logit[:, bass.ts(t, P)], ident[0:EXPERTS, 0:EXPERTS])
                        last.then_inc(v_full, 1)
                    elif kind == "scoreT":
                        pe.wait_ge(score_done, 2 * b + j + 1)
                        pe.transpose(v_open(pe, b, unit)[0:EXPERTS * HTILES, 0:P], score_et[:].rearrange("p e t -> p (e t)"), ident[:]).then_inc(v_full, 1)
                    elif kind == "latent":
                        pe.wait_ge(v_free, v_upto(b, ("x3T", j)))
                        product(pe, v_open(pe, b, unit), [(fc1_hi[:, c, :], fc1_lo[:, c, :], x3T_hi[:, c, :], x3T_lo[:, c, :]) for c in range(CH)]).then_inc(v_full, 1)
                    elif kind == "up":
                        pe.wait_ge(v_free, v_upto(b, ("x3T", j[0])))
                        for k in range(CHUNKS):
                            n = CHUNKS * j[1] + k
                            product(pe, s_open(unit, k), [(up_hi[:, c, bass.ts(n, P)], up_lo[:, c, bass.ts(n, P)], x3T_hi[:, c, :], x3T_lo[:, c, :])
                                                          for c in range(CH)]).then_inc(s_full, 1)
                    elif kind == "expert":
                        h, part = j
                        pe.wait_ge(v_free, v_upto(b, ("latent", h)))
                        for k in range(CHUNKS):
                            e = CHUNKS * part + k
                            product(pe, s_open(unit, k), [(w1_hi[:, e, :], w1_lo[:, e, :], lat_hi[:], lat_lo[:])]).then_inc(s_full, 1)
                            t, some = 2 * part + k // 2, range(4 * (k % 2), 4 * (k % 2) + 4)
                            pe.wait_ge(hid_split, hidden(b, "up", (h, k % 2), CHUNKS - 1)[0] + 1)
                            out = ps[:, v_bank(("out", h), part), :]
                            if k == 0:
                                pe.matmul(v_open(pe, b, ("out", h), part), zeros[:, 0:P], zeros[:], start=True, stop=False)
                            accumulate(pe, out[:, bass.ts(t % 2, C)], [(hid_hi[:, m, bass.ts(t, P)], hid_lo[:, m, bass.ts(t, P)], down_hi[:, m, :], down_lo[:, m, :])
                                                                       for m in some])
                    elif kind == "x2T":
                        pe.wait_ge(s_free, s_upto(b, ("expert", (HALVES - 1, PARTS - 1)), CHUNKS - 1))
                        turn_rows(b + 1, j, lambda c: v_open(pe, b, unit, c))
                    elif kind == "comb":
                        out = v_open(pe, b, unit)
                        for e in range(EXPERTS):
                            n, place = hidden(b, "expert", (j, e // CHUNKS), e % CHUNKS)
                            pe.wait_ge(hid_split, n + 1)
                            pe.matmul(out, w2_hi[:, e, :], hid_hi[:, place, :], start=(e == 0), stop=False)
                            pe.matmul(out, w2_hi[:, e, :], hid_lo[:, place, :], start=False, stop=False)
                            last = pe.matmul(out, w2_lo[:, e, :], hid_hi[:, place, :], start=False, stop=(e == EXPERTS - 1))
                        last.then_inc(v_full, 1)
                    elif kind == "out":
                        pe.wait_ge(v_free, v_upto(b, ("comb", j)))
                        for t in range(HTILES):
                            last = accumulate(pe, ps[:, v_bank(unit, t // 2), bass.ts(t % 2, C)],
                                              [(comb_hi[:, bass.ts(t, P)], comb_lo[:, bass.ts(t, P)], fc2_hi[:, 0, :], fc2_lo[:, 0, :])], stop=(t % 2 == 1))
                            if t % 2:
                                last.then_inc(v_full, 1)

            pe.wait_ge(consts, CONSTS)

            for h in range(HALVES):
                turn_rows(0, h, lambda c: ps[:, v_bank(("x2T", h), c), :])
            pe.wait_ge(w2_split, 2)
            body(0, False)
            with pe.Fori(1, BATCHES - 1) as b:
                body(b, False)
            body(BATCHES - 1, True)


def program(nc, d):
    d["x1"] = nc.dram_tensor("x1_rows", (TOKENS, C), F32).ap()
    d["xs"] = nc.dram_tensor("expert_rows", (REAL * CAP, C), F32).ap()
    d["ys"] = nc.dram_tensor("expert_results", (REAL * CAP + P, C), F32).ap()
    d["slots"] = nc.dram_tensor("slot_rows", (BATCHES * P, 2 * TILES), U32).ap()
    d["gates"] = nc.dram_tensor("gate_rows", (BATCHES * P, 3 * TILES), F32).ap()
    d["score_rows"] = nc.dram_tensor("score_rows", (2 * BATCHES, EXPERTS * HALF), F32).ap()
    stage_a(nc, d)
    with ExitStack() as ctx:
        shapes = {"wq": [P, CH, C], "wk": [P, CH, C], "wv": [P, CH, C], "gateT": [P, CH, EXPERTS], "fc1T": [P, CH, LATENT], "fc2T": [P, 1, C],
                  "w1T": [P, EXPERTS, P], "upT": [P, CH, SHARED], "downT": [P, SHARED // P, C]}
        weights = {name: tuple(ctx.enter_context(nc.sbuf_tensor(f"c_{name}_{part}", shape, F32R)) for part in ("hi", "lo")) for name, shape in shapes.items()}
        stage_b(nc, d, [(d[name], hi, lo, SCALE if name == "wq" else 1.0) for name, (hi, lo) in weights.items()])
        stage_c(nc, d, weights)


def kernel(**inputs):
    import numpy as np
    import concourse.bacc as bacc
    from concourse.bass_utils import run_bass_kernel_spmd

    def rows(name):
        a = np.asarray(inputs[name])
        return a.reshape(-1, a.shape[-1])

    qkv = rows("L0_attn_qkv_weight")
    arrays = {
        "x": rows("L0_attn_x"), "xT": rows("L0_attn_x").T,
        "wqT": qkv[:C].T, "wkvT": qkv[C:].T, "projT": rows("L0_attn_proj_weight").T, "proj_bias": inputs["L0_attn_proj_bias"],
        "routerT": rows("L0_ffn_router_w").T, "router_b": inputs["L0_ffn_router_b"],
        "w_in": rows("L0_ffn_experts_inter"), "w_out": rows("L0_ffn_experts_out"),
        "wq": rows("L1_attn_W_q"), "wk": rows("L1_attn_W_k"), "wv": rows("L1_attn_W_v"),
        "bq": np.asarray(inputs["L1_attn_b_q"]).reshape(CH, P).T, "bk": np.asarray(inputs["L1_attn_b_k"]).reshape(CH, P).T, "bv": inputs["L1_attn_b_v"],
        "gateT": rows("L1_ffn_gate").T, "corr": inputs["L1_ffn_corr_bias"],
        "fc1T": rows("L1_ffn_fc1_w").T, "fc2T": rows("L1_ffn_fc2_w").T,
        "w1T": rows("L1_ffn_w1").T, "w2T": rows("L1_ffn_w2").reshape(EXPERTS, LATENT, -1).transpose(2, 0, 1).reshape(-1, EXPERTS * LATENT),
        "upT": rows("L1_ffn_up_w").T, "downT": rows("L1_ffn_down_w").T,
    }
    arrays = {name: np.ascontiguousarray(a) for name, a in arrays.items()}
    nc = bacc.Bacc("TRN2", target_bir_lowering=False, num_devices=1)
    d = {name: nc.dram_tensor(name, a.shape, mybir.dt.from_np(a.dtype), kind="ExternalInput").ap() for name, a in arrays.items()}
    d["out"] = nc.dram_tensor("out", (TOKENS, C), F32, kind="ExternalOutput").ap()
    program(nc, d)
    got = run_bass_kernel_spmd(nc, [arrays], core_ids=[0])
    return got.results[0]["out"].reshape(BATCHES, SEQ, C)
```
